# Optimizing a Trainium2 kernel written in Bass

```python
import numpy as np
import jax
import jax.numpy as jnp

def _softmax(x, axis=-1):
    return jax.nn.softmax(x, axis=axis)

def _gelu(x):
    return jax.nn.gelu(x, approximate=True)

def _silu(x):
    return jax.nn.silu(x)

def _sigmoid(x):
    return jax.nn.sigmoid(x)

def _layernorm(x, axis=-1, eps=1e-05):
    m = jnp.mean(x, axis=axis, keepdims=True)
    v = jnp.var(x, axis=axis, keepdims=True)
    return (x - m) / jnp.sqrt(v + eps)

def _scatter_add(tgt, idx, src, axis=0):
    return tgt.at[idx].add(src)

def _segment_sum(src, seg, n):
    return jax.ops.segment_sum(src, seg, n)
kernel_name = 'mk_gnn_preln_d4_gnn_r8_c592e9'

def setup_inputs(seed: int=0):
    np.random.seed(seed)
    _w = jnp.asarray

    def _rec_inputs():
        import jax
        import jax.numpy as jnp
        _gk = jax.random.key(seed)
        x = -8.776e-05 + 1 * jax.random.normal(jax.random.fold_in(_gk, 1), (2500, 256), jnp.float32)
        src = jax.random.randint(jax.random.fold_in(_gk, 2), (80000,), 0, 2500, jnp.int32)
        dst = jnp.minimum((2500 * jax.random.uniform(jax.random.fold_in(_gk, 3), (80000,)) ** 2.0).astype(jnp.int32), 19999)
        _o = jnp.argsort(dst, stable=True)
        src = src[_o]
        dst = dst[_o]
        edge_attr_256 = -5.16925e-05 + 1.00005 * jax.random.normal(jax.random.fold_in(_gk, 12), (80000, 256), jnp.float32)
        edge_type_8 = jax.random.randint(jax.random.fold_in(_gk, 14), (80000,), 0, 8, jnp.int32)
        return (x, src, dst, edge_attr_256, edge_type_8)
    x, src, dst, edge_attr_256, edge_type_8 = _rec_inputs()

    def _L0_gnn_setup():
        import jax, jax.numpy as jnp
        import numpy as np
        N_NODES = 2500
        key = jax.random.key(seed)
        k1, k2, k3, k4 = jax.random.split(key, 4)
        d = 256
        E = 40000
        x = jax.random.normal(k1, (N_NODES, d), dtype=jnp.float32)
        edge_index = jax.random.randint(k2, (2, E), 0, N_NODES, dtype=jnp.int64)
        limit = float(np.sqrt(6.0 / (d + d)))
        W_l = jax.random.uniform(k3, (d, d), dtype=jnp.float32, minval=-limit, maxval=limit)
        W_r = jax.random.uniform(k4, (d, d), dtype=jnp.float32, minval=-limit, maxval=limit)
        b_r = jnp.zeros((d,), dtype=jnp.float32)
        return {'x': x, 'edge_index': edge_index, 'W_l': W_l, 'W_r': W_r, 'b_r': b_r}
    _L0_gnn_all = _L0_gnn_setup()
    _L0_gnn_in = {k: v for k, v in _L0_gnn_all.items() if k in ('W_l', 'W_r', 'b_r')}
    del _L0_gnn_all

    def _L1_gnn_setup():
        import jax, jax.numpy as jnp
        import numpy as np
        N_NODES = 12500
        N_EDGES = 50000
        C = 256
        NUM_GRAPHS = 512
        EPS = 1e-05
        key = jax.random.key(seed)
        ks = jax.random.split(key, 12)
        x = jax.random.normal(ks[0], (N_NODES, C), dtype=jnp.float32)
        edge_index = jax.random.randint(ks[1], (2, N_EDGES), 0, N_NODES, dtype=jnp.int32)
        edge_attr = jax.random.normal(ks[2], (N_EDGES, C), dtype=jnp.float32)
        batch = jnp.sort(jax.random.randint(ks[3], (N_NODES,), 0, NUM_GRAPHS, dtype=jnp.int32))
        s1 = 1.0 / np.sqrt(C)
        s2 = 1.0 / np.sqrt(2 * C)
        W1 = jax.random.normal(ks[4], (C, 2 * C), dtype=jnp.float32) * s1
        b1 = jnp.zeros((2 * C,), dtype=jnp.float32)
        bn_gamma = jnp.ones((2 * C,), dtype=jnp.float32)
        bn_beta = jnp.zeros((2 * C,), dtype=jnp.float32)
        W2 = jax.random.normal(ks[5], (2 * C, C), dtype=jnp.float32) * s2
        b2 = jnp.zeros((C,), dtype=jnp.float32)
        ln_w = jnp.ones((C,), dtype=jnp.float32)
        ln_b = jnp.zeros((C,), dtype=jnp.float32)
        gn_w = jnp.ones((C,), dtype=jnp.float32)
        gn_b = jnp.zeros((C,), dtype=jnp.float32)
        gn_ms = jnp.ones((C,), dtype=jnp.float32)
        return dict(x=x, edge_index=edge_index, edge_attr=edge_attr, batch=batch, W1=W1, b1=b1, bn_gamma=bn_gamma, bn_beta=bn_beta, W2=W2, b2=b2, ln_w=ln_w, ln_b=ln_b, gn_w=gn_w, gn_b=gn_b, gn_ms=gn_ms)
    _L1_gnn_all = _L1_gnn_setup()
    _L1_gnn_in = {k: v for k, v in _L1_gnn_all.items() if k in ('W1', 'b1', 'bn_gamma', 'bn_beta', 'W2', 'b2', 'ln_w', 'ln_b', 'gn_w', 'gn_b', 'gn_ms')}
    del _L1_gnn_all

    def _L2_gnn_setup():
        import jax, jax.numpy as jnp
        import numpy as np
        N_NODES = 6250
        N_EDGES = 100000
        D_IN = 256
        D_OUT = 256
        N_REL = 8
        key = jax.random.key(seed)
        k_x, k_ei, k_et, k_w = jax.random.split(key, 4)
        x = jax.random.normal(k_x, (N_NODES, D_IN), dtype=jnp.float32)
        edge_index = jax.random.randint(k_ei, (2, N_EDGES), 0, N_NODES, dtype=jnp.int32)
        edge_type = jax.random.randint(k_et, (N_EDGES,), 0, N_REL, dtype=jnp.int32)
        limit = float(np.sqrt(6.0 / (D_IN + D_OUT)))
        weight = jax.random.uniform(k_w, (N_REL, D_IN, D_OUT), dtype=jnp.float32, minval=-limit, maxval=limit)
        bias = jnp.zeros((D_OUT,), dtype=jnp.float32)
        return {'x': x, 'edge_index': edge_index, 'edge_type': edge_type, 'weight': weight, 'bias': bias}
    _L2_gnn_all = _L2_gnn_setup()
    _L2_gnn_in = {k: v for k, v in _L2_gnn_all.items() if k in ('weight', 'bias')}
    del _L2_gnn_all

    def _L3_gnn_setup():
        import jax, jax.numpy as jnp
        import numpy as np
        N = 6250
        E = 50000
        IN_DIM = 256
        H = 8
        D = 32
        LN_EPS = 1e-05
        key = jax.random.key(seed)
        k_x, k_e, k_w, k_a = jax.random.split(key, 4)
        x = jax.random.normal(k_x, (N, IN_DIM), dtype=jnp.float32)
        edge_index = jax.random.randint(k_e, (2, E), 0, N, dtype=jnp.int32)
        w_lim = np.sqrt(6.0 / (IN_DIM + H * D)) * np.sqrt(2.0)
        W = jax.random.uniform(k_w, (IN_DIM, H * D), minval=-w_lim, maxval=w_lim, dtype=jnp.float32)
        a_lim = np.sqrt(6.0 / (2 * D + 1))
        k_as, k_ad = jax.random.split(k_a)
        a_src = jnp.broadcast_to(jax.random.uniform(k_as, (1, D), minval=-a_lim, maxval=a_lim, dtype=jnp.float32), (H, D)).copy()
        a_dst = jnp.broadcast_to(jax.random.uniform(k_ad, (1, D), minval=-a_lim, maxval=a_lim, dtype=jnp.float32), (H, D)).copy()
        gamma = jnp.ones((H * D,), dtype=jnp.float32)
        beta = jnp.zeros((H * D,), dtype=jnp.float32)
        return {'x': x, 'edge_index': edge_index, 'W': W, 'a_src': a_src, 'a_dst': a_dst, 'gamma': gamma, 'beta': beta}
    _L3_gnn_all = _L3_gnn_setup()
    _L3_gnn_in = {k: v for k, v in _L3_gnn_all.items() if k in ('W', 'a_src', 'a_dst', 'gamma', 'beta')}
    del _L3_gnn_all
    return {'x': x, 'src': src, 'dst': dst, 'edge_attr_256': edge_attr_256, 'edge_type_8': edge_type_8, 'L0_gnn_W_l': _L0_gnn_in['W_l'], 'L0_gnn_W_r': _L0_gnn_in['W_r'], 'L0_gnn_b_r': _L0_gnn_in['b_r'], 'L1_gnn_W1': _L1_gnn_in['W1'], 'L1_gnn_b1': _L1_gnn_in['b1'], 'L1_gnn_bn_gamma': _L1_gnn_in['bn_gamma'], 'L1_gnn_bn_beta': _L1_gnn_in['bn_beta'], 'L1_gnn_W2': _L1_gnn_in['W2'], 'L1_gnn_b2': _L1_gnn_in['b2'], 'L1_gnn_ln_w': _L1_gnn_in['ln_w'], 'L1_gnn_ln_b': _L1_gnn_in['ln_b'], 'L1_gnn_gn_w': _L1_gnn_in['gn_w'], 'L1_gnn_gn_b': _L1_gnn_in['gn_b'], 'L1_gnn_gn_ms': _L1_gnn_in['gn_ms'], 'L2_gnn_weight': _L2_gnn_in['weight'], 'L2_gnn_bias': _L2_gnn_in['bias'], 'L3_gnn_W': _L3_gnn_in['W'], 'L3_gnn_a_src': _L3_gnn_in['a_src'], 'L3_gnn_a_dst': _L3_gnn_in['a_dst'], 'L3_gnn_gamma': _L3_gnn_in['gamma'], 'L3_gnn_beta': _L3_gnn_in['beta']}

def reference(x, src, dst, edge_attr_256, edge_type_8, L0_gnn_W_l, L0_gnn_W_r, L0_gnn_b_r, L1_gnn_W1, L1_gnn_b1, L1_gnn_bn_gamma, L1_gnn_bn_beta, L1_gnn_W2, L1_gnn_b2, L1_gnn_ln_w, L1_gnn_ln_b, L1_gnn_gn_w, L1_gnn_gn_b, L1_gnn_gn_ms, L2_gnn_weight, L2_gnn_bias, L3_gnn_W, L3_gnn_a_src, L3_gnn_a_dst, L3_gnn_gamma, L3_gnn_beta):
    import jax
    import jax.numpy as jnp

    def _L0_gnn_ref(x, edge_index, W_l, W_r, b_r):
        import jax, jax.numpy as jnp
        import numpy as np
        N_NODES = 2500
        src, dst = (edge_index[0], edge_index[1])
        messages = x[src]
        sums = jax.ops.segment_sum(messages, dst, num_segments=N_NODES)
        counts = jax.ops.segment_sum(jnp.ones_like(dst, dtype=x.dtype), dst, num_segments=N_NODES)
        aggr = sums / jnp.maximum(counts, 1.0)[:, None]
        out = aggr @ W_l.T + x @ W_r.T + b_r
        return out

    def _L1_gnn_ref(x, edge_index, edge_attr, batch, W1, b1, bn_gamma, bn_beta, W2, b2, ln_w, ln_b, gn_w, gn_b, gn_ms):
        import jax, jax.numpy as jnp
        import numpy as np
        N_NODES = 12500
        N_EDGES = 50000
        C = 256
        NUM_GRAPHS = 512
        EPS = 1e-05
        src, dst = (edge_index[0], edge_index[1])
        msg = jax.nn.relu(x[src] + edge_attr)
        agg = jnp.zeros_like(x).at[dst].add(msg)
        h = x + agg
        h = h @ W1 + b1
        mu = jnp.mean(h, axis=0)
        var = jnp.mean((h - mu) ** 2, axis=0)
        h = (h - mu) / jnp.sqrt(var + EPS) * bn_gamma + bn_beta
        h = jax.nn.relu(h) @ W2 + b2
        cnt = jax.ops.segment_sum(jnp.ones((h.shape[0],), h.dtype), batch, NUM_GRAPHS)
        denom = jnp.maximum(cnt, 1.0) * C
        mean_g = jax.ops.segment_sum(h.sum(axis=1), batch, NUM_GRAPHS) / denom
        h = h - mean_g[batch][:, None]
        var_g = jax.ops.segment_sum((h * h).sum(axis=1), batch, NUM_GRAPHS) / denom
        h = h * jax.lax.rsqrt(var_g + EPS)[batch][:, None] * ln_w + ln_b
        cnt_c = jnp.maximum(cnt, 1.0)[:, None]
        mean = jax.ops.segment_sum(h, batch, NUM_GRAPHS) / cnt_c
        out = h - mean[batch] * gn_ms
        var2 = jax.ops.segment_sum(out * out, batch, NUM_GRAPHS) / cnt_c
        out = out * jax.lax.rsqrt(var2 + EPS)[batch] * gn_w + gn_b
        out = jax.nn.relu(out)
        return x + out

    def _L2_gnn_ref(x, edge_index, edge_type, weight, bias):
        import jax, jax.numpy as jnp
        import numpy as np
        N_NODES = 6250
        N_EDGES = 100000
        D_IN = 256
        D_OUT = 256
        N_REL = 8
        num_nodes = x.shape[0]
        row, col = (edge_index[0], edge_index[1])
        xt = jnp.einsum('ni,rio->rno', x, weight)
        messages = xt[edge_type, col]
        out = jax.ops.segment_sum(messages, row, num_segments=num_nodes)
        return jax.nn.relu(out + bias)

    def _L3_gnn_ref(x, edge_index, W, a_src, a_dst, gamma, beta):
        import jax, jax.numpy as jnp
        import numpy as np
        N = 6250
        E = 50000
        IN_DIM = 256
        H = 8
        D = 32
        LN_EPS = 1e-05
        n = x.shape[0]
        src, dst = (edge_index[0], edge_index[1])
        hh = (x @ W).reshape(n, H, D)
        s_src = jnp.einsum('nhd,hd->nh', hh, a_src)
        s_dst = jnp.einsum('nhd,hd->nh', hh, a_dst)
        scores = jax.nn.leaky_relu(s_src[src] + s_dst[dst], negative_slope=0.2)
        m = jax.ops.segment_max(scores, dst, num_segments=n)
        e = jnp.exp(scores - m[dst])
        denom = jax.ops.segment_sum(e, dst, num_segments=n)
        alpha = e / denom[dst]
        msgs = hh[src] * alpha[:, :, None]
        out = jax.ops.segment_sum(msgs, dst, num_segments=n).reshape(n, H * D)
        out = out + x
        mu = jnp.mean(out, axis=-1, keepdims=True)
        var = jnp.mean(jnp.square(out - mu), axis=-1, keepdims=True)
        out = (out - mu) / jnp.sqrt(var + LN_EPS) * gamma + beta
        return jax.nn.elu(out)
    edge_index = jnp.stack([src, dst])
    batch0 = jnp.zeros((2500,), jnp.int32)
    h = jnp.maximum(_layernorm(x, axis=-1), 0.0)
    x = x + _L0_gnn_ref(h, edge_index, L0_gnn_W_l, L0_gnn_W_r, L0_gnn_b_r)
    h = jnp.maximum(_layernorm(x, axis=-1), 0.0)
    x = x + _L1_gnn_ref(h, edge_index, edge_attr_256, batch0, L1_gnn_W1, L1_gnn_b1, L1_gnn_bn_gamma, L1_gnn_bn_beta, L1_gnn_W2, L1_gnn_b2, L1_gnn_ln_w, L1_gnn_ln_b, L1_gnn_gn_w, L1_gnn_gn_b, L1_gnn_gn_ms)
    h = jnp.maximum(_layernorm(x, axis=-1), 0.0)
    x = x + _L2_gnn_ref(h, edge_index, edge_type_8, L2_gnn_weight, L2_gnn_bias)
    h = jnp.maximum(_layernorm(x, axis=-1), 0.0)
    x = x + _L3_gnn_ref(h, edge_index, L3_gnn_W, L3_gnn_a_src, L3_gnn_a_dst, L3_gnn_gamma, L3_gnn_beta)
    return x

_drawn_inputs = setup_inputs


def setup_inputs(seed=0):
    import zlib

    import numpy as np

    out = dict(_drawn_inputs(seed))
    spreads = {'L0_gnn_b_r': (0.0, 0.1),
     'L1_gnn_b1': (0.0, 0.8),
     'L1_gnn_bn_gamma': (1.0, 0.2),
     'L1_gnn_bn_beta': (0.0, 0.313),
     'L1_gnn_b2': (0.0, 0.476),
     'L1_gnn_ln_w': (1.0, 0.6),
     'L1_gnn_ln_b': (0.0, 0.8),
     'L1_gnn_gn_w': (1.0, 0.2),
     'L1_gnn_gn_b': (0.0, 0.297),
     'L1_gnn_gn_ms': (1.0, 0.2),
     'L2_gnn_bias': (0.0, 0.606),
     'L3_gnn_gamma': (1.0, 0.571),
     'L3_gnn_beta': (0.0, 0.667)}
    factors = {'L3_gnn_a_src': 3.468, 'L3_gnn_a_dst': 8.0}
    for name, (base, spread) in spreads.items():
        noise = np.random.default_rng([zlib.crc32(name.encode()), seed]).standard_normal(out[name].shape)
        drawn = base * np.exp(spread * noise) if base else spread * noise
        out[name] = jnp.asarray(drawn.astype(out[name].dtype))
    for name, factor in factors.items():
        out[name] = (out[name] * factor).astype(out[name].dtype)
    return out
```

```python
from contextlib import ExitStack

import concourse.bass as bass
from concourse import mybir

F32 = mybir.dt.float32
I32 = mybir.dt.int32
ALU = mybir.AluOpType
ACT = mybir.ActivationFunctionType
AX = mybir.AxisListType


def gnn_kernel(nc, a, out):
    N, D = a["x"].shape
    E = a["src"].shape[0]
    NW, WN = 20, 125
    GT, TE = 5, 128
    GE = GT * TE
    NG = E // GE
    RING = 5
    assert NW * WN == N and NG * GE == E and NG % RING == 0 and NG <= 128
    R = a["L2_gnn_weight"].shape[0]
    H, HD = a["L3_gnn_a_src"].shape
    DH = D + H
    D1 = a["L1_gnn_W1"].shape[1]
    KD, KH = D // 128, D1 // 128
    NC, CN = 5, N // 5
    EPS = 1e-5
    BIG = 1e30
    SLOPE = 0.2
    WEIGHT_LOADS = 20
    MM_STEPS = {0: 1, 2: R // 2, 3: 1}

    with ExitStack() as ctx:
        def sb(name, shape, dt=F32):
            return ctx.enter_context(nc.sbuf_tensor(name, shape, dt))

        def sem(name):
            return ctx.enter_context(nc.semaphore(name))

        h_table = [nc.dram_tensor(f"h_table{l}", (N, D), F32, kind="Internal").ap() for l in range(2)]
        xt_table = nc.dram_tensor("xt_table", (R * N, D), F32, kind="Internal").ap()
        hh_table = nc.dram_tensor("hh_table", (N, DH), F32, kind="Internal").ap()

        x = sb("x", [WN, NW, D])
        h = sb("h", [WN, NW, D])
        acc = sb("acc", [WN, NW, DH])
        stats = sb("stats", [WN, NW, 6])
        mean_var = sb("mean_var", [WN, NW, 2])
        rstd = sb("rstd", [WN, NW])
        shift = sb("shift", [WN, NW])
        stage = sb("stage", [128, RING * GT * (DH + D)])
        rows = stage[:, 0:RING * GT * DH].rearrange("p (r j c) -> p r j c", r=RING, j=GT)
        attr = stage[:, RING * GT * DH:].rearrange("p (r j c) -> p r j c", r=RING, j=GT)
        src_idx = sb("src_idx", [128, NG + RING, GT], I32)
        rel_idx = sb("rel_idx", [128, NG + RING, GT], I32)
        dst_f = sb("dst_f", [128, NG, GT])
        slot = sb("slot", [128, RING, GT], I32)
        spans = sb("spans", [1, 2, NG], I32)
        src_f = sb("src_f", [128, NG, GT])
        onehot = sb("onehot", [128, GT, WN])
        node_iota = sb("node_iota", [128, N])
        ident = sb("ident", [128, 128])
        ones = sb("ones", [128, 128])
        onehot_t = sb("onehot_t", [WN, GE])
        penalty = sb("penalty", [WN, GE])
        diag = attr[:, 1, :, :].rearrange("p j c -> p (j c)")[:, 0:H * TE].rearrange("p (h e) -> p h e", h=H)
        masked = attr[0:WN, 2, :, :].rearrange("p j c -> p (j c)")[:, 0:H * TE].rearrange("p (h e) -> p h e", h=H)
        msg = sb("msg", [128, GT, DH])
        tile_max = sb("tile_max", [WN, GT, H])
        node_ref = sb("node_ref", [WN, 2 * H])
        score = sb("score", [128, GT, H])
        s_dst = sb("s_dst", [WN, NW, H])
        run_max = sb("run_max", [WN, NW, H])
        new_max = sb("new_max", [WN, H])
        decay = sb("decay", [WN, 2, H])
        fresh = sb("fresh", [WN, DH])
        hT = sb("hT", [128, KD, N])
        z1T = stage[:, 0:KH * N].rearrange("p (k n) -> p k n", k=KH)
        nodes_b = sb("nodes_b", [WN, 2, 2 * D])
        nodesT_b = sb("nodesT_b", [128, 2, 4 * WN])
        xt_out = hT[0:WN, :, 0:R * D]
        hh_out = sb("hh_out", [WN, 2, DH])
        prod = sb("prod", [WN, 2, D])
        w0 = sb("w0", [128, 2 * KD, D])
        w1 = sb("w1", [128, KD, D1])
        w2 = sb("w2", [128, KH, D])
        w_rel = stage[:, RING * GT * (DH + D) - KD * R * D:].rearrange("p (k r d) -> p k r d", k=KD, r=R)
        w_att = sb("w_att", [128, KD, D])
        bias0 = sb("bias0", [WN, D])
        bias_rel = sb("bias_rel", [WN, D])
        gamma = sb("gamma", [WN, D])
        beta = sb("beta", [WN, D])
        a_src = sb("a_src", [WN, D])
        a_dst = sb("a_dst", [WN, D])
        v1 = sb("v1", [128, 3, KH])
        v2 = sb("v2", [128, 6, KD])
        st1 = sb("st1", [128, KH, NC, 6])
        mv1 = sb("mv1", [128, KH, 2])
        sc1 = sb("sc1", [128, 2, KH])
        st2 = sb("st2", [128, KD, NC, 6])
        mv2 = sb("mv2", [128, KD, 2])
        t2 = sb("t2", [128, 8, KD])
        g1 = sb("g1", [128, 4])
        bank = [ctx.enter_context(nc.psum_tensor(f"bank{i}", [128, 512], F32)) for i in range(8)]
        raw = stage[0:NG, 0:3 * GE].bitcast(I32).rearrange("p (a e) -> p a e", a=3)
        flt = stage[0:NG, 3 * GE:6 * GE].rearrange("p (a e) -> p a e", a=3)
        span_f = sb("span_f", [NG, 6])
        bounds = sb("bounds", [NG, NW - 1])
        cmp = sb("cmp", [NG, 4, NW - 1])
        rank = sb("rank", [NG, 6])

        s_edges, s_x, s_w, s_const = sem("edges_loaded"), sem("x_loaded"), sem("weights_loaded"), sem("constants_ready")
        s_flt, s_lists_t, s_lists = sem("lists_float"), sem("lists_transposed"), sem("lists_ready")
        s_var = [sem(f"var_ready{l}") for l in range(5)]
        s_std = [sem(f"std_ready{l}") for l in range(5)]
        s_rstd = [sem(f"rstd_ready{l}") for l in range(5)]
        s_h = [sem(f"h_ready{l}") for l in range(4)]
        s_table = [sem(f"table_written{l}") for l in range(2)]
        s_x_new = {l: sem(f"x_new{l}") for l in (2, 3)}
        s_xt = [sem(f"xt_written{b}") for b in range(2)]
        s_hh = [sem(f"hh_written{b}") for b in range(2)]
        s_zero = [sem(f"acc_zero{l}") for l in range(4)]
        s_slot = [sem(f"slot_ready{l}") for l in range(4)]
        s_rows = [[sem(f"rows_gathered{l}_{b}") for b in range(RING)] for l in range(4)]
        s_attr = [sem(f"attr_loaded{b}") for b in range(RING)]
        s_onehot = [sem(f"onehot_ready{l}") for l in range(4)]
        s_sum = [sem(f"group_summed{l}") for l in range(4)]
        s_add, s_relu = sem("rows_added"), sem("rows_relu")
        s_nb, s_nt, s_ntc, s_mm, s_ev = ([sem(f"{n}{l}") for l in range(4)] for n in
                                         ("nodes_staged", "nodes_transposed", "nodesT_ready", "product_ready", "product_taken"))
        s_oht, s_ohtc, s_diag, s_spread, s_ref, s_back, s_arg, s_exp, s_msg, s_dec, s_dexp = (
            sem(n) for n in ("onehot_turned", "onehot_t_ready", "diag_ready", "scores_spread", "node_ref_ready",
                             "refs_at_edges", "exponent_ready", "exp_ready", "msg_ready", "decay_ready", "decay_exp"))
        s_z1p, s_z1, s_st1, s_sd1, s_bn, s_z1n = (sem(n) for n in ("z1_product", "z1_ready", "z1_stats", "z1_std", "bn_ready", "z1_normed"))
        s_z2p, s_z2, s_g = sem("z2_product"), sem("z2_ready"), sem("graph_sums_wanted")
        s_gp, s_sd, s_fin, s_ob, s_obt = sem("graph_sums"), sem("std_wanted"), sem("affine_ready"), sem("out_staged"), sem("out_transposed")
        s_sdr = sem("std_done")
        s_wrel = sem("w_rel_loaded")
        s_begun = sem("gathers_begun")
        s_elu, s_elud, s_out = sem("elu_arg"), sem("elu_done"), sem("out_written")

        def row_bc(v, n):
            return v.rearrange("(a d) -> a d", a=1).broadcast_to([n, v.shape[0]])

        def pairs(eng, step):
            for b in range(2):
                step(0, b, True)
            with eng.Fori(1, NW // 2) as i:
                for b in range(2):
                    step(i, b, False)

        def rings(eng, step):
            with eng.Fori(0, NG // RING) as i:
                for b in range(RING):
                    step(i, b)

        def each_window(eng, g, step, by=0):
            word = eng.value_load(spans[0:1, by, bass.ds(g, 1)], min_val=0, max_val=32 * NW + NW - 1)
            why = "the list holds windows of nodes"
            first = nc.s_assert_within(eng.snap(word & 31), 0, NW - 1, skip_runtime_bounds_check_because=why)
            end = nc.s_assert_within(eng.snap(word >> 5), 1, NW, skip_runtime_bounds_check_because=why)
            with eng.Fori(first, end) as w:
                step(w)

        class Visits:

            def __init__(self, eng, steps=1):
                self.most = steps * NG * NW
                self.eng, self.reg = eng, eng.alloc_register(f"visits_{nc.next_id()}")
                eng.reg_mov(self.reg, 0)

            def next(self):
                self.eng.reg_add(self.reg, self.reg, 1)
                return self.eng.snap(self.reg, min_val=1, max_val=self.most)

        def window(t, w):
            return t[:, bass.ds(w, 1), :].rearrange("p w d -> p (w d)")

        block = ctx.enter_context(nc.Block())

        @block.sync
        def _(sp):
            for i, n in enumerate(("dst", "src", "edge_type_8")):
                sp.dma_start(raw[:, i, :], a[n].rearrange("(g e) -> g e", e=GE)).then_inc(s_edges, 16)
            sp.dma_start(x[:], a["x"].rearrange("(w p) d -> p w d", p=WN)).then_inc(s_x, 16)
            loads = [(w0[:, 0:KD, :], a["L0_gnn_W_l"].rearrange("(k p) d -> p k d", p=128)),
                     (w0[:, KD:2 * KD, :], a["L0_gnn_W_r"].rearrange("(k p) d -> p k d", p=128)),
                     (w1[:], a["L1_gnn_W1"].rearrange("(k p) d -> p k d", p=128)),
                     (w2[:], a["L1_gnn_W2"].rearrange("(k p) d -> p k d", p=128)),
                     (w_att[:], a["L3_gnn_W"].rearrange("(k p) d -> p k d", p=128))]
            loads += [(t[:], row_bc(a[n], WN)) for t, n in ((bias0, "L0_gnn_b_r"), (bias_rel, "L2_gnn_bias"),
                                                           (gamma, "L3_gnn_gamma"), (beta, "L3_gnn_beta"))]
            loads += [(t[:], row_bc(a[n].rearrange("h d -> (h d)"), WN)) for t, n in
                      ((a_src, "L3_gnn_a_src"), (a_dst, "L3_gnn_a_dst"))]
            loads += [(v1[:, i, :], a["L1_gnn_" + n].rearrange("(k p) -> p k", p=128))
                      for i, n in enumerate(("b1", "bn_gamma", "bn_beta"))]
            loads += [(v2[:, i, :], a["L1_gnn_" + n].rearrange("(k p) -> p k", p=128))
                      for i, n in enumerate(("b2", "ln_w", "ln_b", "gn_w", "gn_b", "gn_ms"))]
            assert len(loads) == WEIGHT_LOADS
            with nc.allow_non_contiguous_dma("vectors of a few hundred elements"):
                for dst, src in loads:
                    sp.dma_start(dst, src).then_inc(s_w, 16)

            sp.wait_ge(s_h[0], NW)
            sp.dma_start(h_table[0].rearrange("(w p) d -> p w d", p=WN), h[:]).then_inc(s_table[0], 16)
            sp.wait_ge(s_h[1], NW)
            sp.dma_start(h_table[1].rearrange("(w p) d -> p w d", p=WN), h[:]).then_inc(s_table[1], 16)

            attr_h = a["edge_attr_256"].rearrange("(g j p) d -> g p j d", j=GT, p=TE)
            for b in range(RING):
                sp.dma_start(attr[:, b, :, :], attr_h[b, :, :, :]).then_inc(s_attr[b], 16)
            with sp.Fori(0, NG // RING - 1) as i:
                for b in range(RING):
                    sp.wait_ge(s_add, RING * i + b + 1)
                    sp.dma_start(attr[:, b, :, :],
                                 attr_h[bass.ds(RING * i + RING + b, 1), :, :, :].rearrange("g p j d -> (g p) j d")
                                 ).then_inc(s_attr[b], 16)

            sp.wait_ge(s_z2p, KD * NC)
            for k in range(KD):
                sp.dma_start(w_rel[:, k, :, :], a["L2_gnn_weight"][:, 128 * k:128 * k + 128, :].rearrange("r p d -> p r d")
                             ).then_inc(s_wrel, 16)

            xt_h = xt_table.rearrange("(r w p) d -> w p r d", r=R, p=WN)

            def store_xt(i, b, first):
                sp.wait_ge(s_ev[2], R // 2 * (2 * i + b + 1))
                sp.dma_start(xt_h[bass.ds(2 * i + b, 1), :, :, :].rearrange("w p r d -> (w p) r d"),
                             xt_out[:, b, :].rearrange("p (r d) -> p r d", r=R)).then_inc(s_xt[b], 16)
            pairs(sp, store_xt)

            hh_h = hh_table.rearrange("(w p) d -> w p d", p=WN)

            def store_hh(i, b, first):
                sp.wait_ge(s_ev[3], 2 * i + b + 1)
                sp.dma_start(hh_h[bass.ds(2 * i + b, 1), :, :].rearrange("w p d -> (w p) d"),
                             hh_out[:, b, :]).then_inc(s_hh[b], 16)
            pairs(sp, store_hh)

            sp.wait_ge(s_x_new[3], 1)
            sp.dma_start(out.rearrange("(w p) d -> p w d", p=WN), x[:]).then_inc(s_out, 16)
            sp.wait_ge(s_out, 16)

        @block.gpsimd
        def _(pool):
            nc.gpsimd.memset(ident[:], 0.0)
            nc.gpsimd.memset(ones[:], 1.0)
            nc.gpsimd.memset(src_idx[:, NG:, :], 0)
            nc.gpsimd.memset(rel_idx[:, NG:, :], 0)
            nc.gpsimd.iota(bounds[:], [[WN, NW - 1]], base=WN, channel_multiplier=0, allow_small_or_imprecise_dtypes=True)
            nc.gpsimd.iota(node_iota[:], [[1, N]], base=0, channel_multiplier=0, allow_small_or_imprecise_dtypes=True)
            pool.drain()
            nc.gpsimd.affine_select(out=ident[:], in_=ident[:], compare_op=ALU.not_equal, fill=1.0, base=0,
                                    pattern=[[-1, 128]], channel_multiplier=1).then_inc(s_const, 1)
            nc.gpsimd.memset(acc[:], 0.0).then_inc(s_zero[0], 1)
            pool.wait_ge(s_lists, 1)
            nc.gpsimd.memset(rows[:, :, :, D:D + 1], 1.0).then_inc(s_zero[0], 1)

            def gathers(l, table, width, written):
                for s, n in written:
                    pool.wait_ge(s, n)

                def step(i, b):
                    pool.wait_ge(s_slot[l], RING * i + b + 1)
                    pool.sem_inc(s_begun, 1)
                    for j in range(GT):
                        pool.indirect_dma_start(rows[:, b, j, 0:width], None, table,
                                                bass.IndirectOffsetOnAxis(ap=slot[:, b, j:j + 1], axis=0)
                                                ).then_inc(s_rows[l][b], 16)
                rings(pool, step)

            gathers(0, h_table[0], D, [(s_table[0], 16)])
            pool.wait_ge(s_nb[0], NW)
            nc.gpsimd.memset(acc[:], 0.0).then_inc(s_zero[1], 1)
            gathers(1, h_table[1], D, [(s_table[1], 16)])
            pool.wait_ge(s_nb[1], NW)
            nc.gpsimd.memset(acc[:], 0.0).then_inc(s_zero[2], 1)
            gathers(2, xt_table, D, [(s_xt[b], 16 * NW // 2) for b in range(2)])
            pool.wait_ge(s_x_new[2], 1)
            nc.gpsimd.memset(acc[:], 0.0).then_inc(s_zero[3], 1)
            gathers(3, hh_table, DH, [(s_hh[b], 16 * NW // 2) for b in range(2)])

        @block.scalar
        def _(act):
            def normed(l):
                act.wait_ge(s_var[l], 1)
                nc.scalar.activation(rstd[:], rstd[:], ACT.Sqrt).then_inc(s_std[l], 1)
                act.wait_ge(s_rstd[l], 1)
                with act.Fori(0, NW) as w:
                    nc.scalar.activation(window(h, w), window(x, w), ACT.Relu,
                                         bias=shift[:, bass.ds(w, 1)], scale=rstd[:, bass.ds(w, 1)]).then_inc(s_h[l], 1)

            def turned(l, blocks):
                def step(i, b, first):
                    act.wait_ge(s_nt[l], 2 * i + b + 1)
                    if not first:
                        act.wait_ge(s_mm[l], MM_STEPS[l] * (2 * i + b - 1))
                    nc.scalar.activation(nodesT_b[:, b, 0:blocks * WN], bank[b][:, 0:blocks * WN], ACT.Copy
                                         ).then_inc(s_ntc[l], 1)
                pairs(act, step)

            normed(0)
            turned(0, 2 * KD)
            normed(1)

            def relu_rows(i, b):
                act.wait_ge(s_add, RING * i + b + 1)
                nc.scalar.activation(rows[:, b, :, 0:D], rows[:, b, :, 0:D], ACT.Relu).then_inc(s_relu, 1)
            rings(act, relu_rows)

            def keep_hT(i, b, first):
                act.wait_ge(s_nt[1], 2 * i + b + 1)
                nc.scalar.activation(hT[:, :, bass.ds(WN * (2 * i + b), WN)],
                                     bank[b][:, 0:KD * WN].rearrange("p (k n) -> p k n", k=KD), ACT.Copy
                                     ).then_inc(s_ntc[1], 1)
            pairs(act, keep_hT)
            with act.Fori(0, NC) as c:
                for m in range(KH):
                    act.wait_ge(s_z1p, KH * c + m + 1)
                    nc.scalar.activation(z1T[:, m, bass.ds(CN * c, CN)], bank[2 + m][:, 0:CN], ACT.Identity,
                                         bias=v1[:, 0, m:m + 1]).then_inc(s_z1, 1)
            act.wait_ge(s_st1, 1)
            nc.scalar.activation(sc1[:, 0, :], sc1[:, 0, :], ACT.Sqrt).then_inc(s_sd1, 1)
            act.wait_ge(s_bn, 1)
            for m in range(KH):
                nc.scalar.activation(z1T[:, m, :], z1T[:, m, :], ACT.Relu, bias=sc1[:, 1, m:m + 1],
                                     scale=sc1[:, 0, m:m + 1]).then_inc(s_z1n, 1)
            with act.Fori(0, NC) as c:
                for m in range(KD):
                    act.wait_ge(s_z2p, KD * c + m + 1)
                    nc.scalar.activation(hT[:, m, bass.ds(CN * c, CN)], bank[m][:, 0:CN], ACT.Identity,
                                         bias=v2[:, 0, m:m + 1]).then_inc(s_z2, 1)
            act.wait_ge(s_sd, 1)
            nc.scalar.activation(g1[:, 3:4], g1[:, 3:4], ACT.Sqrt).then_inc(s_sdr, 1)
            act.wait_ge(s_sd, 2)
            nc.scalar.activation(t2[:, 5, :], t2[:, 5, :], ACT.Sqrt).then_inc(s_sdr, 1)
            act.wait_ge(s_fin, 1)

            def final_relu(i, b, first):
                if not first:
                    act.wait_ge(s_obt, 2 * i + b - 1)
                for k in range(KD):
                    last = nc.scalar.activation(nodesT_b[:, b, WN * k:WN * k + WN], hT[:, k, bass.ds(WN * (2 * i + b), WN)],
                                                ACT.Relu, bias=t2[:, 7, k:k + 1], scale=t2[:, 6, k:k + 1])
                last.then_inc(s_ob, 1)
            pairs(act, final_relu)

            normed(2)
            turned(2, KD)
            normed(3)
            turned(3, KD)

            def attention(w):
                v = visits.next()
                act.wait_ge(s_oht, v)
                nc.scalar.activation(onehot_t[:, 0:4 * TE], bank[0][0:WN, :], ACT.Copy)
                nc.scalar.activation(onehot_t[:, 4 * TE:], bank[1][0:WN, 0:TE], ACT.Copy).then_inc(s_ohtc, 1)
                act.wait_ge(s_arg, v)
                nc.scalar.activation(msg[:, :, D:DH], score[:], ACT.Exp).then_inc(s_exp, 1)
                act.wait_ge(s_dec, v)
                nc.scalar.activation(decay[:], decay[:], ACT.Exp).then_inc(s_dexp, 1)
            visits = Visits(act)
            rings(act, lambda i, b: each_window(act, RING * i + b, attention))

            act.wait_ge(s_var[4], 1)
            nc.scalar.activation(rstd[:], rstd[:], ACT.Sqrt).then_inc(s_std[4], 1)
            act.wait_ge(s_elu, 1)
            nc.scalar.activation(acc[:, :, 0:D], acc[:, :, 0:D], ACT.Exp).then_inc(s_elud, 1)

        @block.tensor
        def _(pe):
            pe.wait_ge(s_const, 1)
            pe.wait_ge(s_flt, 1)
            for i in range(3):
                for j in range(GT):
                    q = i * GT + j
                    last = nc.tensor.transpose(bank[q // 4][:, 128 * (q % 4):128 * (q % 4) + NG],
                                               flt[:, i, TE * j:TE * j + TE], ident[0:NG, 0:NG])
            last.then_inc(s_lists_t, 1)
            pe.wait_ge(s_flt, 2)
            for k in range(2):
                last = nc.tensor.transpose(bank[4][0:1, NG * k:NG * k + NG], span_f[:, 4 + k:5 + k], ident[0:NG, 0:NG])
            last.then_inc(s_lists_t, 1)

            def turn(l, blocks):
                def step(i, b, first):
                    pe.wait_ge(s_nb[l], 2 * i + b + 1)
                    if not first:
                        pe.wait_ge(s_ntc[l], 2 * i + b - 1)
                    for k in range(blocks):
                        last = nc.tensor.transpose(bank[b][:, WN * k:WN * k + WN], nodes_b[:, b, 128 * k:128 * k + 128],
                                                   ident[0:WN, 0:WN])
                    last.then_inc(s_nt[l], 1)
                return step

            def two_steps(first_step, second_step):
                for b in range(2):
                    first_step(0, b, True)
                for b in range(2):
                    second_step(0, b, True)
                with pe.Fori(1, NW // 2) as i:
                    for b in range(2):
                        first_step(i, b, False)
                    for b in range(2):
                        second_step(i, b, False)

            def sums(l, width, data, ready):
                visits = Visits(pe)

                def visit(w):
                    pe.wait_ge(s_onehot[l], visits.next())
                    for j in range(GT):
                        last = nc.tensor.matmul(bank[6][0:WN, 0:width], onehot[:, j, :], data(j), start=(j == 0),
                                                stop=(j == GT - 1))
                    last.then_inc(s_sum[l], 1)

                def step(i, b):
                    ready(i, b)
                    data_b[0] = b
                    each_window(pe, RING * i + b, visit, by=int(l == 2))
                rings(pe, step)

            data_b = [0]
            pe.wait_ge(s_zero[0], 2)
            sums(0, D + 1, lambda j: rows[:, data_b[0], j, 0:D + 1],
                 lambda i, b: pe.wait_ge(s_rows[0][b], 16 * GT * (i + 1)))
            pe.wait_ge(s_w, 16 * WEIGHT_LOADS)

            def products0(i, b, first):
                pe.wait_ge(s_ntc[0], 2 * i + b + 1)
                if not first:
                    pe.wait_ge(s_ev[0], 2 * i + b - 1)
                for k in range(2 * KD):
                    last = nc.tensor.matmul(bank[2 + b][0:WN, 0:D], nodesT_b[:, b, WN * k:WN * k + WN], w0[:, k, :],
                                            start=(k == 0), stop=(k == 2 * KD - 1))
                last.then_inc(s_mm[0], 1)
            two_steps(turn(0, 2 * KD), products0)

            sums(1, D, lambda j: rows[:, data_b[0], j, 0:D], lambda i, b: pe.wait_ge(s_relu, RING * i + b + 1))
            pairs(pe, turn(1, KD))
            pe.wait_ge(s_ntc[1], NW)

            def z1_chunk(c, first):
                for m in range(KH):
                    if not first:
                        pe.wait_ge(s_z1, KH * (c - 1) + m + 1)
                    for k in range(KD):
                        last = nc.tensor.matmul(bank[2 + m][:, 0:CN], w1[:, k, 128 * m:128 * m + 128],
                                                hT[:, k, bass.ds(CN * c, CN)], start=(k == 0), stop=(k == KD - 1))
                    last.then_inc(s_z1p, 1)
            z1_chunk(0, True)
            with pe.Fori(1, NC) as c:
                z1_chunk(c, False)

            pe.wait_ge(s_z1n, KH)

            def z2_chunk(c, first):
                for m in range(KD):
                    if not first:
                        pe.wait_ge(s_z2, KD * (c - 1) + m + 1)
                    for k in range(KH):
                        last = nc.tensor.matmul(bank[m][:, 0:CN], w2[:, k, 128 * m:128 * m + 128],
                                                z1T[:, k, bass.ds(CN * c, CN)], start=(k == 0), stop=(k == KH - 1))
                    last.then_inc(s_z2p, 1)
            z2_chunk(0, True)
            with pe.Fori(1, NC) as c:
                z2_chunk(c, False)

            for n in range(2):
                pe.wait_ge(s_g, n + 1)
                nc.tensor.matmul(bank[4][:, 0:1], ones[:], g1[:, n:n + 1], start=True, stop=True).then_inc(s_gp, 1)

            def out_back(i, b, first):
                pe.wait_ge(s_ob, 2 * i + b + 1)
                if not first:
                    pe.wait_ge(s_ev[1], 2 * i + b - 1)
                for k in range(KD):
                    last = nc.tensor.transpose(bank[2 + b][0:WN, 128 * k:128 * k + 128],
                                               nodesT_b[:, b, WN * k:WN * k + WN], ident[:])
                last.then_inc(s_obt, 1)
            pairs(pe, out_back)

            def products2(i, b, first):
                pe.wait_ge(s_ntc[2], 2 * i + b + 1)
                for q in range(R // 2):
                    if not (first and b == 0):
                        pe.wait_ge(s_ev[2], R // 2 * (2 * i + b - 1) + q + 1)
                    for k in range(KD):
                        last = nc.tensor.matmul(bank[2 + q][0:WN, :], nodesT_b[:, b, WN * k:WN * k + WN],
                                                w_rel[:, k, 2 * q:2 * q + 2, :].rearrange("p r d -> p (r d)"),
                                                start=(k == 0), stop=(k == KD - 1))
                    last.then_inc(s_mm[2], 1)
            pe.wait_ge(s_wrel, 16 * KD)
            two_steps(turn(2, KD), products2)
            sums(2, D, lambda j: rows[:, data_b[0], j, 0:D],
                 lambda i, b: pe.wait_ge(s_rows[2][b], 16 * GT * (i + 1)))

            def products3(i, b, first):
                pe.wait_ge(s_ntc[3], 2 * i + b + 1)
                if not first:
                    pe.wait_ge(s_ev[3], 2 * i + b - 1)
                for k in range(KD):
                    last = nc.tensor.matmul(bank[2 + b][0:WN, 0:D], nodesT_b[:, b, WN * k:WN * k + WN], w_att[:, k, :],
                                            start=(k == 0), stop=(k == KD - 1))
                last.then_inc(s_mm[3], 1)
            two_steps(turn(3, KD), products3)

            visits, tiles = Visits(pe), Visits(pe, GT)

            def attention(w):
                v = visits.next()
                pe.wait_ge(s_onehot[3], v)
                for j in range(GT):
                    last = nc.tensor.transpose(bank[j // 4][0:WN, TE * (j % 4):TE * (j % 4) + TE], onehot[:, j, :], ident[:])
                last.then_inc(s_oht, 1)
                for j in range(GT):
                    pe.wait_ge(s_diag, tiles.next())
                    for q in range(2):
                        last = nc.tensor.matmul(bank[2 + q][0:WN, :], onehot[:, j, :],
                                                diag[:, 4 * q:4 * q + 4, :].rearrange("p h e -> p (h e)"), start=True, stop=True)
                    last.then_inc(s_spread, 1)
                pe.wait_ge(s_ref, v)
                for j in range(GT):
                    last = nc.tensor.matmul(bank[4][:, 2 * H * j:2 * H * j + 2 * H], onehot_t[:, TE * j:TE * j + TE],
                                            node_ref[:], start=True, stop=True)
                last.then_inc(s_back, 1)
                pe.wait_ge(s_msg, v)
                for j in range(GT):
                    last = nc.tensor.matmul(bank[6][0:WN, 0:DH], onehot[:, j, :], msg[:, j, :], start=(j == 0),
                                            stop=(j == GT - 1))
                last.then_inc(s_sum[3], 1)
            rings(pe, lambda i, b: each_window(pe, RING * i + b, attention))

        @block.vector
        def _(dve):
            V = nc.vector

            dve.wait_ge(s_edges, 48)
            V.tensor_copy(flt[:], raw[:])
            dve.drain()
            V.scalar_tensor_tensor(flt[:, 2, :], flt[:, 2, :], float(N), flt[:, 0, :], ALU.mult, ALU.add).then_inc(s_flt, 1)
            for k in range(2):
                V.tensor_reduce(span_f[:, k:k + 1], flt[:, k, :], AX.X, ALU.min)
                V.tensor_reduce(span_f[:, 2 + k:3 + k], flt[:, k, :], AX.X, ALU.max)
            dve.wait_ge(s_const, 1)
            dve.drain()
            for q in range(4):
                V.tensor_scalar(cmp[:, q, :], bounds[:], span_f[:, q:q + 1], None, ALU.is_le)
            dve.drain()
            V.tensor_reduce(rank[:, 0:4], cmp[:], AX.X, ALU.add)
            dve.drain()
            V.tensor_scalar(rank[:, 4:6], rank[:, 2:4], 1.0, 32.0, ALU.add, ALU.mult)
            dve.drain()
            V.tensor_tensor(span_f[:, 4:6], rank[:, 4:6], rank[:, 0:2], ALU.add).then_inc(s_flt, 1)
            dve.wait_ge(s_lists_t, 1)
            for i, ts in enumerate(((dst_f,), (src_idx, src_f), (rel_idx,))):
                for j in range(GT):
                    q = i * GT + j
                    for t in ts:
                        V.tensor_copy(t[:, 0:NG, j], bank[q // 4][:, 128 * (q % 4):128 * (q % 4) + NG])
            dve.wait_ge(s_lists_t, 2)
            V.tensor_copy(spans[:], bank[4][0:1, 0:2 * NG].rearrange("p (k g) -> p k g", k=2)).then_inc(s_lists, 1)

            def statistics(w, of):
                V.bn_stats(stats[:, bass.ds(w, 1), :].rearrange("p w s -> p (w s)"), of)

            def norm(l):
                dve.drain()
                for w in range(NW):
                    V.bn_aggr(mean_var[:, w, :], stats[:, w, :])
                dve.drain()
                V.tensor_scalar_add(rstd[:], mean_var[:, :, 1], EPS).then_inc(s_var[l], 1)
                dve.wait_ge(s_std[l], 1)
                V.reciprocal(rstd[:], rstd[:])
                dve.drain()
                V.scalar_tensor_tensor(shift[:], mean_var[:, :, 0], -1.0, rstd[:], ALU.mult, ALU.mult).then_inc(s_rstd[l], 1)

            def fill_slot(idx, g, b, l):
                V.tensor_copy(slot[:, b, :], idx[:, bass.ds(g, 1), :].rearrange("p g j -> p (g j)")).then_inc(s_slot[l], 1)

            def onehots(g, w, l, nodes=dst_f):
                for j in range(GT):
                    last = V.tensor_scalar(onehot[:, j, :], node_iota[:, bass.ds(w * WN, WN)],
                                           nodes[:, bass.ds(g, 1), j], None, ALU.is_equal)
                last.then_inc(s_onehot[l], 1)

            def sums(l, width, idx, before):
                for b in range(RING):
                    fill_slot(idx, b, b, l)
                visits = Visits(dve)
                dve.wait_ge(s_zero[l], 1)

                def step(i, b):
                    g = RING * i + b
                    before(i, b)

                    def visit(w):
                        v = visits.next()
                        onehots(g, w, l, src_f if l == 2 else dst_f)
                        dve.wait_ge(s_sum[l], v)
                        V.tensor_tensor(acc[:, bass.ds(w, 1), 0:width].rearrange("p w d -> p (w d)"),
                                        acc[:, bass.ds(w, 1), 0:width].rearrange("p w d -> p (w d)"),
                                        bank[6][0:WN, 0:width], ALU.add)
                        dve.drain()
                    each_window(dve, g, visit, by=int(l == 2))
                    fill_slot(idx, g + RING, b, l)
                rings(dve, step)

            dve.wait_ge(s_x, 16)
            with dve.Fori(0, NW) as w:
                statistics(w, window(x, w))
            norm(0)
            sums(0, D + 1, src_idx, lambda i, b: None)
            dve.drain()
            V.tensor_scalar_max(rstd[:], acc[:, :, D], 1.0)
            dve.drain()
            V.reciprocal(rstd[:], rstd[:])
            dve.drain()

            def stage0(i, b, first):
                if not first:
                    dve.wait_ge(s_nt[0], 2 * i + b - 1)
                w = 2 * i + b
                V.tensor_scalar(nodes_b[:, b, 0:D], acc[:, bass.ds(w, 1), 0:D].rearrange("p w d -> p (w d)"),
                                rstd[:, bass.ds(w, 1)], None, ALU.mult)
                V.tensor_copy(nodes_b[:, b, D:2 * D], window(h, w)).then_inc(s_nb[0], 1)

            def take0(i, b, first):
                w = 2 * i + b
                dve.wait_ge(s_mm[0], w + 1)
                V.tensor_tensor(prod[:, b, :], bank[2 + b][0:WN, 0:D], bias0[:], ALU.add).then_inc(s_ev[0], 1)
                dve.drain()
                V.tensor_tensor(window(x, w), window(x, w), prod[:, b, :], ALU.add)
                dve.drain()
                statistics(w, window(x, w))
            dve.wait_ge(s_w, 16 * WEIGHT_LOADS)

            def staged_and_taken(stage_, take):
                for b in range(2):
                    stage_(0, b, True)
                for b in range(2):
                    take(0, b, True)
                with dve.Fori(1, NW // 2) as i:
                    for b in range(2):
                        stage_(i, b, False)
                    for b in range(2):
                        take(i, b, False)
            staged_and_taken(stage0, take0)
            norm(1)

            def add_attr(i, b):
                dve.wait_ge(s_rows[1][b], 16 * GT * (i + 1))
                dve.wait_ge(s_attr[b], 16 * (i + 1))
                V.tensor_tensor(rows[:, b, :, 0:D], rows[:, b, :, 0:D], attr[:, b, :, :], ALU.add).then_inc(s_add, 1)
            sums(1, D, src_idx, add_attr)

            def stage1(i, b, first):
                if not first:
                    dve.wait_ge(s_nt[1], 2 * i + b - 1)
                w = 2 * i + b
                V.tensor_tensor(nodes_b[:, b, 0:D], acc[:, bass.ds(w, 1), 0:D].rearrange("p w d -> p (w d)"),
                                window(h, w), ALU.add).then_inc(s_nb[1], 1)
            pairs(dve, stage1)
            with dve.Fori(0, NC) as c:
                for m in range(KH):
                    dve.wait_ge(s_z1, KH * c + m + 1)
                    V.bn_stats(st1[:, m, bass.ds(c, 1), :].rearrange("p c s -> p (c s)"), z1T[:, m, bass.ds(CN * c, CN)])
            dve.drain()
            for m in range(KH):
                V.bn_aggr(mv1[:, m, :], st1[:, m, :, :].rearrange("p c s -> p (c s)"))
            dve.drain()
            V.tensor_scalar_add(sc1[:, 0, :], mv1[:, :, 1], EPS).then_inc(s_st1, 1)
            dve.wait_ge(s_sd1, 1)
            V.reciprocal(sc1[:, 0, :], sc1[:, 0, :])
            dve.drain()
            V.tensor_tensor(sc1[:, 0, :], sc1[:, 0, :], v1[:, 1, :], ALU.mult)
            dve.drain()
            V.tensor_tensor(sc1[:, 1, :], mv1[:, :, 0], sc1[:, 0, :], ALU.mult)
            dve.drain()
            V.tensor_tensor(sc1[:, 1, :], v1[:, 2, :], sc1[:, 1, :], ALU.subtract).then_inc(s_bn, 1)
            with dve.Fori(0, NC) as c:
                for m in range(KD):
                    dve.wait_ge(s_z2, KD * c + m + 1)
                    V.bn_stats(st2[:, m, bass.ds(c, 1), :].rearrange("p c s -> p (c s)"), hT[:, m, bass.ds(CN * c, CN)])
            dve.drain()
            for m in range(KD):
                V.bn_aggr(mv2[:, m, :], st2[:, m, :, :].rearrange("p c s -> p (c s)"))
            dve.drain()
            mean, var = mv2[:, :, 0], mv2[:, :, 1]
            ln_w, ln_b, gn_w, gn_b, gn_ms = (v2[:, i, :] for i in range(1, 6))
            V.tensor_reduce(g1[:, 0:1], mean, AX.X, ALU.add).then_inc(s_g, 1)
            dve.wait_ge(s_gp, 1)
            V.tensor_scalar(g1[:, 2:3], bank[4][:, 0:1], 1.0 / D, None, ALU.mult)
            dve.drain()
            V.tensor_scalar(t2[:, 0, :], mean, g1[:, 2:3], None, ALU.subtract)
            dve.drain()
            V.tensor_tensor(t2[:, 1, :], t2[:, 0, :], t2[:, 0, :], ALU.mult)
            dve.drain()
            V.tensor_tensor(t2[:, 1, :], t2[:, 1, :], var, ALU.add)
            dve.drain()
            V.tensor_reduce(g1[:, 1:2], t2[:, 1, :], AX.X, ALU.add).then_inc(s_g, 1)
            dve.wait_ge(s_gp, 2)
            V.tensor_scalar(g1[:, 3:4], bank[4][:, 0:1], 1.0 / D, EPS, ALU.mult, ALU.add).then_inc(s_sd, 1)
            dve.wait_ge(s_sdr, 1)
            V.reciprocal(g1[:, 3:4], g1[:, 3:4])
            dve.drain()
            V.tensor_scalar(t2[:, 2, :], ln_w, g1[:, 3:4], None, ALU.mult)
            dve.drain()
            V.tensor_tensor(t2[:, 3, :], t2[:, 0, :], t2[:, 2, :], ALU.mult)
            dve.drain()
            V.tensor_tensor(t2[:, 3, :], t2[:, 3, :], ln_b, ALU.add)
            dve.drain()
            V.tensor_tensor(t2[:, 4, :], t2[:, 3, :], gn_ms, ALU.mult)
            dve.drain()
            V.tensor_tensor(t2[:, 4, :], t2[:, 3, :], t2[:, 4, :], ALU.subtract)
            V.tensor_tensor(t2[:, 5, :], t2[:, 2, :], t2[:, 2, :], ALU.mult)
            dve.drain()
            V.tensor_tensor(t2[:, 5, :], t2[:, 5, :], var, ALU.mult)
            V.tensor_tensor(t2[:, 1, :], t2[:, 4, :], t2[:, 4, :], ALU.mult)
            dve.drain()
            V.scalar_tensor_tensor(t2[:, 5, :], t2[:, 5, :], EPS, t2[:, 1, :], ALU.add, ALU.add).then_inc(s_sd, 1)
            dve.wait_ge(s_sdr, 2)
            V.reciprocal(t2[:, 5, :], t2[:, 5, :])
            dve.drain()
            V.tensor_tensor(t2[:, 5, :], t2[:, 5, :], gn_w, ALU.mult)
            dve.drain()
            V.tensor_tensor(t2[:, 6, :], t2[:, 2, :], t2[:, 5, :], ALU.mult)
            V.tensor_tensor(t2[:, 7, :], t2[:, 4, :], t2[:, 5, :], ALU.mult)
            dve.drain()
            V.tensor_tensor(t2[:, 7, :], t2[:, 7, :], gn_b, ALU.add)
            V.tensor_tensor(t2[:, 1, :], t2[:, 6, :], mean, ALU.mult)
            dve.drain()
            V.tensor_tensor(t2[:, 7, :], t2[:, 7, :], t2[:, 1, :], ALU.subtract).then_inc(s_fin, 1)

            def take1(i, b, first):
                w = 2 * i + b
                dve.wait_ge(s_obt, w + 1)
                V.tensor_tensor(prod[:, b, :], bank[2 + b][0:WN, 0:D], window(h, w), ALU.add).then_inc(s_ev[1], 1)
                dve.drain()
                V.tensor_tensor(window(x, w), window(x, w), prod[:, b, :], ALU.add)
                dve.drain()
                statistics(w, window(x, w))
            pairs(dve, take1)
            norm(2)

            def stage_h(l):
                def step(i, b, first):
                    dve.wait_ge(s_h[l], 2 * i + b + 1)
                    if not first:
                        dve.wait_ge(s_nt[l], 2 * i + b - 1)
                    V.tensor_copy(nodes_b[:, b, 0:D], window(h, 2 * i + b)).then_inc(s_nb[l], 1)
                return step

            def take2(i, b, first):
                if not first:
                    dve.wait_ge(s_xt[b], 16 * i)
                for q in range(R // 2):
                    dve.wait_ge(s_mm[2], R // 2 * (2 * i + b) + q + 1)
                    V.tensor_copy(xt_out[:, b, 2 * D * q:2 * D * q + 2 * D], bank[2 + q][0:WN, :]).then_inc(s_ev[2], 1)
            staged_and_taken(stage_h(2), take2)
            sums(2, D, rel_idx, lambda i, b: None)
            dve.drain()
            V.tensor_tensor(acc[:, :, 0:D], acc[:, :, 0:D], bias_rel[:].rearrange("p (a d) -> p a d", a=1).broadcast_to([WN, NW, D]),
                            ALU.add)
            dve.drain()
            V.scalar_tensor_tensor(x[:], acc[:, :, 0:D], 0.0, x[:], ALU.max, ALU.add).then_inc(s_x_new[2], 1)
            dve.drain()
            with dve.Fori(0, NW) as w:
                statistics(w, window(x, w))
            norm(3)

            def take3(i, b, first):
                if not first:
                    dve.wait_ge(s_hh[b], 16 * i)
                w = 2 * i + b
                dve.wait_ge(s_mm[3], w + 1)
                hh = bank[2 + b][0:WN, 0:D]
                V.tensor_copy(hh_out[:, b, 0:D], hh)
                V.tensor_tensor(prod[:, 0, :], hh, a_src[:], ALU.mult)
                V.tensor_tensor(prod[:, 1, :], hh, a_dst[:], ALU.mult)
                dve.drain()
                V.tensor_reduce(window(s_dst, w), prod[:, 1, :].rearrange("p (h d) -> p h d", h=H), AX.X, ALU.add)
                V.tensor_reduce(hh_out[:, b, D:DH], prod[:, 0, :].rearrange("p (h d) -> p h d", h=H), AX.X, ALU.add
                                ).then_inc(s_ev[3], 1)
                dve.drain()
            staged_and_taken(stage_h(3), take3)
            V.memset(run_max[:], -BIG)
            for b in range(RING):
                fill_slot(src_idx, b, b, 3)
            visits, tiles = Visits(dve), Visits(dve, GT)
            dve.wait_ge(s_zero[3], 1)
            heads = lambda t: t.rearrange("p (h d) -> p h d", h=H)

            def attention(i, b):
                g = RING * i + b
                dve.wait_ge(s_rows[3][b], 16 * GT * (i + 1))

                def visit(w):
                    v = visits.next()
                    onehots(g, w, 3)
                    dve.wait_ge(s_ohtc, v)
                    V.tensor_scalar(penalty[:], onehot_t[:], BIG, -BIG, ALU.mult, ALU.add)
                    for j in range(GT):
                        s_src = rows[:, b, j, D:DH].rearrange("p (h e) -> p h e", e=1).broadcast_to([128, H, TE])
                        V.tensor_tensor(diag, ident[:].rearrange("p (h e) -> p h e", h=1).broadcast_to([128, H, TE]), s_src,
                                        ALU.mult).then_inc(s_diag, 1)
                        dve.drain()
                        dve.wait_ge(s_spread, tiles.next())
                        pen = penalty[:, TE * j:TE * j + TE].rearrange("p (h e) -> p h e", h=1).broadcast_to([WN, 4, TE])
                        for q in range(2):
                            V.tensor_tensor(masked[:, 4 * q:4 * q + 4, :],
                                            bank[2 + q][0:WN, :].rearrange("p (h e) -> p h e", h=4), pen, ALU.add)
                        dve.drain()
                        V.tensor_reduce(tile_max[:, j, :], masked, AX.X, ALU.max)
                    dve.drain()
                    V.tensor_reduce(node_ref[:, H:2 * H], tile_max[:].rearrange("p j h -> p h j"), AX.X, ALU.max)
                    dve.drain()
                    V.tensor_tensor(node_ref[:, H:2 * H], node_ref[:, H:2 * H], window(s_dst, w), ALU.add)
                    V.tensor_copy(node_ref[:, 0:H], window(s_dst, w))
                    dve.drain()
                    V.scalar_tensor_tensor(node_ref[:, H:2 * H], node_ref[:, H:2 * H], SLOPE, node_ref[:, H:2 * H],
                                           ALU.mult, ALU.max).then_inc(s_ref, 1)
                    dve.wait_ge(s_back, v)
                    back = bank[4][:, 0:GT * 2 * H].rearrange("p (j c) -> p j c", j=GT)
                    V.tensor_tensor(score[:], rows[:, b, :, D:DH], back[:, :, 0:H], ALU.add)
                    dve.drain()
                    V.scalar_tensor_tensor(score[:], score[:], SLOPE, score[:], ALU.mult, ALU.max)
                    dve.drain()
                    V.tensor_tensor(score[:], score[:], back[:, :, H:2 * H], ALU.subtract)
                    dve.drain()
                    V.tensor_scalar_min(score[:], score[:], 0.0).then_inc(s_arg, 1)
                    V.tensor_tensor(new_max[:], window(run_max, w), node_ref[:, H:2 * H], ALU.max)
                    dve.drain()
                    V.tensor_tensor(decay[:, 0, :], window(run_max, w), new_max[:], ALU.subtract)
                    V.tensor_tensor(decay[:, 1, :], node_ref[:, H:2 * H], new_max[:], ALU.subtract).then_inc(s_dec, 1)
                    dve.drain()
                    V.tensor_copy(window(run_max, w), new_max[:])
                    dve.wait_ge(s_exp, v)
                    weight = msg[:, :, D:DH].rearrange("p j (h e) -> p j h e", e=1).broadcast_to([128, GT, H, HD])
                    V.tensor_tensor(msg[:, :, 0:D].rearrange("p j (h d) -> p j h d", h=H),
                                    rows[:, b, :, 0:D].rearrange("p j (h d) -> p j h d", h=H), weight, ALU.mult
                                    ).then_inc(s_msg, 1)
                    dve.wait_ge(s_sum[3], v)
                    dve.wait_ge(s_dexp, v)
                    mine = acc[:, bass.ds(w, 1), :].rearrange("p w d -> p (w d)")
                    for of, to, dec in ((mine, mine, 0), (bank[6][0:WN, 0:DH], fresh[:], 1)):
                        e = decay[:, dec, :]
                        V.tensor_tensor(heads(to[:, 0:D]), heads(of[:, 0:D]),
                                        e.rearrange("p (h d) -> p h d", d=1).broadcast_to([WN, H, HD]), ALU.mult)
                        V.tensor_tensor(to[:, D:DH], of[:, D:DH], e, ALU.mult)
                    dve.drain()
                    V.tensor_tensor(mine, mine, fresh[:], ALU.add)
                    dve.drain()
                each_window(dve, g, visit)
                fill_slot(src_idx, g + RING, b, 3)
            rings(dve, attention)
            dve.drain()
            V.tensor_scalar_max(s_dst[:], acc[:, :, D:DH], 1e-30)
            dve.drain()
            V.reciprocal(s_dst[:], s_dst[:])
            dve.drain()
            V.tensor_tensor(acc[:, :, 0:D].rearrange("p w (h d) -> p w h d", h=H),
                            acc[:, :, 0:D].rearrange("p w (h d) -> p w h d", h=H),
                            s_dst[:].rearrange("p w (h d) -> p w h d", d=1).broadcast_to([WN, NW, H, HD]), ALU.mult)
            dve.drain()
            V.tensor_tensor(h[:], acc[:, :, 0:D], h[:], ALU.add)
            dve.drain()
            with dve.Fori(0, NW) as w:
                statistics(w, window(h, w))
            norm(4)
            dve.drain()
            with dve.Fori(0, NW) as w:
                V.tensor_scalar(window(h, w), window(h, w), rstd[:, bass.ds(w, 1)], shift[:, bass.ds(w, 1)], ALU.mult, ALU.add)
            dve.drain()
            all_windows = lambda t: t[:].rearrange("p (a d) -> p a d", a=1).broadcast_to([WN, NW, D])
            V.tensor_tensor(h[:], h[:], all_windows(gamma), ALU.mult)
            dve.drain()
            V.tensor_tensor(h[:], h[:], all_windows(beta), ALU.add)
            dve.drain()
            V.tensor_scalar_min(acc[:, :, 0:D], h[:], 0.0).then_inc(s_elu, 1)
            V.scalar_tensor_tensor(x[:], h[:], 0.0, x[:], ALU.max, ALU.add)
            dve.wait_ge(s_elud, 1)
            dve.drain()
            V.scalar_tensor_tensor(x[:], acc[:, :, 0:D], -1.0, x[:], ALU.add, ALU.add).then_inc(s_x_new[3], 1)


_INPUTS = ["x", "src", "dst", "edge_attr_256", "edge_type_8", "L0_gnn_W_l", "L0_gnn_W_r", "L0_gnn_b_r", "L1_gnn_W1",
           "L1_gnn_b1", "L1_gnn_bn_gamma", "L1_gnn_bn_beta", "L1_gnn_W2", "L1_gnn_b2", "L1_gnn_ln_w", "L1_gnn_ln_b",
           "L1_gnn_gn_w", "L1_gnn_gn_b", "L1_gnn_gn_ms", "L2_gnn_weight", "L2_gnn_bias", "L3_gnn_W", "L3_gnn_a_src",
           "L3_gnn_a_dst", "L3_gnn_gamma", "L3_gnn_beta"]
_TRANSPOSED = ("L0_gnn_W_l", "L0_gnn_W_r")


def kernel(**inputs):
    import numpy as np
    import concourse.bacc as bacc
    from concourse import mybir as mb
    from concourse.bass_utils import run_bass_kernel_spmd as run

    nc = bacc.Bacc("TRN2", target_bir_lowering=False, num_devices=1)
    arrays, aps = {}, {}
    for name in _INPUTS:
        v = np.asarray(inputs[name])
        v = np.ascontiguousarray(v.T if name in _TRANSPOSED else v)
        arrays[f"in_{name}"] = v
        aps[name] = nc.dram_tensor(f"in_{name}", v.shape, mb.dt.from_np(v.dtype), kind="ExternalInput").ap()
    out = nc.dram_tensor("out_x", arrays["in_x"].shape, mb.dt.float32, kind="ExternalOutput").ap()
    gnn_kernel(nc, aps, out)
    r = run(nc, [arrays], core_ids=[0])
    return r.results[0]["out_x"]
```

```python
from contextlib import ExitStack

import concourse.bass as bass
from concourse import mybir

F32 = mybir.dt.float32
I32 = mybir.dt.int32
F16 = mybir.dt.float16
ALU = mybir.AluOpType
ACT = mybir.ActivationFunctionType
AX = mybir.AxisListType


def gnn_kernel(nc, a, out):
    N, D = a["x"].shape
    E = a["src"].shape[0]
    NW, WN = 20, 125
    GT, TE = 5, 128
    GE = GT * TE
    NG = E // GE
    RING = 5
    assert NW * WN == N and NG * GE == E and NG % RING == 0 and NG <= 128
    R = a["L2_gnn_weight"].shape[0]
    H, HD = a["L3_gnn_a_src"].shape
    DH = D + H
    D1 = a["L1_gnn_W1"].shape[1]
    KD, KH = D // 128, D1 // 128
    NC, CN = 5, N // 5
    EPS = 1e-5
    BIG = 1e30
    SLOPE = 0.2
    WEIGHT_LOADS = 20
    MM_STEPS = {0: 1, 2: R // 2, 3: 1}

    with ExitStack() as ctx:
        def sb(name, shape, dt=F32):
            return ctx.enter_context(nc.sbuf_tensor(name, shape, dt))

        def sem(name):
            return ctx.enter_context(nc.semaphore(name))

        h_table = [nc.dram_tensor(f"h_table{l}", (N, D), F32, kind="Internal").ap() for l in range(2)]
        xt_table = nc.dram_tensor("xt_table", (R * N, D), F32, kind="Internal").ap()
        start_table = nc.dram_tensor("start_table", (NG, GE), F32, kind="Internal").ap()
        hh_table = nc.dram_tensor("hh_table", (N, DH), F32, kind="Internal").ap()

        x = sb("x", [WN, NW, D])
        h = sb("h", [WN, NW, D])
        acc = sb("acc", [WN, NW, DH])
        stats = sb("stats", [WN, NW, 6])
        mean_var = sb("mean_var", [WN, NW, 2])
        rstd = sb("rstd", [WN, NW])
        shift = sb("shift", [WN, NW])
        stage = sb("stage", [128, RING * GT * (DH + D)])
        rows = stage[:, 0:RING * GT * DH].rearrange("p (r j c) -> p r j c", r=RING, j=GT)
        attr = stage[:, RING * GT * DH:].rearrange("p (r j c) -> p r j c", r=RING, j=GT)
        src_idx = sb("src_idx", [128, NG + RING, GT], I32)
        rel_idx = sb("rel_idx", [128, NG + RING, GT], I32)
        dst_f = sb("dst_f", [128, NG, GT])
        slot = sb("slot", [128, RING, GT], I32)
        spans = sb("spans", [1, 2, NG], I32)
        src_f = sb("src_f", [128, NG, GT])
        onehot = sb("onehot", [128, GT, WN])
        node_iota = sb("node_iota", [128, N])
        ident = sb("ident", [128, 128])
        ones = sb("ones", [128, 128])
        hT = sb("hT", [128, KD, N])
        scratch = hT[:].rearrange("p k n -> p (k n)")
        onehot_t = scratch[0:WN, 0:GE]
        penalty = scratch[0:WN, GE:2 * GE]
        msg = scratch[:, 2 * GE:2 * GE + GT * DH].rearrange("p (j c) -> p j c", j=GT)
        run = scratch[0:H, 2 * GE + GT * DH:3 * GE + GT * DH]
        tail = stage[:, RING * GT * DH:]
        diag = tail[:, 0:H * TE].rearrange("p (h e) -> p h e", h=H)
        masked = tail[0:WN, H * TE:2 * H * TE].rearrange("p (h e) -> p h e", h=H)
        starts = tail[0:H, 2 * H * TE:2 * H * TE + RING * GE].rearrange("p (r e) -> p r e", r=RING)
        last_f = sb("last_f", [128, NG, GT])
        last_max = sb("last_max", [128, GT, H + 1])
        seen = sb("seen", [WN, 1])
        tile_max = sb("tile_max", [WN, GT, H])
        node_ref = sb("node_ref", [WN, 2 * H])
        score = sb("score", [128, GT, H])
        s_dst = sb("s_dst", [WN, NW, H])
        run_max = sb("run_max", [WN, NW, H])
        new_max = sb("new_max", [WN, H])
        decay = sb("decay", [WN, 2, H])
        fresh = sb("fresh", [WN, DH])
        z1T = stage[:, 0:KH * N].rearrange("p (k n) -> p k n", k=KH)
        nodes_b = sb("nodes_b", [WN, 2, 2 * D])
        nodesT_b = sb("nodesT_b", [128, 2, 4 * WN])
        xt_out = hT[0:WN, :, 0:R * D]
        hh_out = sb("hh_out", [WN, 2, DH])
        prod = sb("prod", [WN, 2, D])
        w0 = sb("w0", [128, 2 * KD, D])
        w1 = sb("w1", [128, KD, D1])
        w2 = sb("w2", [128, KH, D])
        w_rel = stage[:, RING * GT * (DH + D) - KD * R * D:].rearrange("p (k r d) -> p k r d", k=KD, r=R)
        w_att = sb("w_att", [128, KD, D])
        bias0 = sb("bias0", [WN, D])
        bias_rel = sb("bias_rel", [WN, D])
        gamma = sb("gamma", [WN, D])
        beta = sb("beta", [WN, D])
        a_src = sb("a_src", [WN, D])
        a_dst = sb("a_dst", [WN, D])
        v1 = sb("v1", [128, 3, KH])
        v2 = sb("v2", [128, 6, KD])
        st1 = sb("st1", [128, KH, NC, 6])
        mv1 = sb("mv1", [128, KH, 2])
        sc1 = sb("sc1", [128, 2, KH])
        st2 = sb("st2", [128, KD, NC, 6])
        mv2 = sb("mv2", [128, KD, 2])
        t2 = sb("t2", [128, 8, KD])
        g1 = sb("g1", [128, 4])
        psum = ctx.enter_context(nc.psum_tensor("psum", [128, 8 * 512], F32))
        bank = [psum[:, 512 * i:512 * i + 512] for i in range(8)]
        raw = stage[0:NG, 0:3 * GE].bitcast(I32).rearrange("p (a e) -> p a e", a=3)
        flt = stage[0:NG, 3 * GE:7 * GE].rearrange("p (a e) -> p a e", a=4)
        starts_g = stage[0:NG, 7 * GE:8 * GE]
        span_f = sb("span_f", [NG, 6])
        bounds = sb("bounds", [128, NW + RING + 1])
        cmp = sb("cmp", [NG, 2, NW - 1])
        rank = sb("rank", [NG, 7])
        src_g, rel_g, pos_g, win_g, above, inside, order = (scratch[0:NG, GE * k:GE * k + GE] for k in range(7))
        spare = stage[0:NG, 0:GE]
        iotas = scratch[:, 7 * GE:7 * GE + (NG * GT + 1 + TE) // 2].bitcast(F16)
        tile_iota, lane_iota = iotas[:, 0:NG * GT], iotas[:, NG * GT + 1:NG * GT + 1 + TE]
        zeros = sb("zeros", [128, 320])
        place_of_group = sb("place_of_group", [NG, 2])
        before = sb("before", [128, 128])
        reach = sb("reach", [NG, NW + 1])
        share = sb("share", [NG, NW])
        total = sb("total", [128, NW])
        offset = sb("offset", [128, NW])
        base = sb("base", [NG, NW + RING])
        moves = sb("moves", [128, 4, NG, GT])
        turn_t = scratch[:, 0:GT * 320].bitcast(F16).rearrange("p (j t) -> p j t", j=GT)
        turn_p = scratch[:, GT * 320:GT * 320 + GT * TE].bitcast(F16).rearrange("p (j k e) -> p j k e", j=GT, k=2)

        s_edges, s_x, s_w, s_const = sem("edges_loaded"), sem("x_loaded"), sem("weights_loaded"), sem("constants_ready")
        s_flt, s_lists_t, s_lists = sem("lists_float"), sem("lists_transposed"), sem("lists_ready")
        s_var = [sem(f"var_ready{l}") for l in range(5)]
        s_std = [sem(f"std_ready{l}") for l in range(5)]
        s_rstd = [sem(f"rstd_ready{l}") for l in range(5)]
        s_h = [sem(f"h_ready{l}") for l in range(4)]
        s_table = [sem(f"table_written{l}") for l in range(2)]
        s_x_new = {l: sem(f"x_new{l}") for l in (2, 3)}
        s_xt = [sem(f"xt_written{b}") for b in range(2)]
        s_hh = [sem(f"hh_written{b}") for b in range(2)]
        s_zero = [sem(f"acc_zero{l}") for l in range(4)]
        s_slot = [sem(f"slot_ready{l}") for l in range(4)]
        s_rows = [[sem(f"rows_gathered{l}_{b}") for b in range(RING)] for l in range(4)]
        s_attr = [sem(f"attr_loaded{b}") for b in range(RING)]
        s_onehot = [sem(f"onehot_ready{l}") for l in range(4)]
        s_sum = [sem(f"group_summed{l}") for l in range(4)]
        s_add, s_relu = sem("rows_added"), sem("rows_relu")
        s_nb, s_nt, s_ntc, s_mm, s_ev = ([sem(f"{n}{l}") for l in range(4)] for n in
                                         ("nodes_staged", "nodes_transposed", "nodesT_ready", "product_ready", "product_taken"))
        s_oht, s_ohtc, s_diag, s_spread, s_ref, s_back, s_arg, s_exp, s_msg, s_dec, s_dexp = (
            sem(n) for n in ("onehot_turned", "onehot_t_ready", "diag_ready", "scores_spread", "node_ref_ready",
                             "refs_at_edges", "exponent_ready", "exp_ready", "msg_ready", "decay_ready", "decay_exp"))
        s_z1p, s_z1, s_st1, s_sd1, s_bn, s_z1n = (sem(n) for n in ("z1_product", "z1_ready", "z1_stats", "z1_std", "bn_ready", "z1_normed"))
        s_z2p, s_z2, s_g = sem("z2_product"), sem("z2_ready"), sem("graph_sums_wanted")
        s_gp, s_sd, s_fin, s_ob, s_obt = sem("graph_sums"), sem("std_wanted"), sem("affine_ready"), sem("out_staged"), sem("out_transposed")
        s_sdr = sem("std_done")
        s_wrel = sem("w_rel_loaded")
        s_pen, s_pent, s_starts = sem("starts_ready"), sem("start_table_written"), [sem(f"starts_loaded{b}") for b in range(RING)]
        s_share, s_prefix, s_digits, s_digits_t, s_moves = (sem(n) for n in ("shares_ready", "shares_summed", "digits_ready", "digits_turned", "moves_ready"))
        s_turn, s_turned, s_perm, s_posi = sem("turns_ready"), sem("edges_turned"), sem("permuted_out"), sem("positions_ready")
        s_sT, s_run, s_runT, s_lastv, s_nmax = (sem(n) for n in ("scores_turned", "runs_ready", "runs_back", "last_max_ready", "node_max_ready"))
        s_scanned = sem("scans_seen")
        s_begun = sem("gathers_begun")
        s_elu, s_elud, s_out = sem("elu_arg"), sem("elu_done"), sem("out_written")

        def row_bc(v, n):
            return v.rearrange("(a d) -> a d", a=1).broadcast_to([n, v.shape[0]])

        def pairs(eng, step):
            for b in range(2):
                step(0, b, True)
            with eng.Fori(1, NW // 2) as i:
                for b in range(2):
                    step(i, b, False)

        def rings(eng, step):
            with eng.Fori(0, NG // RING) as i:
                for b in range(RING):
                    step(i, b)

        def each_window(eng, g, step, by=0, flag=False):
            word = eng.value_load(spans[0:1, by, bass.ds(g, 1)], min_val=0, max_val=1024 + 32 * NW + NW - 1)
            why = "the list holds windows of nodes"
            first = nc.s_assert_within(eng.snap(word & 31), 0, NW - 1, skip_runtime_bounds_check_because=why)
            end = nc.s_assert_within(eng.snap((word >> 5) & 31), 1, NW, skip_runtime_bounds_check_because=why)
            mixed = eng.snap(word >> 10) if flag else None
            with eng.Fori(first, end) as w:
                step(w, mixed) if flag else step(w)

        class Visits:

            def __init__(self, eng, steps=1):
                self.most = steps * NG * NW
                self.eng, self.reg = eng, eng.alloc_register(f"visits_{nc.next_id()}")
                eng.reg_mov(self.reg, 0)

            def next(self):
                self.eng.reg_add(self.reg, self.reg, 1)
                return self.eng.snap(self.reg, min_val=1, max_val=self.most)

        def window(t, w):
            return t[:, bass.ds(w, 1), :].rearrange("p w d -> p (w d)")

        block = ctx.enter_context(nc.Block())

        @block.sync
        def _(sp):
            for i, n in enumerate(("dst", "src", "edge_type_8")):
                sp.dma_start(raw[:, i, :], a[n].rearrange("(g e) -> g e", e=GE)).then_inc(s_edges, 16)
            sp.dma_start(x[:], a["x"].rearrange("(w p) d -> p w d", p=WN)).then_inc(s_x, 16)
            loads = [(w0[:, 0:KD, :], a["L0_gnn_W_l"].rearrange("(k p) d -> p k d", p=128)),
                     (w0[:, KD:2 * KD, :], a["L0_gnn_W_r"].rearrange("(k p) d -> p k d", p=128)),
                     (w1[:], a["L1_gnn_W1"].rearrange("(k p) d -> p k d", p=128)),
                     (w2[:], a["L1_gnn_W2"].rearrange("(k p) d -> p k d", p=128)),
                     (w_att[:], a["L3_gnn_W"].rearrange("(k p) d -> p k d", p=128))]
            loads += [(t[:], row_bc(a[n], WN)) for t, n in ((bias0, "L0_gnn_b_r"), (bias_rel, "L2_gnn_bias"),
                                                           (gamma, "L3_gnn_gamma"), (beta, "L3_gnn_beta"))]
            loads += [(t[:], row_bc(a[n].rearrange("h d -> (h d)"), WN)) for t, n in
                      ((a_src, "L3_gnn_a_src"), (a_dst, "L3_gnn_a_dst"))]
            loads += [(v1[:, i, :], a["L1_gnn_" + n].rearrange("(k p) -> p k", p=128))
                      for i, n in enumerate(("b1", "bn_gamma", "bn_beta"))]
            loads += [(v2[:, i, :], a["L1_gnn_" + n].rearrange("(k p) -> p k", p=128))
                      for i, n in enumerate(("b2", "ln_w", "ln_b", "gn_w", "gn_b", "gn_ms"))]
            assert len(loads) == WEIGHT_LOADS
            with nc.allow_non_contiguous_dma("vectors of a few hundred elements"):
                for dst, src in loads:
                    sp.dma_start(dst, src).then_inc(s_w, 16)

            sp.wait_ge(s_pen, 1)
            sp.dma_start(start_table, starts_g).then_inc(s_pent, 16)
            sp.wait_ge(s_h[0], NW)
            sp.dma_start(h_table[0].rearrange("(w p) d -> p w d", p=WN), h[:]).then_inc(s_table[0], 16)
            sp.wait_ge(s_h[1], NW)
            sp.dma_start(h_table[1].rearrange("(w p) d -> p w d", p=WN), h[:]).then_inc(s_table[1], 16)

            attr_h = a["edge_attr_256"].rearrange("(g j p) d -> g p j d", j=GT, p=TE)
            for b in range(RING):
                sp.dma_start(attr[:, b, :, :], attr_h[b, :, :, :]).then_inc(s_attr[b], 16)
            with sp.Fori(0, NG // RING - 1) as i:
                for b in range(RING):
                    sp.wait_ge(s_add, RING * i + b + 1)
                    sp.dma_start(attr[:, b, :, :],
                                 attr_h[bass.ds(RING * i + RING + b, 1), :, :, :].rearrange("g p j d -> (g p) j d")
                                 ).then_inc(s_attr[b], 16)

            sp.wait_ge(s_z2p, KD * NC)
            for k in range(KD):
                sp.dma_start(w_rel[:, k, :, :], a["L2_gnn_weight"][:, 128 * k:128 * k + 128, :].rearrange("r p d -> p r d")
                             ).then_inc(s_wrel, 16)

            xt_h = xt_table.rearrange("(r w p) d -> w p r d", r=R, p=WN)

            def store_xt(i, b, first):
                sp.wait_ge(s_ev[2], R // 2 * (2 * i + b + 1))
                sp.dma_start(xt_h[bass.ds(2 * i + b, 1), :, :, :].rearrange("w p r d -> (w p) r d"),
                             xt_out[:, b, :].rearrange("p (r d) -> p r d", r=R)).then_inc(s_xt[b], 16)
            pairs(sp, store_xt)

            hh_h = hh_table.rearrange("(w p) d -> w p d", p=WN)

            def store_hh(i, b, first):
                sp.wait_ge(s_ev[3], 2 * i + b + 1)
                sp.dma_start(hh_h[bass.ds(2 * i + b, 1), :, :].rearrange("w p d -> (w p) d"),
                             hh_out[:, b, :]).then_inc(s_hh[b], 16)
            pairs(sp, store_hh)

            def load_starts(g, b):
                sp.dma_start(starts[:, b, :], start_table[bass.ds(g, 1), :].broadcast_to([H, GE])).then_inc(s_starts[b], 16)
            sp.wait_ge(s_x_new[2], 1)
            for b in range(RING):
                load_starts(b, b)
            with sp.Fori(0, NG // RING - 1) as i:
                for b in range(RING):
                    sp.wait_ge(s_slot[3], RING * i + b + 1 + RING)
                    load_starts(RING * i + b + RING, b)
            sp.wait_ge(s_x_new[3], 1)
            sp.dma_start(out.rearrange("(w p) d -> p w d", p=WN), x[:]).then_inc(s_out, 16)
            sp.wait_ge(s_out, 16)

        @block.gpsimd
        def _(pool):
            nc.gpsimd.memset(ident[:], 0.0)
            nc.gpsimd.memset(ones[:], 1.0)
            nc.gpsimd.memset(src_idx[:, NG:, :], 0)
            nc.gpsimd.memset(rel_idx[:, NG:, :], 0)
            nc.gpsimd.memset(zeros[:], 0.0)
            nc.gpsimd.iota(place_of_group[:], [[GE - 1, 2]], base=0, channel_multiplier=GE, allow_small_or_imprecise_dtypes=True)
            nc.gpsimd.memset(before[:], 1.0)
            nc.gpsimd.memset(base[:], 0.0)
            nc.gpsimd.iota(tile_iota, [[1, NG * GT]], base=0, channel_multiplier=0, allow_small_or_imprecise_dtypes=True)
            nc.gpsimd.iota(lane_iota, [[1, TE]], base=0, channel_multiplier=0, allow_small_or_imprecise_dtypes=True)
            nc.gpsimd.iota(bounds[:], [[WN, NW + RING + 1]], base=0, channel_multiplier=0, allow_small_or_imprecise_dtypes=True)
            nc.gpsimd.iota(node_iota[:], [[1, N]], base=0, channel_multiplier=0, allow_small_or_imprecise_dtypes=True)
            pool.drain()
            nc.gpsimd.affine_select(out=before[:], in_=before[:], compare_op=ALU.is_gt, fill=0.0, base=0,
                                    pattern=[[1, 128]], channel_multiplier=-1)
            nc.gpsimd.affine_select(out=ident[:], in_=ident[:], compare_op=ALU.not_equal, fill=1.0, base=0,
                                    pattern=[[-1, 128]], channel_multiplier=1).then_inc(s_const, 1)
            nc.gpsimd.memset(acc[:], 0.0).then_inc(s_zero[0], 1)
            pool.wait_ge(s_lists, 1)
            pool.wait_ge(s_pent, 16)
            nc.gpsimd.memset(rows[:, :, :, D:D + 1], 1.0).then_inc(s_zero[0], 1)

            def gathers(l, table, width, written):
                for s, n in written:
                    pool.wait_ge(s, n)

                def step(i, b):
                    pool.wait_ge(s_slot[l], RING * i + b + 1)
                    pool.sem_inc(s_begun, 1)
                    for j in range(GT):
                        pool.indirect_dma_start(rows[:, b, j, 0:width], None, table,
                                                bass.IndirectOffsetOnAxis(ap=slot[:, b, j:j + 1], axis=0)
                                                ).then_inc(s_rows[l][b], 16)
                rings(pool, step)

            gathers(0, h_table[0], D, [(s_table[0], 16)])
            pool.wait_ge(s_nb[0], NW)
            nc.gpsimd.memset(acc[:], 0.0).then_inc(s_zero[1], 1)
            gathers(1, h_table[1], D, [(s_table[1], 16)])
            pool.wait_ge(s_perm, 1)
            nc.gpsimd.iota(moves[:, 2, :, :].rearrange("p g j -> p (g j)"), [[TE, NG * GT]], base=0, channel_multiplier=1,
                           allow_small_or_imprecise_dtypes=True).then_inc(s_posi, 1)
            pool.wait_ge(s_nb[1], NW)
            nc.gpsimd.memset(acc[:], 0.0).then_inc(s_zero[2], 1)
            gathers(2, xt_table, D, [(s_xt[b], 16 * NW // 2) for b in range(2)])
            pool.wait_ge(s_x_new[2], 1)
            nc.gpsimd.memset(acc[:], 0.0).then_inc(s_zero[3], 1)
            gathers(3, hh_table, DH, [(s_hh[b], 16 * NW // 2) for b in range(2)])

        @block.scalar
        def _(act):
            def normed(l):
                act.wait_ge(s_var[l], 1)
                nc.scalar.activation(rstd[:], rstd[:], ACT.Sqrt).then_inc(s_std[l], 1)
                act.wait_ge(s_rstd[l], 1)
                with act.Fori(0, NW) as w:
                    nc.scalar.activation(window(h, w), window(x, w), ACT.Relu,
                                         bias=shift[:, bass.ds(w, 1)], scale=rstd[:, bass.ds(w, 1)]).then_inc(s_h[l], 1)

            def turned(l, blocks):
                def step(i, b, first):
                    act.wait_ge(s_nt[l], 2 * i + b + 1)
                    if not first:
                        act.wait_ge(s_mm[l], MM_STEPS[l] * (2 * i + b - 1))
                    nc.scalar.activation(nodesT_b[:, b, 0:blocks * WN], bank[b][:, 0:blocks * WN], ACT.Copy
                                         ).then_inc(s_ntc[l], 1)
                pairs(act, step)

            normed(0)
            turned(0, 2 * KD)
            normed(1)

            def relu_rows(i, b):
                act.wait_ge(s_add, RING * i + b + 1)
                nc.scalar.activation(rows[:, b, :, 0:D], rows[:, b, :, 0:D], ACT.Relu).then_inc(s_relu, 1)
            rings(act, relu_rows)

            def keep_hT(i, b, first):
                act.wait_ge(s_nt[1], 2 * i + b + 1)
                nc.scalar.activation(hT[:, :, bass.ds(WN * (2 * i + b), WN)],
                                     bank[b][:, 0:KD * WN].rearrange("p (k n) -> p k n", k=KD), ACT.Copy
                                     ).then_inc(s_ntc[1], 1)
            pairs(act, keep_hT)
            with act.Fori(0, NC) as c:
                for m in range(KH):
                    act.wait_ge(s_z1p, KH * c + m + 1)
                    nc.scalar.activation(z1T[:, m, bass.ds(CN * c, CN)], bank[2 + m][:, 0:CN], ACT.Identity,
                                         bias=v1[:, 0, m:m + 1]).then_inc(s_z1, 1)
            act.wait_ge(s_st1, 1)
            nc.scalar.activation(sc1[:, 0, :], sc1[:, 0, :], ACT.Sqrt).then_inc(s_sd1, 1)
            act.wait_ge(s_bn, 1)
            for m in range(KH):
                nc.scalar.activation(z1T[:, m, :], z1T[:, m, :], ACT.Relu, bias=sc1[:, 1, m:m + 1],
                                     scale=sc1[:, 0, m:m + 1]).then_inc(s_z1n, 1)
            with act.Fori(0, NC) as c:
                for m in range(KD):
                    act.wait_ge(s_z2p, KD * c + m + 1)
                    nc.scalar.activation(hT[:, m, bass.ds(CN * c, CN)], bank[m][:, 0:CN], ACT.Identity,
                                         bias=v2[:, 0, m:m + 1]).then_inc(s_z2, 1)
            act.wait_ge(s_sd, 1)
            nc.scalar.activation(g1[:, 3:4], g1[:, 3:4], ACT.Sqrt).then_inc(s_sdr, 1)
            act.wait_ge(s_sd, 2)
            nc.scalar.activation(t2[:, 5, :], t2[:, 5, :], ACT.Sqrt).then_inc(s_sdr, 1)
            act.wait_ge(s_fin, 1)

            def final_relu(i, b, first):
                if not first:
                    act.wait_ge(s_obt, 2 * i + b - 1)
                for k in range(KD):
                    last = nc.scalar.activation(nodesT_b[:, b, WN * k:WN * k + WN], hT[:, k, bass.ds(WN * (2 * i + b), WN)],
                                                ACT.Relu, bias=t2[:, 7, k:k + 1], scale=t2[:, 6, k:k + 1])
                last.then_inc(s_ob, 1)
            pairs(act, final_relu)

            normed(2)
            turned(2, KD)
            normed(3)
            turned(3, KD)

            def attention(w):
                v = visits.next()
                act.wait_ge(s_oht, v)
                nc.scalar.activation(onehot_t[:, 0:4 * TE], bank[0][0:WN, :], ACT.Copy)
                nc.scalar.activation(onehot_t[:, 4 * TE:], bank[1][0:WN, 0:TE], ACT.Copy).then_inc(s_ohtc, 1)
                act.wait_ge(s_arg, v)
                nc.scalar.activation(msg[:, :, D:DH], score[:], ACT.Exp).then_inc(s_exp, 1)
                act.wait_ge(s_dec, v)
                nc.scalar.activation(decay[:], decay[:], ACT.Exp).then_inc(s_dexp, 1)
            visits = Visits(act)
            rings(act, lambda i, b: each_window(act, RING * i + b, attention))

            act.wait_ge(s_var[4], 1)
            nc.scalar.activation(rstd[:], rstd[:], ACT.Sqrt).then_inc(s_std[4], 1)
            act.wait_ge(s_elu, 1)
            nc.scalar.activation(acc[:, :, 0:D], acc[:, :, 0:D], ACT.Exp).then_inc(s_elud, 1)

        @block.tensor
        def _(pe):
            pe.wait_ge(s_const, 1)
            pe.wait_ge(s_flt, 1)
            for i, part in enumerate((flt[:, 0, :], flt[:, 1, :], flt[:, 3, :])):
                for j in range(GT):
                    q = i * GT + j
                    last = nc.tensor.transpose(bank[q // 4][:, 128 * (q % 4):128 * (q % 4) + NG],
                                               part[:, TE * j:TE * j + TE], ident[0:NG, 0:NG])
            last.then_inc(s_lists_t, 1)
            pe.wait_ge(s_flt, 2)
            nc.tensor.transpose(bank[4][0:1, 0:NG], span_f[:, 2:3], ident[0:NG, 0:NG]).then_inc(s_lists_t, 1)
            pe.wait_ge(s_share, 1)
            nc.tensor.matmul(bank[5][0:NG, 0:NW], before[0:NG, 0:NG], share[:], start=True, stop=True)
            nc.tensor.matmul(bank[5][:, NW:2 * NW], ones[0:NG, :], share[:], start=True, stop=True).then_inc(s_prefix, 1)

            def turn(l, blocks):
                def step(i, b, first):
                    pe.wait_ge(s_nb[l], 2 * i + b + 1)
                    if not first:
                        pe.wait_ge(s_ntc[l], 2 * i + b - 1)
                    for k in range(blocks):
                        last = nc.tensor.transpose(bank[b][:, WN * k:WN * k + WN], nodes_b[:, b, 128 * k:128 * k + 128],
                                                   ident[0:WN, 0:WN])
                    last.then_inc(s_nt[l], 1)
                return step

            def two_steps(first_step, second_step):
                for b in range(2):
                    first_step(0, b, True)
                for b in range(2):
                    second_step(0, b, True)
                with pe.Fori(1, NW // 2) as i:
                    for b in range(2):
                        first_step(i, b, False)
                    for b in range(2):
                        second_step(i, b, False)

            def sums(l, width, data, ready, after=lambda i, b: None):
                visits = Visits(pe)

                def visit(w):
                    pe.wait_ge(s_onehot[l], visits.next())
                    for j in range(GT):
                        last = nc.tensor.matmul(bank[6][0:WN, 0:width], onehot[:, j, :], data(j), start=(j == 0),
                                                stop=(j == GT - 1))
                    last.then_inc(s_sum[l], 1)

                def step(i, b):
                    ready(i, b)
                    data_b[0] = b
                    each_window(pe, RING * i + b, visit, by=int(l == 2))
                    after(i, b)
                rings(pe, step)

            data_b = [0]
            pe.wait_ge(s_zero[0], 2)
            sums(0, D + 1, lambda j: rows[:, data_b[0], j, 0:D + 1],
                 lambda i, b: pe.wait_ge(s_rows[0][b], 16 * GT * (i + 1)))
            pe.wait_ge(s_digits, 1)
            for i, part in enumerate((order, inside, above, rel_g)):
                for j in range(GT):
                    q = i * GT + j
                    last = nc.tensor.transpose(bank[q // 4][:, 128 * (q % 4):128 * (q % 4) + NG],
                                               part[:, TE * j:TE * j + TE], ident[0:NG, 0:NG])
            last.then_inc(s_digits_t, 1)
            pe.wait_ge(s_moves, 1)
            pe.wait_ge(s_w, 16 * WEIGHT_LOADS)

            def products0(i, b, first):
                pe.wait_ge(s_ntc[0], 2 * i + b + 1)
                if not first:
                    pe.wait_ge(s_ev[0], 2 * i + b - 1)
                for k in range(2 * KD):
                    last = nc.tensor.matmul(bank[2 + b][0:WN, 0:D], nodesT_b[:, b, WN * k:WN * k + WN], w0[:, k, :],
                                            start=(k == 0), stop=(k == 2 * KD - 1))
                last.then_inc(s_mm[0], 1)
            two_steps(turn(0, 2 * KD), products0)

            HALF = (NG * GT + 1) // 2

            def permute(j_stat, j_mov, start, stop):
                for k in range(2):
                    for part in range(2):
                        n = min(HALF, NG * GT - HALF * part)
                        last = nc.tensor.matmul(bank[2 * k + part][:, 0:n], j_stat(k), j_mov(HALF * part, n), start=start, stop=stop)
                return last
            pe.wait_ge(s_ntc[0], NW)
            pe.wait_ge(s_ev[0], NW)
            permute(lambda k: ident[:], lambda o, n: zeros[:, 0:n], True, False).then_inc(s_turned, 1)

            def permute_group(i, b):
                pe.wait_ge(s_turn, RING * i + b + 1)
                for j in range(GT):
                    last = permute(lambda k: turn_p[:, j, k, :], lambda o, n: turn_t[:, j, o:o + n], False, False)
                last.then_inc(s_turned, 1)
            sums(1, D, lambda j: rows[:, data_b[0], j, 0:D], lambda i, b: pe.wait_ge(s_relu, RING * i + b + 1),
                 permute_group)
            permute(lambda k: ident[:], lambda o, n: zeros[:, 0:n], False, True).then_inc(s_turned, 1)
            pe.wait_ge(s_perm, 1)
            pairs(pe, turn(1, KD))
            pe.wait_ge(s_ntc[1], NW)

            def z1_chunk(c, first):
                for m in range(KH):
                    if not first:
                        pe.wait_ge(s_z1, KH * (c - 1) + m + 1)
                    for k in range(KD):
                        last = nc.tensor.matmul(bank[2 + m][:, 0:CN], w1[:, k, 128 * m:128 * m + 128],
                                                hT[:, k, bass.ds(CN * c, CN)], start=(k == 0), stop=(k == KD - 1))
                    last.then_inc(s_z1p, 1)
            z1_chunk(0, True)
            with pe.Fori(1, NC) as c:
                z1_chunk(c, False)

            pe.wait_ge(s_z1n, KH)

            def z2_chunk(c, first):
                for m in range(KD):
                    if not first:
                        pe.wait_ge(s_z2, KD * (c - 1) + m + 1)
                    for k in range(KH):
                        last = nc.tensor.matmul(bank[m][:, 0:CN], w2[:, k, 128 * m:128 * m + 128],
                                                z1T[:, k, bass.ds(CN * c, CN)], start=(k == 0), stop=(k == KH - 1))
                    last.then_inc(s_z2p, 1)
            z2_chunk(0, True)
            with pe.Fori(1, NC) as c:
                z2_chunk(c, False)

            for n in range(2):
                pe.wait_ge(s_g, n + 1)
                nc.tensor.matmul(bank[4][:, 0:1], ones[:], g1[:, n:n + 1], start=True, stop=True).then_inc(s_gp, 1)

            def out_back(i, b, first):
                pe.wait_ge(s_ob, 2 * i + b + 1)
                if not first:
                    pe.wait_ge(s_ev[1], 2 * i + b - 1)
                for k in range(KD):
                    last = nc.tensor.transpose(bank[2 + b][0:WN, 128 * k:128 * k + 128],
                                               nodesT_b[:, b, WN * k:WN * k + WN], ident[:])
                last.then_inc(s_obt, 1)
            pairs(pe, out_back)

            def products2(i, b, first):
                pe.wait_ge(s_ntc[2], 2 * i + b + 1)
                for q in range(R // 2):
                    if not (first and b == 0):
                        pe.wait_ge(s_ev[2], R // 2 * (2 * i + b - 1) + q + 1)
                    for k in range(KD):
                        last = nc.tensor.matmul(bank[2 + q][0:WN, :], nodesT_b[:, b, WN * k:WN * k + WN],
                                                w_rel[:, k, 2 * q:2 * q + 2, :].rearrange("p r d -> p (r d)"),
                                                start=(k == 0), stop=(k == KD - 1))
                    last.then_inc(s_mm[2], 1)
            pe.wait_ge(s_wrel, 16 * KD)
            two_steps(turn(2, KD), products2)
            pe.wait_ge(s_flt, 3)
            nc.tensor.transpose(bank[6][0:1, 0:NG], span_f[:, 2:3], ident[0:NG, 0:NG]).then_inc(s_lists_t, 1)
            pe.wait_ge(s_lists, 2)
            sums(2, D, lambda j: rows[:, data_b[0], j, 0:D],
                 lambda i, b: pe.wait_ge(s_rows[2][b], 16 * GT * (i + 1)))

            def products3(i, b, first):
                pe.wait_ge(s_ntc[3], 2 * i + b + 1)
                if not first:
                    pe.wait_ge(s_ev[3], 2 * i + b - 1)
                for k in range(KD):
                    last = nc.tensor.matmul(bank[2 + b][0:WN, 0:D], nodesT_b[:, b, WN * k:WN * k + WN], w_att[:, k, :],
                                            start=(k == 0), stop=(k == KD - 1))
                last.then_inc(s_mm[3], 1)
            two_steps(turn(3, KD), products3)

            visits, tiles = Visits(pe), Visits(pe, GT)

            fast = Visits(pe)

            def highest_by_scan():
                u = fast.next()
                for j in range(GT):
                    last = nc.tensor.transpose(psum[0:H, 1024 + TE * j:1024 + TE * j + TE], rows[:, data_b[0], j, D:DH], ident[:])
                last.then_inc(s_sT, 1)
                pe.wait_ge(s_run, u)
                pe.sem_inc(s_scanned, 1)
                for j in range(GT):
                    last = nc.tensor.transpose(bank[5][:, H * j:H * j + H], run[:, TE * j:TE * j + TE], ident[0:H, 0:H])
                last.then_inc(s_runT, 1)
                pe.wait_ge(s_lastv, u)
                for j in range(GT):
                    last = nc.tensor.matmul(bank[7][0:WN, 0:H + 1], onehot[:, j, :], last_max[:, j, :], start=(j == 0), stop=(j == GT - 1))
                last.then_inc(s_nmax, 1)

            def highest_by_mask():
                for j in range(GT):
                    pe.wait_ge(s_diag, tiles.next())
                    for q in range(2):
                        last = nc.tensor.matmul(bank[2 + q][0:WN, :], onehot[:, j, :],
                                                diag[:, 4 * q:4 * q + 4, :].rearrange("p h e -> p (h e)"), start=True, stop=True)
                    last.then_inc(s_spread, 1)

            def attention(w, mixed):
                v = visits.next()
                pe.wait_ge(s_onehot[3], v)
                for j in range(GT):
                    last = nc.tensor.transpose(bank[j // 4][0:WN, TE * (j % 4):TE * (j % 4) + TE], onehot[:, j, :], ident[:])
                last.then_inc(s_oht, 1)
                with pe.If(mixed > 0):
                    highest_by_mask()
                with pe.Else():
                    highest_by_scan()
                pe.wait_ge(s_ref, v)
                for j in range(GT):
                    last = nc.tensor.matmul(bank[4][:, 2 * H * j:2 * H * j + 2 * H], onehot_t[:, TE * j:TE * j + TE],
                                            node_ref[:], start=True, stop=True)
                last.then_inc(s_back, 1)
                pe.wait_ge(s_msg, v)
                for j in range(GT):
                    last = nc.tensor.matmul(bank[6][0:WN, 0:DH], onehot[:, j, :], msg[:, j, :], start=(j == 0),
                                            stop=(j == GT - 1))
                last.then_inc(s_sum[3], 1)
            def step3(i, b):
                pe.wait_ge(s_rows[3][b], 16 * GT * (i + 1))
                data_b[0] = b
                each_window(pe, RING * i + b, attention, flag=True)
            rings(pe, step3)

        @block.vector
        def _(dve):
            V = nc.vector

            dve.wait_ge(s_edges, 48)
            V.tensor_copy(flt[:, 0:3, :], raw[:])
            dve.drain()
            V.tensor_tensor(flt[:, 3, 0:GE - 1], flt[:, 0, 0:GE - 1], flt[:, 0, 1:GE], ALU.not_equal)
            V.memset(flt[:, 3, GE - 1:GE], 1.0).then_inc(s_flt, 1)
            V.scalar_tensor_tensor(rel_g, flt[:, 2, :], float(N), flt[:, 0, :], ALU.mult, ALU.add)
            V.tensor_copy(src_g, flt[:, 1, :])
            dve.drain()
            V.tensor_tensor(flt[:, 2, 0:GE - 1], flt[:, 0, 0:GE - 1], flt[:, 0, 1:GE], ALU.is_gt)
            V.tensor_reduce(span_f[:, 0:1], flt[:, 0, :], AX.X, ALU.min)
            V.tensor_reduce(span_f[:, 1:2], flt[:, 0, :], AX.X, ALU.max)
            dve.drain()
            V.memset(starts_g[:, 0:1], -BIG)
            V.tensor_scalar(starts_g[:, 1:GE], flt[:, 3, 0:GE - 1], -BIG, None, ALU.mult).then_inc(s_pen, 1)
            V.tensor_reduce(rank[:, 6:7], flt[:, 2, 0:GE - 1], AX.X, ALU.max)
            dve.wait_ge(s_const, 1)
            dve.drain()
            def span(windows):
                for q in range(2):
                    V.tensor_scalar(cmp[:, q, :], windows, span_f[:, q:q + 1], None, ALU.is_le)
                dve.drain()
                V.tensor_reduce(rank[:, 0:2], cmp[:], AX.X, ALU.add)
                dve.drain()
                V.tensor_scalar(rank[:, 2:3], rank[:, 1:2], 1.0, 32.0, ALU.add, ALU.mult)
                dve.drain()
                V.tensor_tensor(span_f[:, 2:3], rank[:, 2:3], rank[:, 0:1], ALU.add)
                dve.drain()
            span(bounds[0:NG, 1:NW])
            V.scalar_tensor_tensor(span_f[:, 2:3], rank[:, 6:7], 1024.0, span_f[:, 2:3], ALU.mult, ALU.add).then_inc(s_flt, 1)
            dve.wait_ge(s_lists_t, 1)
            for i, t in enumerate((dst_f, src_idx, last_f)):
                for j in range(GT):
                    q = i * GT + j
                    V.tensor_copy(t[:, 0:NG, j], bank[q // 4][:, 128 * (q % 4):128 * (q % 4) + NG])
            dve.wait_ge(s_lists_t, 2)
            V.tensor_copy(spans[0:1, 0, :], bank[4][0:1, 0:NG]).then_inc(s_lists, 1)

            def statistics(w, of):
                V.bn_stats(stats[:, bass.ds(w, 1), :].rearrange("p w s -> p (w s)"), of)

            def norm(l):
                dve.drain()
                for w in range(NW):
                    V.bn_aggr(mean_var[:, w, :], stats[:, w, :])
                dve.drain()
                V.tensor_scalar_add(rstd[:], mean_var[:, :, 1], EPS).then_inc(s_var[l], 1)
                dve.wait_ge(s_std[l], 1)
                V.reciprocal(rstd[:], rstd[:])
                dve.drain()
                V.scalar_tensor_tensor(shift[:], mean_var[:, :, 0], -1.0, rstd[:], ALU.mult, ALU.mult).then_inc(s_rstd[l], 1)

            def fill_slot(idx, g, b, l):
                V.tensor_copy(slot[:, b, :], idx[:, bass.ds(g, 1), :].rearrange("p g j -> p (g j)")).then_inc(s_slot[l], 1)

            def onehots(g, w, l, nodes=dst_f):
                for j in range(GT):
                    last = V.tensor_scalar(onehot[:, j, :], node_iota[:, bass.ds(w * WN, WN)],
                                           nodes[:, bass.ds(g, 1), j], None, ALU.is_equal)
                last.then_inc(s_onehot[l], 1)

            def sums(l, width, idx, before):
                for b in range(RING):
                    fill_slot(idx, b, b, l)
                visits = Visits(dve)
                dve.wait_ge(s_zero[l], 1)

                def step(i, b):
                    g = RING * i + b
                    before(i, b)

                    def visit(w):
                        v = visits.next()
                        onehots(g, w, l, src_f if l == 2 else dst_f)
                        dve.wait_ge(s_sum[l], v)
                        V.tensor_tensor(acc[:, bass.ds(w, 1), 0:width].rearrange("p w d -> p (w d)"),
                                        acc[:, bass.ds(w, 1), 0:width].rearrange("p w d -> p (w d)"),
                                        bank[6][0:WN, 0:width], ALU.add)
                        dve.drain()
                    each_window(dve, g, visit, by=int(l == 2))
                    fill_slot(idx, g + RING, b, l)
                rings(dve, step)

            dve.wait_ge(s_x, 16)
            with dve.Fori(0, NW) as w:
                statistics(w, window(x, w))
            norm(0)
            V.memset(reach[:, 0:1], float(GE))
            V.memset(reach[:, NW:NW + 1], 0.0)
            with dve.Fori(1, NW) as w:
                V.tensor_scalar(above, src_g, bounds[0:NG, bass.ds(w, 1)], None, ALU.is_ge)
                dve.drain()
                V.tensor_reduce(reach[:, bass.ds(w, 1)], above, AX.X, ALU.add)
                dve.drain()
            V.memset(pos_g, 0.0)
            V.memset(win_g, 0.0)
            dve.drain()
            V.tensor_tensor(share[:], reach[:, 0:NW], reach[:, 1:NW + 1], ALU.subtract).then_inc(s_share, 1)
            dve.wait_ge(s_prefix, 1)
            V.tensor_copy(total[:], bank[5][:, NW:2 * NW])
            dve.drain()
            V.tensor_tensor_scan(offset[:], total[:], zeros[:, 0:NW], 0.0, ALU.add, ALU.add)
            dve.drain()
            V.tensor_tensor(offset[:], offset[:], total[:], ALU.subtract)
            dve.drain()
            V.scalar_tensor_tensor(base[:, 0:NW], bank[5][0:NG, 0:NW], -1.0, offset[0:NG, :], ALU.add, ALU.add)
            dve.drain()

            def rank_edges(i, b):
                if b:
                    return
                w = bass.ds(i, 1)
                V.tensor_scalar(above, src_g, bounds[0:NG, bass.ds(i + 1, 1)], None, ALU.is_ge)
                dve.drain()
                V.scalar_tensor_tensor(inside, src_g, bounds[0:NG, w], above, ALU.is_ge, ALU.subtract)
                V.tensor_tensor(win_g, win_g, above, ALU.add)
                dve.drain()
                V.tensor_tensor_scan(order, inside, zeros[0:NG, 0:1].broadcast_to([NG, GE]), base[:, w], ALU.add, ALU.add)
                dve.drain()
                V.tensor_tensor(order, order, inside, ALU.mult)
                dve.drain()
                V.tensor_tensor(pos_g, pos_g, order, ALU.add)
                dve.drain()
            sums(0, D + 1, src_idx, rank_edges)
            dve.drain()
            ints = lambda t: t.bitcast(I32)
            V.tensor_copy(ints(above), pos_g)
            V.tensor_copy(ints(spare), rel_g)
            V.scalar_tensor_tensor(src_g, win_g, -float(WN), src_g, ALU.mult, ALU.add)
            dve.drain()
            V.tensor_single_scalar(ints(inside), ints(above), 7, ALU.arith_shift_right)
            dve.drain()
            V.tensor_single_scalar(ints(above), ints(above), TE - 1, ALU.bitwise_and)
            V.tensor_single_scalar(ints(win_g), ints(spare), 11, ALU.arith_shift_right)
            V.tensor_single_scalar(ints(rel_g), ints(spare), 2047, ALU.bitwise_and)
            dve.drain()
            V.tensor_copy(order, ints(above))
            V.tensor_copy(pos_g, ints(inside))
            dve.drain()
            V.tensor_copy(above, ints(rel_g))
            V.tensor_copy(inside, ints(win_g))
            dve.drain()
            V.scalar_tensor_tensor(rel_g, src_g, 16.0, inside, ALU.mult, ALU.add)
            dve.drain()
            V.tensor_copy(inside, pos_g).then_inc(s_digits, 1)
            dve.wait_ge(s_digits_t, 1)
            for i in range(4):
                for j in range(GT):
                    q = i * GT + j
                    last = V.tensor_copy(moves[:, i, :, j], bank[q // 4][:, 128 * (q % 4):128 * (q % 4) + NG])
            last.then_inc(s_moves, 1)
            V.tensor_scalar_max(rstd[:], acc[:, :, D], 1.0)
            dve.drain()
            V.reciprocal(rstd[:], rstd[:])
            dve.drain()

            def stage0(i, b, first):
                if not first:
                    dve.wait_ge(s_nt[0], 2 * i + b - 1)
                w = 2 * i + b
                V.tensor_scalar(nodes_b[:, b, 0:D], acc[:, bass.ds(w, 1), 0:D].rearrange("p w d -> p (w d)"),
                                rstd[:, bass.ds(w, 1)], None, ALU.mult)
                V.tensor_copy(nodes_b[:, b, D:2 * D], window(h, w)).then_inc(s_nb[0], 1)

            def take0(i, b, first):
                w = 2 * i + b
                dve.wait_ge(s_mm[0], w + 1)
                V.tensor_tensor(prod[:, b, :], bank[2 + b][0:WN, 0:D], bias0[:], ALU.add).then_inc(s_ev[0], 1)
                dve.drain()
                V.tensor_tensor(window(x, w), window(x, w), prod[:, b, :], ALU.add)
                dve.drain()
                statistics(w, window(x, w))
            dve.wait_ge(s_w, 16 * WEIGHT_LOADS)

            def staged_and_taken(stage_, take):
                for b in range(2):
                    stage_(0, b, True)
                for b in range(2):
                    take(0, b, True)
                with dve.Fori(1, NW // 2) as i:
                    for b in range(2):
                        stage_(i, b, False)
                    for b in range(2):
                        take(i, b, False)
            staged_and_taken(stage0, take0)
            norm(1)

            def add_attr(i, b):
                dve.wait_ge(s_rows[1][b], 16 * GT * (i + 1))
                dve.wait_ge(s_attr[b], 16 * (i + 1))
                V.tensor_tensor(rows[:, b, :, 0:D], rows[:, b, :, 0:D], attr[:, b, :, :], ALU.add).then_inc(s_add, 1)
                g = RING * i + b
                dve.wait_ge(s_turned, g + 1)
                for j in range(GT):
                    lane, tile, low, high = (moves[:, k, bass.ds(g, 1), j] for k in range(4))
                    V.tensor_scalar(turn_t[:, j, 0:NG * GT], tile_iota, tile, None, ALU.is_equal)
                    V.tensor_scalar(turn_p[:, j, 0, :], lane_iota, lane, low, ALU.is_equal, ALU.mult)
                    last = V.tensor_scalar(turn_p[:, j, 1, :], lane_iota, lane, high, ALU.is_equal, ALU.mult)
                last.then_inc(s_turn, 1)
            sums(1, D, src_idx, add_attr)
            dve.wait_ge(s_turned, NG + 2)
            HALF = (NG * GT + 1) // 2
            flat = lambda t: t.rearrange("p g j -> p (g j)")
            for k in range(2):
                V.tensor_copy(flat(moves[:, k, :, :])[:, 0:HALF], bank[2 * k][:, 0:HALF])
                last = V.tensor_copy(flat(moves[:, k, :, :])[:, HALF:], bank[2 * k + 1][:, 0:NG * GT - HALF])
            last.then_inc(s_perm, 1)

            def stage1(i, b, first):
                if not first:
                    dve.wait_ge(s_nt[1], 2 * i + b - 1)
                w = 2 * i + b
                V.tensor_tensor(nodes_b[:, b, 0:D], acc[:, bass.ds(w, 1), 0:D].rearrange("p w d -> p (w d)"),
                                window(h, w), ALU.add).then_inc(s_nb[1], 1)
            pairs(dve, stage1)
            with dve.Fori(0, NC) as c:
                for m in range(KH):
                    dve.wait_ge(s_z1, KH * c + m + 1)
                    V.bn_stats(st1[:, m, bass.ds(c, 1), :].rearrange("p c s -> p (c s)"), z1T[:, m, bass.ds(CN * c, CN)])
            dve.drain()
            for m in range(KH):
                V.bn_aggr(mv1[:, m, :], st1[:, m, :, :].rearrange("p c s -> p (c s)"))
            dve.drain()
            V.tensor_scalar_add(sc1[:, 0, :], mv1[:, :, 1], EPS).then_inc(s_st1, 1)
            dve.wait_ge(s_sd1, 1)
            V.reciprocal(sc1[:, 0, :], sc1[:, 0, :])
            dve.drain()
            V.tensor_tensor(sc1[:, 0, :], sc1[:, 0, :], v1[:, 1, :], ALU.mult)
            dve.drain()
            V.tensor_tensor(sc1[:, 1, :], mv1[:, :, 0], sc1[:, 0, :], ALU.mult)
            dve.drain()
            V.tensor_tensor(sc1[:, 1, :], v1[:, 2, :], sc1[:, 1, :], ALU.subtract).then_inc(s_bn, 1)
            with dve.Fori(0, NC) as c:
                for m in range(KD):
                    dve.wait_ge(s_z2, KD * c + m + 1)
                    V.bn_stats(st2[:, m, bass.ds(c, 1), :].rearrange("p c s -> p (c s)"), hT[:, m, bass.ds(CN * c, CN)])
            dve.drain()
            for m in range(KD):
                V.bn_aggr(mv2[:, m, :], st2[:, m, :, :].rearrange("p c s -> p (c s)"))
            dve.drain()
            mean, var = mv2[:, :, 0], mv2[:, :, 1]
            ln_w, ln_b, gn_w, gn_b, gn_ms = (v2[:, i, :] for i in range(1, 6))
            V.tensor_reduce(g1[:, 0:1], mean, AX.X, ALU.add).then_inc(s_g, 1)
            dve.wait_ge(s_gp, 1)
            V.tensor_scalar(g1[:, 2:3], bank[4][:, 0:1], 1.0 / D, None, ALU.mult)
            dve.drain()
            V.tensor_scalar(t2[:, 0, :], mean, g1[:, 2:3], None, ALU.subtract)
            dve.drain()
            V.tensor_tensor(t2[:, 1, :], t2[:, 0, :], t2[:, 0, :], ALU.mult)
            dve.drain()
            V.tensor_tensor(t2[:, 1, :], t2[:, 1, :], var, ALU.add)
            dve.drain()
            V.tensor_reduce(g1[:, 1:2], t2[:, 1, :], AX.X, ALU.add).then_inc(s_g, 1)
            dve.wait_ge(s_gp, 2)
            V.tensor_scalar(g1[:, 3:4], bank[4][:, 0:1], 1.0 / D, EPS, ALU.mult, ALU.add).then_inc(s_sd, 1)
            dve.wait_ge(s_sdr, 1)
            V.reciprocal(g1[:, 3:4], g1[:, 3:4])
            dve.drain()
            V.tensor_scalar(t2[:, 2, :], ln_w, g1[:, 3:4], None, ALU.mult)
            dve.drain()
            V.tensor_tensor(t2[:, 3, :], t2[:, 0, :], t2[:, 2, :], ALU.mult)
            dve.drain()
            V.tensor_tensor(t2[:, 3, :], t2[:, 3, :], ln_b, ALU.add)
            dve.drain()
            V.tensor_tensor(t2[:, 4, :], t2[:, 3, :], gn_ms, ALU.mult)
            dve.drain()
            V.tensor_tensor(t2[:, 4, :], t2[:, 3, :], t2[:, 4, :], ALU.subtract)
            V.tensor_tensor(t2[:, 5, :], t2[:, 2, :], t2[:, 2, :], ALU.mult)
            dve.drain()
            V.tensor_tensor(t2[:, 5, :], t2[:, 5, :], var, ALU.mult)
            V.tensor_tensor(t2[:, 1, :], t2[:, 4, :], t2[:, 4, :], ALU.mult)
            dve.drain()
            V.scalar_tensor_tensor(t2[:, 5, :], t2[:, 5, :], EPS, t2[:, 1, :], ALU.add, ALU.add).then_inc(s_sd, 1)
            dve.wait_ge(s_sdr, 2)
            V.reciprocal(t2[:, 5, :], t2[:, 5, :])
            dve.drain()
            V.tensor_tensor(t2[:, 5, :], t2[:, 5, :], gn_w, ALU.mult)
            dve.drain()
            V.tensor_tensor(t2[:, 6, :], t2[:, 2, :], t2[:, 5, :], ALU.mult)
            V.tensor_tensor(t2[:, 7, :], t2[:, 4, :], t2[:, 5, :], ALU.mult)
            dve.drain()
            V.tensor_tensor(t2[:, 7, :], t2[:, 7, :], gn_b, ALU.add)
            V.tensor_tensor(t2[:, 1, :], t2[:, 6, :], mean, ALU.mult)
            dve.drain()
            V.tensor_tensor(t2[:, 7, :], t2[:, 7, :], t2[:, 1, :], ALU.subtract).then_inc(s_fin, 1)

            def take1(i, b, first):
                w = 2 * i + b
                dve.wait_ge(s_obt, w + 1)
                V.tensor_tensor(prod[:, b, :], bank[2 + b][0:WN, 0:D], window(h, w), ALU.add).then_inc(s_ev[1], 1)
                dve.drain()
                V.tensor_tensor(window(x, w), window(x, w), prod[:, b, :], ALU.add)
                dve.drain()
                statistics(w, window(x, w))
            pairs(dve, take1)
            norm(2)

            def stage_h(l):
                def step(i, b, first):
                    dve.wait_ge(s_h[l], 2 * i + b + 1)
                    if not first:
                        dve.wait_ge(s_nt[l], 2 * i + b - 1)
                    V.tensor_copy(nodes_b[:, b, 0:D], window(h, 2 * i + b)).then_inc(s_nb[l], 1)
                return step

            def take2(i, b, first):
                if not first:
                    dve.wait_ge(s_xt[b], 16 * i)
                for q in range(R // 2):
                    dve.wait_ge(s_mm[2], R // 2 * (2 * i + b) + q + 1)
                    V.tensor_copy(xt_out[:, b, 2 * D * q:2 * D * q + 2 * D], bank[2 + q][0:WN, :]).then_inc(s_ev[2], 1)
            low, high, place, spare2 = (flat(moves[:, k, :, :]) for k in range(4))
            V.tensor_copy(ints(spare2), high)
            dve.drain()
            V.tensor_single_scalar(ints(high), ints(spare2), 15, ALU.bitwise_and)
            V.tensor_single_scalar(ints(spare2), ints(spare2), 4, ALU.arith_shift_right)
            dve.drain()
            V.scalar_tensor_tensor(flat(rel_idx[:, 0:NG, :]), ints(high), 2048.0, low, ALU.mult, ALU.add)
            V.tensor_copy(flat(src_f[:]), ints(spare2))
            dve.wait_ge(s_posi, 1)
            dve.drain()
            for w in range(1, NW):
                V.tensor_scalar(low, place, offset[:, w:w + 1], float(WN), ALU.is_ge, ALU.mult)
                dve.drain()
                V.tensor_tensor(flat(src_f[:]), flat(src_f[:]), low, ALU.add)
                dve.drain()
            for q in range(2):
                V.tensor_copy(span_f[:, q:q + 1], place_of_group[:, q:q + 1])
            dve.drain()
            span(offset[0:NG, 1:NW])
            V.tensor_copy(span_f[:, 0:1], span_f[:, 0:1]).then_inc(s_flt, 1)
            staged_and_taken(stage_h(2), take2)
            dve.wait_ge(s_lists_t, 3)
            V.tensor_copy(spans[0:1, 1, :], bank[6][0:1, 0:NG]).then_inc(s_lists, 1)
            dve.wait_ge(s_lists, 2)
            sums(2, D, rel_idx, lambda i, b: None)
            dve.drain()
            V.tensor_tensor(acc[:, :, 0:D], acc[:, :, 0:D], bias_rel[:].rearrange("p (a d) -> p a d", a=1).broadcast_to([WN, NW, D]),
                            ALU.add)
            dve.drain()
            V.scalar_tensor_tensor(x[:], acc[:, :, 0:D], 0.0, x[:], ALU.max, ALU.add).then_inc(s_x_new[2], 1)
            dve.drain()
            with dve.Fori(0, NW) as w:
                statistics(w, window(x, w))
            norm(3)

            def take3(i, b, first):
                if not first:
                    dve.wait_ge(s_hh[b], 16 * i)
                w = 2 * i + b
                dve.wait_ge(s_mm[3], w + 1)
                hh = bank[2 + b][0:WN, 0:D]
                V.tensor_copy(hh_out[:, b, 0:D], hh)
                V.tensor_tensor(prod[:, 0, :], hh, a_src[:], ALU.mult)
                V.tensor_tensor(prod[:, 1, :], hh, a_dst[:], ALU.mult)
                dve.drain()
                V.tensor_reduce(window(s_dst, w), prod[:, 1, :].rearrange("p (h d) -> p h d", h=H), AX.X, ALU.add)
                V.tensor_reduce(hh_out[:, b, D:DH], prod[:, 0, :].rearrange("p (h d) -> p h d", h=H), AX.X, ALU.add
                                ).then_inc(s_ev[3], 1)
                dve.drain()
            staged_and_taken(stage_h(3), take3)
            V.memset(run_max[:], -BIG)
            for b in range(RING):
                fill_slot(src_idx, b, b, 3)
            visits, tiles, fast = Visits(dve), Visits(dve, GT), Visits(dve)
            dve.wait_ge(s_zero[3], 1)
            heads = lambda t: t.rearrange("p (h d) -> p h d", h=H)

            def attention(i, b):
                g = RING * i + b
                dve.wait_ge(s_rows[3][b], 16 * GT * (i + 1))

                def highest_by_scan():
                    u = fast.next()
                    dve.wait_ge(s_starts[b], 16 * (i + 1))
                    dve.wait_ge(s_sT, u)
                    V.tensor_tensor_scan(run, starts[:, b, :], psum[0:H, 1024:1024 + GE], -BIG, ALU.add, ALU.max
                                         ).then_inc(s_run, 1)
                    dve.wait_ge(s_runT, u)
                    is_last = last_f[:, bass.ds(g, 1), :].rearrange("p g (j h) -> p (g j) h", h=1)
                    V.tensor_tensor(last_max[:, :, 0:H], bank[5][:, 0:GT * H].rearrange("p (j h) -> p j h", j=GT),
                                    is_last.broadcast_to([128, GT, H]), ALU.mult)
                    V.tensor_copy(last_max[:, :, H:H + 1], is_last).then_inc(s_lastv, 1)
                    dve.wait_ge(s_nmax, u)
                    V.tensor_scalar(seen[:], bank[7][0:WN, H:H + 1], BIG, -BIG, ALU.mult, ALU.add)
                    dve.drain()
                    V.tensor_scalar(node_ref[:, H:2 * H], bank[7][0:WN, 0:H], seen[:], None, ALU.add)
                    dve.drain()

                def highest_by_mask():
                    V.tensor_scalar(penalty[:], onehot_t[:], BIG, -BIG, ALU.mult, ALU.add)
                    for j in range(GT):
                        s_src = rows[:, b, j, D:DH].rearrange("p (h e) -> p h e", e=1).broadcast_to([128, H, TE])
                        V.tensor_tensor(diag, ident[:].rearrange("p (h e) -> p h e", h=1).broadcast_to([128, H, TE]), s_src,
                                        ALU.mult).then_inc(s_diag, 1)
                        dve.drain()
                        dve.wait_ge(s_spread, tiles.next())
                        pen = penalty[:, TE * j:TE * j + TE].rearrange("p (h e) -> p h e", h=1).broadcast_to([WN, 4, TE])
                        for q in range(2):
                            V.tensor_tensor(masked[:, 4 * q:4 * q + 4, :],
                                            bank[2 + q][0:WN, :].rearrange("p (h e) -> p h e", h=4), pen, ALU.add)
                        dve.drain()
                        V.tensor_reduce(tile_max[:, j, :], masked, AX.X, ALU.max)
                    dve.drain()
                    V.tensor_reduce(node_ref[:, H:2 * H], tile_max[:].rearrange("p j h -> p h j"), AX.X, ALU.max)
                    dve.drain()

                def visit(w, mixed):
                    v = visits.next()
                    onehots(g, w, 3)
                    dve.wait_ge(s_ohtc, v)
                    with dve.If(mixed > 0):
                        highest_by_mask()
                    with dve.Else():
                        highest_by_scan()
                    V.tensor_tensor(node_ref[:, H:2 * H], node_ref[:, H:2 * H], window(s_dst, w), ALU.add)
                    V.tensor_copy(node_ref[:, 0:H], window(s_dst, w))
                    dve.drain()
                    V.scalar_tensor_tensor(node_ref[:, H:2 * H], node_ref[:, H:2 * H], SLOPE, node_ref[:, H:2 * H],
                                           ALU.mult, ALU.max).then_inc(s_ref, 1)
                    dve.wait_ge(s_back, v)
                    back = bank[4][:, 0:GT * 2 * H].rearrange("p (j c) -> p j c", j=GT)
                    V.tensor_tensor(score[:], rows[:, b, :, D:DH], back[:, :, 0:H], ALU.add)
                    dve.drain()
                    V.scalar_tensor_tensor(score[:], score[:], SLOPE, score[:], ALU.mult, ALU.max)
                    dve.drain()
                    V.tensor_tensor(score[:], score[:], back[:, :, H:2 * H], ALU.subtract)
                    dve.drain()
                    V.tensor_scalar_min(score[:], score[:], 0.0).then_inc(s_arg, 1)
                    V.tensor_tensor(new_max[:], window(run_max, w), node_ref[:, H:2 * H], ALU.max)
                    dve.drain()
                    V.tensor_tensor(decay[:, 0, :], window(run_max, w), new_max[:], ALU.subtract)
                    V.tensor_tensor(decay[:, 1, :], node_ref[:, H:2 * H], new_max[:], ALU.subtract).then_inc(s_dec, 1)
                    dve.drain()
                    V.tensor_copy(window(run_max, w), new_max[:])
                    dve.wait_ge(s_exp, v)
                    weight = msg[:, :, D:DH].rearrange("p j (h e) -> p j h e", e=1).broadcast_to([128, GT, H, HD])
                    V.tensor_tensor(msg[:, :, 0:D].rearrange("p j (h d) -> p j h d", h=H),
                                    rows[:, b, :, 0:D].rearrange("p j (h d) -> p j h d", h=H), weight, ALU.mult
                                    ).then_inc(s_msg, 1)
                    dve.wait_ge(s_sum[3], v)
                    dve.wait_ge(s_dexp, v)
                    mine = acc[:, bass.ds(w, 1), :].rearrange("p w d -> p (w d)")
                    for of, to, dec in ((mine, mine, 0), (bank[6][0:WN, 0:DH], fresh[:], 1)):
                        e = decay[:, dec, :]
                        V.tensor_tensor(heads(to[:, 0:D]), heads(of[:, 0:D]),
                                        e.rearrange("p (h d) -> p h d", d=1).broadcast_to([WN, H, HD]), ALU.mult)
                        V.tensor_tensor(to[:, D:DH], of[:, D:DH], e, ALU.mult)
                    dve.drain()
                    V.tensor_tensor(mine, mine, fresh[:], ALU.add)
                    dve.drain()
                each_window(dve, g, visit, flag=True)
                fill_slot(src_idx, g + RING, b, 3)
            rings(dve, attention)
            dve.drain()
            V.tensor_scalar_max(s_dst[:], acc[:, :, D:DH], 1e-30)
            dve.drain()
            V.reciprocal(s_dst[:], s_dst[:])
            dve.drain()
            V.tensor_tensor(acc[:, :, 0:D].rearrange("p w (h d) -> p w h d", h=H),
                            acc[:, :, 0:D].rearrange("p w (h d) -> p w h d", h=H),
                            s_dst[:].rearrange("p w (h d) -> p w h d", d=1).broadcast_to([WN, NW, H, HD]), ALU.mult)
            dve.drain()
            V.tensor_tensor(h[:], acc[:, :, 0:D], h[:], ALU.add)
            dve.drain()
            with dve.Fori(0, NW) as w:
                statistics(w, window(h, w))
            norm(4)
            dve.drain()
            with dve.Fori(0, NW) as w:
                V.tensor_scalar(window(h, w), window(h, w), rstd[:, bass.ds(w, 1)], shift[:, bass.ds(w, 1)], ALU.mult, ALU.add)
            dve.drain()
            all_windows = lambda t: t[:].rearrange("p (a d) -> p a d", a=1).broadcast_to([WN, NW, D])
            V.tensor_tensor(h[:], h[:], all_windows(gamma), ALU.mult)
            dve.drain()
            V.tensor_tensor(h[:], h[:], all_windows(beta), ALU.add)
            dve.drain()
            V.tensor_scalar_min(acc[:, :, 0:D], h[:], 0.0).then_inc(s_elu, 1)
            V.scalar_tensor_tensor(x[:], h[:], 0.0, x[:], ALU.max, ALU.add)
            dve.wait_ge(s_elud, 1)
            dve.drain()
            V.scalar_tensor_tensor(x[:], acc[:, :, 0:D], -1.0, x[:], ALU.add, ALU.add).then_inc(s_x_new[3], 1)


_INPUTS = ["x", "src", "dst", "edge_attr_256", "edge_type_8", "L0_gnn_W_l", "L0_gnn_W_r", "L0_gnn_b_r", "L1_gnn_W1",
           "L1_gnn_b1", "L1_gnn_bn_gamma", "L1_gnn_bn_beta", "L1_gnn_W2", "L1_gnn_b2", "L1_gnn_ln_w", "L1_gnn_ln_b",
           "L1_gnn_gn_w", "L1_gnn_gn_b", "L1_gnn_gn_ms", "L2_gnn_weight", "L2_gnn_bias", "L3_gnn_W", "L3_gnn_a_src",
           "L3_gnn_a_dst", "L3_gnn_gamma", "L3_gnn_beta"]
_TRANSPOSED = ("L0_gnn_W_l", "L0_gnn_W_r")


def kernel(**inputs):
    import numpy as np
    import concourse.bacc as bacc
    from concourse import mybir as mb
    from concourse.bass_utils import run_bass_kernel_spmd as run

    nc = bacc.Bacc("TRN2", target_bir_lowering=False, num_devices=1)
    arrays, aps = {}, {}
    for name in _INPUTS:
        v = np.asarray(inputs[name])
        v = np.ascontiguousarray(v.T if name in _TRANSPOSED else v)
        arrays[f"in_{name}"] = v
        aps[name] = nc.dram_tensor(f"in_{name}", v.shape, mb.dt.from_np(v.dtype), kind="ExternalInput").ap()
    out = nc.dram_tensor("out_x", arrays["in_x"].shape, mb.dt.float32, kind="ExternalOutput").ap()
    gnn_kernel(nc, aps, out)
    r = run(nc, [arrays], core_ids=[0])
    return r.results[0]["out_x"]
```

```python
from contextlib import ExitStack

import concourse.bass as bass
from concourse import mybir

F32 = mybir.dt.float32
I32 = mybir.dt.int32
F16 = mybir.dt.float16
ALU = mybir.AluOpType
ACT = mybir.ActivationFunctionType
AX = mybir.AxisListType


def gnn_kernel(nc, a, out):
    N, D = a["x"].shape
    E = a["src"].shape[0]
    NW, WN = 20, 125
    GT, TE = 5, 128
    GE = GT * TE
    NG = E // GE
    RING = 5
    assert NW * WN == N and NG * GE == E and NG % RING == 0 and NG <= 128
    R = a["L2_gnn_weight"].shape[0]
    H, HD = a["L3_gnn_a_src"].shape
    DH = D + H
    D1 = a["L1_gnn_W1"].shape[1]
    KD, KH = D // 128, D1 // 128
    NC, CN = 5, N // 5
    EPS = 1e-5
    BIG = 1e30
    SLOPE = 0.2
    WEIGHT_LOADS = 20
    MM_STEPS = {0: 1, 2: R // 2, 3: 1}

    with ExitStack() as ctx:
        def sb(name, shape, dt=F32):
            return ctx.enter_context(nc.sbuf_tensor(name, shape, dt))

        def sem(name):
            return ctx.enter_context(nc.semaphore(name))

        h_table = [nc.dram_tensor(f"h_table{l}", (N, D), F32, kind="Internal").ap() for l in range(2)]
        xt_table = nc.dram_tensor("xt_table", (R * N, D), F32, kind="Internal").ap()
        start_table = nc.dram_tensor("start_table", (NG, GE), F32, kind="Internal").ap()
        hh_table = nc.dram_tensor("hh_table", (N, DH), F32, kind="Internal").ap()

        x = sb("x", [WN, NW, D])
        h = sb("h", [WN, NW, D])
        acc = sb("acc", [WN, NW, DH])
        stats = sb("stats", [WN, NW, 6])
        mean_var = sb("mean_var", [WN, NW, 2])
        rstd = sb("rstd", [WN, NW])
        shift = sb("shift", [WN, NW])
        stage = sb("stage", [128, RING * GT * (DH + D)])
        rows = stage[:, 0:RING * GT * DH].rearrange("p (r j c) -> p r j c", r=RING, j=GT)
        attr = stage[:, RING * GT * DH:].rearrange("p (r j c) -> p r j c", r=RING, j=GT)
        src_idx = sb("src_idx", [128, NG + RING, GT], I32)
        rel_idx = sb("rel_idx", [128, NG + RING, GT], I32)
        dst_f = sb("dst_f", [128, NG, GT])
        slot = sb("slot", [128, RING, GT], I32)
        spans = sb("spans", [1, 2, NG], I32)
        src_f = sb("src_f", [128, NG, GT])
        node_iota = sb("node_iota", [128, N])
        ident = sb("ident", [128, 128])
        ones = sb("ones", [128, 128])
        hT = sb("hT", [128, KD, N])
        scratch = hT[:].rearrange("p k n -> p (k n)")
        onehot_t = scratch[0:WN, 0:GE]
        penalty = scratch[0:WN, GE:2 * GE]
        msg = scratch[:, 2 * GE:2 * GE + GT * DH].rearrange("p (j c) -> p j c", j=GT)
        run = scratch[0:H, 2 * GE + GT * DH:3 * GE + GT * DH]
        tail = stage[:, RING * GT * DH:]
        diag = tail[:, 0:H * TE].rearrange("p (h e) -> p h e", h=H)
        masked = tail[0:WN, H * TE:2 * H * TE].rearrange("p (h e) -> p h e", h=H)
        starts = tail[0:H, 2 * H * TE:2 * H * TE + RING * GE].rearrange("p (r e) -> p r e", r=RING)
        last_f = sb("last_f", [128, NG, GT])
        last_max = sb("last_max", [128, GT, H + 1])
        seen = sb("seen", [WN, 1])
        tile_max = sb("tile_max", [WN, GT, H])
        node_ref = sb("node_ref", [WN, 2 * H])
        score = sb("score", [128, GT, H])
        s_dst = sb("s_dst", [WN, NW, H])
        run_max = sb("run_max", [WN, NW, H])
        decay = sb("decay", [WN, H])
        weight = sb("weight", [128, GT, H])
        z1T = stage[:, 0:KH * N].rearrange("p (k n) -> p k n", k=KH)
        nodes_b = sb("nodes_b", [WN, 2, 2 * D])
        nodesT_b = sb("nodesT_b", [128, 2, 4 * WN])
        onehot = [sb("onehot", [128, GT, WN])[:],
                  nodesT_b[:].rearrange("p b n -> p (b n)")[:, 0:GT * WN].rearrange("p (j n) -> p j n", j=GT)]
        xt_out = hT[0:WN, :, 0:R * D]
        hh_out = sb("hh_out", [WN, 2, DH])
        prod = sb("prod", [WN, 2, D])
        w0 = sb("w0", [128, 2 * KD, D])
        w1 = sb("w1", [128, KD, D1])
        w2 = sb("w2", [128, KH, D])
        w_rel = stage[:, RING * GT * (DH + D) - KD * R * D:].rearrange("p (k r d) -> p k r d", k=KD, r=R)
        w_att = sb("w_att", [128, KD, D])
        bias0 = sb("bias0", [WN, D])
        bias_rel = sb("bias_rel", [WN, D])
        gamma = sb("gamma", [WN, D])
        beta = sb("beta", [WN, D])
        a_src = sb("a_src", [WN, D])
        a_dst = sb("a_dst", [WN, D])
        v1 = sb("v1", [128, 3, KH])
        v2 = sb("v2", [128, 6, KD])
        st1 = sb("st1", [128, KH, NC, 6])
        mv1 = sb("mv1", [128, KH, 2])
        sc1 = sb("sc1", [128, 2, KH])
        st2 = sb("st2", [128, KD, NC, 6])
        mv2 = sb("mv2", [128, KD, 2])
        t2 = sb("t2", [128, 8, KD])
        g1 = sb("g1", [128, 4])
        psum = ctx.enter_context(nc.psum_tensor("psum", [128, 8 * 512], F32))
        bank = [psum[:, 512 * i:512 * i + 512] for i in range(8)]
        raw = stage[0:NG, 0:3 * GE].bitcast(I32).rearrange("p (a e) -> p a e", a=3)
        flt = stage[0:NG, 3 * GE:7 * GE].rearrange("p (a e) -> p a e", a=4)
        starts_g = stage[0:NG, 7 * GE:8 * GE]
        span_f = sb("span_f", [NG, 6])
        bounds = sb("bounds", [128, NW + RING + 1])
        cmp = sb("cmp", [NG, 2, NW - 1])
        rank = sb("rank", [NG, 7])
        src_g, rel_g, pos_g, win_g, above, inside, order = (scratch[0:NG, GE * k:GE * k + GE] for k in range(7))
        spare = stage[0:NG, 0:GE]
        iotas = scratch[:, 7 * GE:7 * GE + (NG * GT + 1 + TE) // 2].bitcast(F16)
        tile_iota, lane_iota = iotas[:, 0:NG * GT], iotas[:, NG * GT + 1:NG * GT + 1 + TE]
        zeros = sb("zeros", [128, 320])
        place_of_group = sb("place_of_group", [NG, 2])
        before = sb("before", [128, 128])
        reach = sb("reach", [NG, NW + 1])
        share = sb("share", [NG, NW])
        total = sb("total", [128, NW])
        offset = sb("offset", [128, NW])
        base = sb("base", [NG, NW + RING])
        moves = sb("moves", [128, 4, NG, GT])
        turn_t = scratch[:, 0:GT * 320].bitcast(F16).rearrange("p (j t) -> p j t", j=GT)
        turn_p = scratch[:, GT * 320:GT * 320 + GT * TE].bitcast(F16).rearrange("p (j k e) -> p j k e", j=GT, k=2)

        s_edges, s_x, s_w, s_const = sem("edges_loaded"), sem("x_loaded"), sem("weights_loaded"), sem("constants_ready")
        s_flt, s_lists_t, s_lists = sem("lists_float"), sem("lists_transposed"), sem("lists_ready")
        s_var = [sem(f"var_ready{l}") for l in range(5)]
        s_std = [sem(f"std_ready{l}") for l in range(5)]
        s_rstd = [sem(f"rstd_ready{l}") for l in range(5)]
        s_h = [sem(f"h_ready{l}") for l in range(4)]
        s_table = [sem(f"table_written{l}") for l in range(2)]
        s_x_new = {l: sem(f"x_new{l}") for l in (2, 3)}
        s_xt = [sem(f"xt_written{b}") for b in range(2)]
        s_hh = [sem(f"hh_written{b}") for b in range(2)]
        s_zero = [sem(f"acc_zero{l}") for l in range(4)]
        s_slot = [sem(f"slot_ready{l}") for l in range(4)]
        s_rows = [[sem(f"rows_gathered{l}_{b}") for b in range(RING)] for l in range(4)]
        s_attr = [sem(f"attr_loaded{b}") for b in range(RING)]
        s_onehot = [sem(f"onehot_ready{l}") for l in range(4)]
        s_sum = [sem(f"group_summed{l}") for l in range(4)]
        s_add, s_relu = sem("rows_added"), sem("rows_relu")
        s_nb, s_nt, s_ntc, s_mm, s_ev = ([sem(f"{n}{l}") for l in range(4)] for n in
                                         ("nodes_staged", "nodes_transposed", "nodesT_ready", "product_ready", "product_taken"))
        s_oht, s_ohtc, s_diag, s_spread, s_ref, s_back, s_arg, s_exp, s_msg, s_dec, s_dexp = (
            sem(n) for n in ("onehot_turned", "onehot_t_ready", "diag_ready", "scores_spread", "node_ref_ready",
                             "refs_at_edges", "exponent_ready", "exp_ready", "msg_ready", "decay_ready", "decay_exp"))
        s_z1p, s_z1, s_st1, s_sd1, s_bn, s_z1n = (sem(n) for n in ("z1_product", "z1_ready", "z1_stats", "z1_std", "bn_ready", "z1_normed"))
        s_z2p, s_z2, s_g = sem("z2_product"), sem("z2_ready"), sem("graph_sums_wanted")
        s_gp, s_sd, s_fin, s_ob, s_obt = sem("graph_sums"), sem("std_wanted"), sem("affine_ready"), sem("out_staged"), sem("out_transposed")
        s_sdr = sem("std_done")
        s_wrel = sem("w_rel_loaded")
        s_pen, s_pent, s_starts = sem("starts_ready"), sem("start_table_written"), [sem(f"starts_loaded{b}") for b in range(RING)]
        s_share, s_prefix, s_digits, s_digits_t, s_moves = (sem(n) for n in ("shares_ready", "shares_summed", "digits_ready", "digits_turned", "moves_ready"))
        s_turn, s_turned, s_perm, s_posi = sem("turns_ready"), sem("edges_turned"), sem("permuted_out"), sem("positions_ready")
        s_sT, s_run, s_runT, s_lastv, s_nmax = (sem(n) for n in ("scores_turned", "runs_ready", "runs_back", "last_max_ready", "node_max_ready"))
        s_scanned = sem("scans_seen")
        s_begun = sem("gathers_begun")
        s_elu, s_elud, s_out = sem("elu_arg"), sem("elu_done"), sem("out_written")

        def row_bc(v, n):
            return v.rearrange("(a d) -> a d", a=1).broadcast_to([n, v.shape[0]])

        def pairs(eng, step):
            for b in range(2):
                step(0, b, True)
            with eng.Fori(1, NW // 2) as i:
                for b in range(2):
                    step(i, b, False)

        def rings(eng, step):
            with eng.Fori(0, NG // RING) as i:
                for b in range(RING):
                    step(i, b)

        def each_window(eng, g, first_visit, further_visit, by=0):
            word = eng.value_load(spans[0:1, by, bass.ds(g, 1)], min_val=0, max_val=1024 + 32 * NW + NW - 1)
            why = "the list holds windows of nodes"
            first = nc.s_assert_within(eng.snap(word & 31), 0, NW - 1, skip_runtime_bounds_check_because=why)
            end = nc.s_assert_within(eng.snap((word >> 5) & 31), 1, NW, skip_runtime_bounds_check_because=why)
            mixed = eng.snap(word >> 10) if by == 0 else None
            first_visit(first, mixed)
            with eng.If(eng.snap(end - first) > 1):
                second = nc.s_assert_within(eng.snap(first + 1), 1, NW - 1, skip_runtime_bounds_check_because=why)
                with eng.Fori(second, end) as w:
                    further_visit(w, mixed)

        def ring_before(b):
            return (b - 1) % RING

        class Visits:

            def __init__(self, eng, steps=1):
                self.most = steps * NG * NW + 1
                self.eng, self.reg = eng, eng.alloc_register(f"visits_{nc.next_id()}")
                eng.reg_mov(self.reg, 0)

            def next(self):
                self.eng.reg_add(self.reg, self.reg, 1)
                return self.now()

            def now(self):
                return self.eng.snap(self.reg, min_val=1, max_val=self.most)

        def window(t, w):
            return t[:, bass.ds(w, 1), :].rearrange("p w d -> p (w d)")

        block = ctx.enter_context(nc.Block())

        @block.sync
        def _(sp):
            for i, n in enumerate(("dst", "src", "edge_type_8")):
                sp.dma_start(raw[:, i, :], a[n].rearrange("(g e) -> g e", e=GE)).then_inc(s_edges, 16)
            sp.dma_start(x[:], a["x"].rearrange("(w p) d -> p w d", p=WN)).then_inc(s_x, 16)
            loads = [(w0[:, 0:KD, :], a["L0_gnn_W_l"].rearrange("(k p) d -> p k d", p=128)),
                     (w0[:, KD:2 * KD, :], a["L0_gnn_W_r"].rearrange("(k p) d -> p k d", p=128)),
                     (w1[:], a["L1_gnn_W1"].rearrange("(k p) d -> p k d", p=128)),
                     (w2[:], a["L1_gnn_W2"].rearrange("(k p) d -> p k d", p=128)),
                     (w_att[:], a["L3_gnn_W"].rearrange("(k p) d -> p k d", p=128))]
            loads += [(t[:], row_bc(a[n], WN)) for t, n in ((bias0, "L0_gnn_b_r"), (bias_rel, "L2_gnn_bias"),
                                                           (gamma, "L3_gnn_gamma"), (beta, "L3_gnn_beta"))]
            loads += [(t[:], row_bc(a[n].rearrange("h d -> (h d)"), WN)) for t, n in
                      ((a_src, "L3_gnn_a_src"), (a_dst, "L3_gnn_a_dst"))]
            loads += [(v1[:, i, :], a["L1_gnn_" + n].rearrange("(k p) -> p k", p=128))
                      for i, n in enumerate(("b1", "bn_gamma", "bn_beta"))]
            loads += [(v2[:, i, :], a["L1_gnn_" + n].rearrange("(k p) -> p k", p=128))
                      for i, n in enumerate(("b2", "ln_w", "ln_b", "gn_w", "gn_b", "gn_ms"))]
            assert len(loads) == WEIGHT_LOADS
            with nc.allow_non_contiguous_dma("vectors of a few hundred elements"):
                for dst, src in loads:
                    sp.dma_start(dst, src).then_inc(s_w, 16)

            sp.wait_ge(s_pen, 1)
            sp.dma_start(start_table, starts_g).then_inc(s_pent, 16)
            sp.wait_ge(s_h[0], NW)
            sp.dma_start(h_table[0].rearrange("(w p) d -> p w d", p=WN), h[:]).then_inc(s_table[0], 16)
            sp.wait_ge(s_h[1], NW)
            sp.dma_start(h_table[1].rearrange("(w p) d -> p w d", p=WN), h[:]).then_inc(s_table[1], 16)

            attr_h = a["edge_attr_256"].rearrange("(g j p) d -> g p j d", j=GT, p=TE)
            for b in range(RING):
                sp.dma_start(attr[:, b, :, :], attr_h[b, :, :, :]).then_inc(s_attr[b], 16)
            with sp.Fori(0, NG // RING - 1) as i:
                for b in range(RING):
                    sp.wait_ge(s_add, RING * i + b + 1)
                    sp.dma_start(attr[:, b, :, :],
                                 attr_h[bass.ds(RING * i + RING + b, 1), :, :, :].rearrange("g p j d -> (g p) j d")
                                 ).then_inc(s_attr[b], 16)

            sp.wait_ge(s_z2p, KD * NC)
            for k in range(KD):
                sp.dma_start(w_rel[:, k, :, :], a["L2_gnn_weight"][:, 128 * k:128 * k + 128, :].rearrange("r p d -> p r d")
                             ).then_inc(s_wrel, 16)

            xt_h = xt_table.rearrange("(r w p) d -> w p r d", r=R, p=WN)

            def store_xt(i, b, first):
                sp.wait_ge(s_ev[2], R // 2 * (2 * i + b + 1))
                sp.dma_start(xt_h[bass.ds(2 * i + b, 1), :, :, :].rearrange("w p r d -> (w p) r d"),
                             xt_out[:, b, :].rearrange("p (r d) -> p r d", r=R)).then_inc(s_xt[b], 16)
            pairs(sp, store_xt)

            hh_h = hh_table.rearrange("(w p) d -> w p d", p=WN)

            def store_hh(i, b, first):
                sp.wait_ge(s_ev[3], 2 * i + b + 1)
                sp.dma_start(hh_h[bass.ds(2 * i + b, 1), :, :].rearrange("w p d -> (w p) d"),
                             hh_out[:, b, :]).then_inc(s_hh[b], 16)
            pairs(sp, store_hh)

            def load_starts(g, b):
                sp.dma_start(starts[:, b, :], start_table[bass.ds(g, 1), :].broadcast_to([H, GE])).then_inc(s_starts[b], 16)
            sp.wait_ge(s_x_new[2], 1)
            for b in range(RING):
                load_starts(b, b)
            with sp.Fori(0, NG // RING - 1) as i:
                for b in range(RING):
                    sp.wait_ge(s_slot[3], RING * i + b + RING + 1)
                    load_starts(RING * i + b + RING, b)
            sp.wait_ge(s_x_new[3], 1)
            sp.dma_start(out.rearrange("(w p) d -> p w d", p=WN), x[:]).then_inc(s_out, 16)
            sp.wait_ge(s_out, 16)

        @block.gpsimd
        def _(pool):
            nc.gpsimd.memset(ident[:], 0.0)
            nc.gpsimd.memset(ones[:], 1.0)
            nc.gpsimd.memset(src_idx[:, NG:, :], 0)
            nc.gpsimd.memset(rel_idx[:, NG:, :], 0)
            nc.gpsimd.memset(zeros[:], 0.0)
            nc.gpsimd.iota(place_of_group[:], [[GE - 1, 2]], base=0, channel_multiplier=GE, allow_small_or_imprecise_dtypes=True)
            nc.gpsimd.memset(before[:], 1.0)
            nc.gpsimd.memset(base[:], 0.0)
            nc.gpsimd.iota(tile_iota, [[1, NG * GT]], base=0, channel_multiplier=0, allow_small_or_imprecise_dtypes=True)
            nc.gpsimd.iota(lane_iota, [[1, TE]], base=0, channel_multiplier=0, allow_small_or_imprecise_dtypes=True)
            nc.gpsimd.iota(bounds[:], [[WN, NW + RING + 1]], base=0, channel_multiplier=0, allow_small_or_imprecise_dtypes=True)
            nc.gpsimd.iota(node_iota[:], [[1, N]], base=0, channel_multiplier=0, allow_small_or_imprecise_dtypes=True)
            pool.drain()
            nc.gpsimd.affine_select(out=before[:], in_=before[:], compare_op=ALU.is_gt, fill=0.0, base=0,
                                    pattern=[[1, 128]], channel_multiplier=-1)
            nc.gpsimd.affine_select(out=ident[:], in_=ident[:], compare_op=ALU.not_equal, fill=1.0, base=0,
                                    pattern=[[-1, 128]], channel_multiplier=1).then_inc(s_const, 1)
            nc.gpsimd.memset(acc[:], 0.0).then_inc(s_zero[0], 1)
            pool.wait_ge(s_lists, 1)
            pool.wait_ge(s_pent, 16)
            nc.gpsimd.memset(rows[:, :, :, D:D + 1], 1.0).then_inc(s_zero[0], 1)

            def gathers(l, table, width, written):
                for s, n in written:
                    pool.wait_ge(s, n)

                def step(i, b):
                    pool.wait_ge(s_slot[l], RING * i + b + 1)
                    pool.sem_inc(s_begun, 1)
                    for j in range(GT):
                        pool.indirect_dma_start(rows[:, b, j, 0:width], None, table,
                                                bass.IndirectOffsetOnAxis(ap=slot[:, b, j:j + 1], axis=0)
                                                ).then_inc(s_rows[l][b], 16)
                rings(pool, step)

            gathers(0, h_table[0], D, [(s_table[0], 16)])
            pool.wait_ge(s_nb[0], NW)
            nc.gpsimd.memset(acc[:], 0.0).then_inc(s_zero[1], 1)
            gathers(1, h_table[1], D, [(s_table[1], 16)])
            pool.wait_ge(s_perm, 1)
            nc.gpsimd.iota(moves[:, 2, :, :].rearrange("p g j -> p (g j)"), [[TE, NG * GT]], base=0, channel_multiplier=1,
                           allow_small_or_imprecise_dtypes=True).then_inc(s_posi, 1)
            pool.wait_ge(s_nb[1], NW)
            nc.gpsimd.memset(acc[:], 0.0).then_inc(s_zero[2], 1)
            gathers(2, xt_table, D, [(s_xt[b], 16 * NW // 2) for b in range(2)])
            pool.wait_ge(s_x_new[2], 1)
            nc.gpsimd.memset(acc[:], 0.0).then_inc(s_zero[3], 1)
            gathers(3, hh_table, DH, [(s_hh[b], 16 * NW // 2) for b in range(2)])

        @block.scalar
        def _(act):
            def normed(l):
                act.wait_ge(s_var[l], 1)
                nc.scalar.activation(rstd[:], rstd[:], ACT.Sqrt).then_inc(s_std[l], 1)
                act.wait_ge(s_rstd[l], 1)
                with act.Fori(0, NW) as w:
                    nc.scalar.activation(window(h, w), window(x, w), ACT.Relu,
                                         bias=shift[:, bass.ds(w, 1)], scale=rstd[:, bass.ds(w, 1)]).then_inc(s_h[l], 1)

            def turned(l, blocks):
                def step(i, b, first):
                    act.wait_ge(s_nt[l], 2 * i + b + 1)
                    if not first:
                        act.wait_ge(s_mm[l], MM_STEPS[l] * (2 * i + b - 1))
                    nc.scalar.activation(nodesT_b[:, b, 0:blocks * WN], bank[b][:, 0:blocks * WN], ACT.Copy
                                         ).then_inc(s_ntc[l], 1)
                pairs(act, step)

            normed(0)
            turned(0, 2 * KD)
            normed(1)

            def relu_rows(i, b):
                act.wait_ge(s_add, RING * i + b + 1)
                nc.scalar.activation(rows[:, b, :, 0:D], rows[:, b, :, 0:D], ACT.Relu).then_inc(s_relu, 1)
            rings(act, relu_rows)

            def keep_hT(i, b, first):
                act.wait_ge(s_nt[1], 2 * i + b + 1)
                nc.scalar.activation(hT[:, :, bass.ds(WN * (2 * i + b), WN)],
                                     bank[b][:, 0:KD * WN].rearrange("p (k n) -> p k n", k=KD), ACT.Copy
                                     ).then_inc(s_ntc[1], 1)
            pairs(act, keep_hT)
            with act.Fori(0, NC) as c:
                for m in range(KH):
                    act.wait_ge(s_z1p, KH * c + m + 1)
                    nc.scalar.activation(z1T[:, m, bass.ds(CN * c, CN)], bank[2 + m][:, 0:CN], ACT.Identity,
                                         bias=v1[:, 0, m:m + 1]).then_inc(s_z1, 1)
            act.wait_ge(s_st1, 1)
            nc.scalar.activation(sc1[:, 0, :], sc1[:, 0, :], ACT.Sqrt).then_inc(s_sd1, 1)
            act.wait_ge(s_bn, 1)
            for m in range(KH):
                nc.scalar.activation(z1T[:, m, :], z1T[:, m, :], ACT.Relu, bias=sc1[:, 1, m:m + 1],
                                     scale=sc1[:, 0, m:m + 1]).then_inc(s_z1n, 1)
            with act.Fori(0, NC) as c:
                for m in range(KD):
                    act.wait_ge(s_z2p, KD * c + m + 1)
                    nc.scalar.activation(hT[:, m, bass.ds(CN * c, CN)], bank[m][:, 0:CN], ACT.Identity,
                                         bias=v2[:, 0, m:m + 1]).then_inc(s_z2, 1)
            act.wait_ge(s_sd, 1)
            nc.scalar.activation(g1[:, 3:4], g1[:, 3:4], ACT.Sqrt).then_inc(s_sdr, 1)
            act.wait_ge(s_sd, 2)
            nc.scalar.activation(t2[:, 5, :], t2[:, 5, :], ACT.Sqrt).then_inc(s_sdr, 1)
            act.wait_ge(s_fin, 1)

            def final_relu(i, b, first):
                if not first:
                    act.wait_ge(s_obt, 2 * i + b - 1)
                for k in range(KD):
                    last = nc.scalar.activation(nodesT_b[:, b, WN * k:WN * k + WN], hT[:, k, bass.ds(WN * (2 * i + b), WN)],
                                                ACT.Relu, bias=t2[:, 7, k:k + 1], scale=t2[:, 6, k:k + 1])
                last.then_inc(s_ob, 1)
            pairs(act, final_relu)

            normed(2)
            turned(2, KD)
            normed(3)
            turned(3, KD)

            def attention(w, mixed):
                v = visits.next()
                act.wait_ge(s_oht, v)
                nc.scalar.activation(onehot_t[:, 0:4 * TE], bank[0][0:WN, :], ACT.Copy)
                nc.scalar.activation(onehot_t[:, 4 * TE:], bank[1][0:WN, 0:TE], ACT.Copy).then_inc(s_ohtc, 1)
                act.wait_ge(s_dec, v)
                nc.scalar.activation(decay[:], decay[:], ACT.Exp).then_inc(s_dexp, 1)
                act.wait_ge(s_arg, v)
                nc.scalar.activation(weight[:], score[:], ACT.Exp).then_inc(s_exp, 1)
            visits = Visits(act)
            rings(act, lambda i, b: each_window(act, RING * i + b, attention, attention))

            act.wait_ge(s_var[4], 1)
            nc.scalar.activation(rstd[:], rstd[:], ACT.Sqrt).then_inc(s_std[4], 1)
            act.wait_ge(s_elu, 1)
            nc.scalar.activation(acc[:, :, 0:D], acc[:, :, 0:D], ACT.Exp).then_inc(s_elud, 1)

        @block.tensor
        def _(pe):
            pe.wait_ge(s_const, 1)
            pe.wait_ge(s_flt, 1)
            for i, part in enumerate((flt[:, 0, :], flt[:, 1, :], flt[:, 3, :])):
                for j in range(GT):
                    q = i * GT + j
                    last = nc.tensor.transpose(bank[q // 4][:, 128 * (q % 4):128 * (q % 4) + NG],
                                               part[:, TE * j:TE * j + TE], ident[0:NG, 0:NG])
            last.then_inc(s_lists_t, 1)
            pe.wait_ge(s_flt, 2)
            nc.tensor.transpose(bank[4][0:1, 0:NG], span_f[:, 2:3], ident[0:NG, 0:NG]).then_inc(s_lists_t, 1)
            pe.wait_ge(s_share, 1)
            nc.tensor.matmul(bank[5][0:NG, 0:NW], before[0:NG, 0:NG], share[:], start=True, stop=True)
            nc.tensor.matmul(bank[5][:, NW:2 * NW], ones[0:NG, :], share[:], start=True, stop=True).then_inc(s_prefix, 1)

            def turn(l, blocks):
                def step(i, b, first):
                    pe.wait_ge(s_nb[l], 2 * i + b + 1)
                    if not first:
                        pe.wait_ge(s_ntc[l], 2 * i + b - 1)
                    for k in range(blocks):
                        last = nc.tensor.transpose(bank[b][:, WN * k:WN * k + WN], nodes_b[:, b, 128 * k:128 * k + 128],
                                                   ident[0:WN, 0:WN])
                    last.then_inc(s_nt[l], 1)
                return step

            def two_steps(first_step, second_step):
                for b in range(2):
                    first_step(0, b, True)
                for b in range(2):
                    second_step(0, b, True)
                with pe.Fori(1, NW // 2) as i:
                    for b in range(2):
                        first_step(i, b, False)
                    for b in range(2):
                        second_step(i, b, False)

            def sums(l, width, ready, after=lambda i, b: None):
                visits = Visits(pe)
                nc.tensor.matmul(bank[6][0:WN, 0:width], ident[:, 0:WN], zeros[:, 0:width], start=True, stop=True).then_inc(s_sum[l], 1)

                def step(i, b):
                    def visit(w, mixed):
                        pe.wait_ge(s_onehot[l], visits.next())
                        for j in range(GT):
                            last = nc.tensor.matmul(bank[6 + b % 2][0:WN, 0:width], onehot[b % 2][:, j, :], rows[:, b, j, 0:width],
                                                    start=(j == 0), stop=(j == GT - 1))
                        last.then_inc(s_sum[l], 1)
                    ready(i, b)
                    each_window(pe, RING * i + b, visit, visit, by=int(l == 2))
                    after(i, b)
                rings(pe, step)

            pe.wait_ge(s_zero[0], 2)
            sums(0, D + 1, lambda i, b: pe.wait_ge(s_rows[0][b], 16 * GT * (i + 1)))
            pe.wait_ge(s_digits, 1)
            for i, part in enumerate((order, inside, above, rel_g)):
                for j in range(GT):
                    q = i * GT + j
                    last = nc.tensor.transpose(bank[q // 4][:, 128 * (q % 4):128 * (q % 4) + NG],
                                               part[:, TE * j:TE * j + TE], ident[0:NG, 0:NG])
            last.then_inc(s_digits_t, 1)
            pe.wait_ge(s_moves, 1)
            pe.wait_ge(s_w, 16 * WEIGHT_LOADS)

            def products0(i, b, first):
                pe.wait_ge(s_ntc[0], 2 * i + b + 1)
                if not first:
                    pe.wait_ge(s_ev[0], 2 * i + b - 1)
                for k in range(2 * KD):
                    last = nc.tensor.matmul(bank[2 + b][0:WN, 0:D], nodesT_b[:, b, WN * k:WN * k + WN], w0[:, k, :],
                                            start=(k == 0), stop=(k == 2 * KD - 1))
                last.then_inc(s_mm[0], 1)
            two_steps(turn(0, 2 * KD), products0)

            HALF = (NG * GT + 1) // 2

            def permute(j_stat, j_mov, start, stop):
                for k in range(2):
                    for part in range(2):
                        n = min(HALF, NG * GT - HALF * part)
                        last = nc.tensor.matmul(bank[2 * k + part][:, 0:n], j_stat(k), j_mov(HALF * part, n), start=start, stop=stop)
                return last
            pe.wait_ge(s_ntc[0], NW)
            pe.wait_ge(s_ev[0], NW)
            permute(lambda k: ident[:], lambda o, n: zeros[:, 0:n], True, False).then_inc(s_turned, 1)

            def permute_group(i, b):
                pe.wait_ge(s_turn, RING * i + b + 1)
                for j in range(GT):
                    last = permute(lambda k: turn_p[:, j, k, :], lambda o, n: turn_t[:, j, o:o + n], False, False)
                last.then_inc(s_turned, 1)
            sums(1, D, lambda i, b: pe.wait_ge(s_relu, RING * i + b + 1), permute_group)
            permute(lambda k: ident[:], lambda o, n: zeros[:, 0:n], False, True).then_inc(s_turned, 1)
            pe.wait_ge(s_perm, 1)
            pairs(pe, turn(1, KD))
            pe.wait_ge(s_ntc[1], NW)

            def z1_chunk(c, first):
                for m in range(KH):
                    if not first:
                        pe.wait_ge(s_z1, KH * (c - 1) + m + 1)
                    for k in range(KD):
                        last = nc.tensor.matmul(bank[2 + m][:, 0:CN], w1[:, k, 128 * m:128 * m + 128],
                                                hT[:, k, bass.ds(CN * c, CN)], start=(k == 0), stop=(k == KD - 1))
                    last.then_inc(s_z1p, 1)
            z1_chunk(0, True)
            with pe.Fori(1, NC) as c:
                z1_chunk(c, False)

            pe.wait_ge(s_z1n, KH)

            def z2_chunk(c, first):
                for m in range(KD):
                    if not first:
                        pe.wait_ge(s_z2, KD * (c - 1) + m + 1)
                    for k in range(KH):
                        last = nc.tensor.matmul(bank[m][:, 0:CN], w2[:, k, 128 * m:128 * m + 128],
                                                z1T[:, k, bass.ds(CN * c, CN)], start=(k == 0), stop=(k == KH - 1))
                    last.then_inc(s_z2p, 1)
            z2_chunk(0, True)
            with pe.Fori(1, NC) as c:
                z2_chunk(c, False)

            for n in range(2):
                pe.wait_ge(s_g, n + 1)
                nc.tensor.matmul(bank[4][:, 0:1], ones[:], g1[:, n:n + 1], start=True, stop=True).then_inc(s_gp, 1)

            def out_back(i, b, first):
                pe.wait_ge(s_ob, 2 * i + b + 1)
                if not first:
                    pe.wait_ge(s_ev[1], 2 * i + b - 1)
                for k in range(KD):
                    last = nc.tensor.transpose(bank[2 + b][0:WN, 128 * k:128 * k + 128],
                                               nodesT_b[:, b, WN * k:WN * k + WN], ident[:])
                last.then_inc(s_obt, 1)
            pairs(pe, out_back)

            def products2(i, b, first):
                pe.wait_ge(s_ntc[2], 2 * i + b + 1)
                for q in range(R // 2):
                    if not (first and b == 0):
                        pe.wait_ge(s_ev[2], R // 2 * (2 * i + b - 1) + q + 1)
                    for k in range(KD):
                        last = nc.tensor.matmul(bank[2 + q][0:WN, :], nodesT_b[:, b, WN * k:WN * k + WN],
                                                w_rel[:, k, 2 * q:2 * q + 2, :].rearrange("p r d -> p (r d)"),
                                                start=(k == 0), stop=(k == KD - 1))
                    last.then_inc(s_mm[2], 1)
            pe.wait_ge(s_wrel, 16 * KD)
            two_steps(turn(2, KD), products2)
            pe.wait_ge(s_flt, 3)
            nc.tensor.transpose(bank[6][0:1, 0:NG], span_f[:, 2:3], ident[0:NG, 0:NG]).then_inc(s_lists_t, 1)
            pe.wait_ge(s_lists, 2)
            sums(2, D, lambda i, b: pe.wait_ge(s_rows[2][b], 16 * GT * (i + 1)))

            def products3(i, b, first):
                pe.wait_ge(s_ntc[3], 2 * i + b + 1)
                if not first:
                    pe.wait_ge(s_ev[3], 2 * i + b - 1)
                for k in range(KD):
                    last = nc.tensor.matmul(bank[2 + b][0:WN, 0:D], nodesT_b[:, b, WN * k:WN * k + WN], w_att[:, k, :],
                                            start=(k == 0), stop=(k == KD - 1))
                last.then_inc(s_mm[3], 1)
            two_steps(turn(3, KD), products3)

            visits, tiles, fast = Visits(pe), Visits(pe, GT), Visits(pe)

            def weighted_sum(b):
                for j in range(GT):
                    last = nc.tensor.matmul(bank[6 + b % 2][0:WN, 0:DH], onehot[b % 2][:, j, :], msg[:, j, :], start=(j == 0),
                                            stop=(j == GT - 1))
                last.then_inc(s_sum[3], 1)

            def turn_scores(b):
                for j in range(GT):
                    last = nc.tensor.transpose(psum[0:H, 1024 + TE * j:1024 + TE * j + TE], rows[:, b, j, D:DH], ident[:])
                last.then_inc(s_sT, 1)

            def turn_onehots(b):
                for j in range(GT):
                    last = nc.tensor.transpose(bank[j // 4][0:WN, TE * (j % 4):TE * (j % 4) + TE], onehot[b % 2][:, j, :], ident[:])
                last.then_inc(s_oht, 1)

            def highest_by_scan(b):
                u = fast.next()
                pe.wait_ge(s_run, u)
                pe.sem_inc(s_scanned, 1)
                for j in range(GT):
                    last = nc.tensor.transpose(bank[5][:, H * j:H * j + H], run[:, TE * j:TE * j + TE], ident[0:H, 0:H])
                last.then_inc(s_runT, 1)
                pe.wait_ge(s_lastv, u)
                for j in range(GT):
                    last = nc.tensor.matmul(bank[5][0:WN, 64:64 + H + 1], onehot[b % 2][:, j, :], last_max[:, j, :], start=(j == 0), stop=(j == GT - 1))
                last.then_inc(s_nmax, 1)

            def highest_by_mask(b):
                for j in range(GT):
                    pe.wait_ge(s_diag, tiles.next())
                    for q in range(2):
                        last = nc.tensor.matmul(bank[2 + q][0:WN, :], onehot[b % 2][:, j, :],
                                                diag[:, 4 * q:4 * q + 4, :].rearrange("p h e -> p (h e)"), start=True, stop=True)
                    last.then_inc(s_spread, 1)

            nc.tensor.matmul(bank[6][0:WN, 0:DH], ident[:, 0:WN], zeros[:, 0:DH], start=True, stop=True).then_inc(s_sum[3], 1)

            def attention(b, before, apart):
                def visit(w, mixed):
                    v = visits.next()
                    if not apart:
                        pe.wait_ge(s_msg, v)
                        weighted_sum(before)
                    turn_scores(b)
                    pe.wait_ge(s_onehot[3], v)
                    turn_onehots(b)

                    def sum_before():
                        if apart:
                            pe.wait_ge(s_msg, v)
                            weighted_sum(before)
                    with pe.If(mixed > 0):
                        sum_before()
                        highest_by_mask(b)
                    with pe.Else():
                        highest_by_scan(b)
                        sum_before()
                    pe.wait_ge(s_ohtc, v)
                    pe.wait_ge(s_ref, v)
                    for j in range(GT):
                        last = nc.tensor.matmul(bank[4][:, 2 * H * j:2 * H * j + 2 * H], onehot_t[:, TE * j:TE * j + TE],
                                                node_ref[:], start=True, stop=True)
                    last.then_inc(s_back, 1)
                return visit

            def step3(i, b):
                pe.wait_ge(s_rows[3][b], 16 * GT * (i + 1))
                before = ring_before(b)
                each_window(pe, RING * i + b, attention(b, before, before % 2 != b % 2), attention(b, b, False))
            rings(pe, step3)
            pe.wait_ge(s_msg, visits.next())
            weighted_sum(RING - 1)

        @block.vector
        def _(dve):
            V = nc.vector

            dve.wait_ge(s_edges, 48)
            V.tensor_copy(flt[:, 0:3, :], raw[:])
            dve.drain()
            V.tensor_tensor(flt[:, 3, 0:GE - 1], flt[:, 0, 0:GE - 1], flt[:, 0, 1:GE], ALU.not_equal)
            V.memset(flt[:, 3, GE - 1:GE], 1.0).then_inc(s_flt, 1)
            V.scalar_tensor_tensor(rel_g, flt[:, 2, :], float(N), flt[:, 0, :], ALU.mult, ALU.add)
            V.tensor_copy(src_g, flt[:, 1, :])
            dve.drain()
            V.tensor_tensor(flt[:, 2, 0:GE - 1], flt[:, 0, 0:GE - 1], flt[:, 0, 1:GE], ALU.is_gt)
            V.tensor_reduce(span_f[:, 0:1], flt[:, 0, :], AX.X, ALU.min)
            V.tensor_reduce(span_f[:, 1:2], flt[:, 0, :], AX.X, ALU.max)
            dve.drain()
            V.memset(starts_g[:, 0:1], -BIG)
            V.tensor_scalar(starts_g[:, 1:GE], flt[:, 3, 0:GE - 1], -BIG, None, ALU.mult).then_inc(s_pen, 1)
            V.tensor_reduce(rank[:, 6:7], flt[:, 2, 0:GE - 1], AX.X, ALU.max)
            dve.wait_ge(s_const, 1)
            dve.drain()
            def span(windows):
                for q in range(2):
                    V.tensor_scalar(cmp[:, q, :], windows, span_f[:, q:q + 1], None, ALU.is_le)
                dve.drain()
                V.tensor_reduce(rank[:, 0:2], cmp[:], AX.X, ALU.add)
                dve.drain()
                V.tensor_scalar(rank[:, 2:3], rank[:, 1:2], 1.0, 32.0, ALU.add, ALU.mult)
                dve.drain()
                V.tensor_tensor(span_f[:, 2:3], rank[:, 2:3], rank[:, 0:1], ALU.add)
                dve.drain()
            span(bounds[0:NG, 1:NW])
            V.scalar_tensor_tensor(span_f[:, 2:3], rank[:, 6:7], 1024.0, span_f[:, 2:3], ALU.mult, ALU.add).then_inc(s_flt, 1)
            dve.wait_ge(s_lists_t, 1)
            for i, t in enumerate((dst_f, src_idx, last_f)):
                for j in range(GT):
                    q = i * GT + j
                    V.tensor_copy(t[:, 0:NG, j], bank[q // 4][:, 128 * (q % 4):128 * (q % 4) + NG])
            dve.wait_ge(s_lists_t, 2)
            V.tensor_copy(spans[0:1, 0, :], bank[4][0:1, 0:NG]).then_inc(s_lists, 1)

            def statistics(w, of):
                V.bn_stats(stats[:, bass.ds(w, 1), :].rearrange("p w s -> p (w s)"), of)

            def norm(l):
                dve.drain()
                for w in range(NW):
                    V.bn_aggr(mean_var[:, w, :], stats[:, w, :])
                dve.drain()
                V.tensor_scalar_add(rstd[:], mean_var[:, :, 1], EPS).then_inc(s_var[l], 1)
                dve.wait_ge(s_std[l], 1)
                V.reciprocal(rstd[:], rstd[:])
                dve.drain()
                V.scalar_tensor_tensor(shift[:], mean_var[:, :, 0], -1.0, rstd[:], ALU.mult, ALU.mult).then_inc(s_rstd[l], 1)

            def fill_slot(idx, g, b, l):
                V.tensor_copy(slot[:, b, :], idx[:, bass.ds(g, 1), :].rearrange("p g j -> p (g j)")).then_inc(s_slot[l], 1)

            def onehots(g, w, l, q, nodes=dst_f):
                V.tensor_tensor(onehot[q], node_iota[:, bass.ds(w * WN, WN)].rearrange("p (j n) -> p j n", j=1).broadcast_to([128, GT, WN]),
                                nodes[:, bass.ds(g, 1), :].rearrange("p g (j n) -> p (g j) n", n=1).broadcast_to([128, GT, WN]),
                                ALU.is_equal).then_inc(s_onehot[l], 1)

            def window_register():
                reg = dve.alloc_register(f"window_{nc.next_id()}")
                dve.reg_mov(reg, 0)
                return reg

            def held(reg):
                return nc.s_assert_within(dve.snap(reg), 0, NW - 1, skip_runtime_bounds_check_because="it holds a window of nodes")

            def hold(reg, w):
                dve.reg_add(reg, dve.snap(w), 0)

            def sums(l, width, idx, before, after=lambda i, b: None):
                for b in range(RING - 1):
                    fill_slot(idx, b, b, l)
                visits, pending = Visits(dve), window_register()
                nodes = src_f if l == 2 else dst_f
                dve.wait_ge(s_zero[l], 1)

                def add_pending(b):
                    w = held(pending)
                    dve.drain()
                    dve.wait_ge(s_sum[l], visits.now())
                    V.tensor_tensor(acc[:, bass.ds(w, 1), 0:width].rearrange("p w d -> p (w d)"),
                                    acc[:, bass.ds(w, 1), 0:width].rearrange("p w d -> p (w d)"),
                                    bank[6 + b % 2][0:WN, 0:width], ALU.add)

                def step(i, b):
                    g = RING * i + b
                    last = ring_before(b)
                    before(i, b)

                    def first_visit(w, mixed):
                        visits.next()
                        if last % 2 != b % 2:
                            onehots(g, w, l, b % 2, nodes)
                            add_pending(last)
                        else:
                            add_pending(last)
                            onehots(g, w, l, b % 2, nodes)
                        hold(pending, w)
                        fill_slot(idx, g + RING - 1, last, l)

                    def further_visit(w, mixed):
                        visits.next()
                        add_pending(b)
                        onehots(g, w, l, b % 2, nodes)
                        hold(pending, w)
                    each_window(dve, g, first_visit, further_visit, by=int(l == 2))
                    after(i, b)
                rings(dve, step)
                visits.next()
                add_pending(RING - 1)

            dve.wait_ge(s_x, 16)
            with dve.Fori(0, NW) as w:
                statistics(w, window(x, w))
            norm(0)
            V.memset(reach[:, 0:1], float(GE))
            V.memset(reach[:, NW:NW + 1], 0.0)
            with dve.Fori(1, NW) as w:
                V.tensor_scalar(above, src_g, bounds[0:NG, bass.ds(w, 1)], None, ALU.is_ge)
                dve.drain()
                V.tensor_reduce(reach[:, bass.ds(w, 1)], above, AX.X, ALU.add)
                dve.drain()
            V.memset(pos_g, 0.0)
            V.memset(win_g, 0.0)
            dve.drain()
            V.tensor_tensor(share[:], reach[:, 0:NW], reach[:, 1:NW + 1], ALU.subtract).then_inc(s_share, 1)
            dve.wait_ge(s_prefix, 1)
            V.tensor_copy(total[:], bank[5][:, NW:2 * NW])
            dve.drain()
            V.tensor_tensor_scan(offset[:], total[:], zeros[:, 0:NW], 0.0, ALU.add, ALU.add)
            dve.drain()
            V.tensor_tensor(offset[:], offset[:], total[:], ALU.subtract)
            dve.drain()
            V.scalar_tensor_tensor(base[:, 0:NW], bank[5][0:NG, 0:NW], -1.0, offset[0:NG, :], ALU.add, ALU.add)
            dve.drain()

            def rank_edges(i, b):
                if b:
                    return
                w = bass.ds(i, 1)
                V.tensor_scalar(above, src_g, bounds[0:NG, bass.ds(i + 1, 1)], None, ALU.is_ge)
                dve.drain()
                V.scalar_tensor_tensor(inside, src_g, bounds[0:NG, w], above, ALU.is_ge, ALU.subtract)
                V.tensor_tensor(win_g, win_g, above, ALU.add)
                dve.drain()
                V.tensor_tensor_scan(order, inside, zeros[0:NG, 0:1].broadcast_to([NG, GE]), base[:, w], ALU.add, ALU.add)
                dve.drain()
                V.tensor_tensor(order, order, inside, ALU.mult)
                dve.drain()
                V.tensor_tensor(pos_g, pos_g, order, ALU.add)
                dve.drain()
            sums(0, D + 1, src_idx, rank_edges)
            dve.drain()
            ints = lambda t: t.bitcast(I32)
            V.tensor_copy(ints(above), pos_g)
            V.tensor_copy(ints(spare), rel_g)
            V.scalar_tensor_tensor(src_g, win_g, -float(WN), src_g, ALU.mult, ALU.add)
            dve.drain()
            V.tensor_single_scalar(ints(inside), ints(above), 7, ALU.arith_shift_right)
            dve.drain()
            V.tensor_single_scalar(ints(above), ints(above), TE - 1, ALU.bitwise_and)
            V.tensor_single_scalar(ints(win_g), ints(spare), 11, ALU.arith_shift_right)
            V.tensor_single_scalar(ints(rel_g), ints(spare), 2047, ALU.bitwise_and)
            dve.drain()
            V.tensor_copy(order, ints(above))
            V.tensor_copy(pos_g, ints(inside))
            dve.drain()
            V.tensor_copy(above, ints(rel_g))
            V.tensor_copy(inside, ints(win_g))
            dve.drain()
            V.scalar_tensor_tensor(rel_g, src_g, 16.0, inside, ALU.mult, ALU.add)
            dve.drain()
            V.tensor_copy(inside, pos_g).then_inc(s_digits, 1)
            dve.wait_ge(s_digits_t, 1)
            for i in range(4):
                for j in range(GT):
                    q = i * GT + j
                    last = V.tensor_copy(moves[:, i, :, j], bank[q // 4][:, 128 * (q % 4):128 * (q % 4) + NG])
            last.then_inc(s_moves, 1)
            V.tensor_scalar_max(rstd[:], acc[:, :, D], 1.0)
            dve.drain()
            V.reciprocal(rstd[:], rstd[:])
            dve.drain()

            def stage0(i, b, first):
                if not first:
                    dve.wait_ge(s_nt[0], 2 * i + b - 1)
                w = 2 * i + b
                V.tensor_scalar(nodes_b[:, b, 0:D], acc[:, bass.ds(w, 1), 0:D].rearrange("p w d -> p (w d)"),
                                rstd[:, bass.ds(w, 1)], None, ALU.mult)
                V.tensor_copy(nodes_b[:, b, D:2 * D], window(h, w)).then_inc(s_nb[0], 1)

            def take0(i, b, first):
                w = 2 * i + b
                dve.wait_ge(s_mm[0], w + 1)
                V.tensor_tensor(prod[:, b, :], bank[2 + b][0:WN, 0:D], bias0[:], ALU.add).then_inc(s_ev[0], 1)
                dve.drain()
                V.tensor_tensor(window(x, w), window(x, w), prod[:, b, :], ALU.add)
                dve.drain()
                statistics(w, window(x, w))
            dve.wait_ge(s_w, 16 * WEIGHT_LOADS)

            def staged_and_taken(stage_, take):
                for b in range(2):
                    stage_(0, b, True)
                for b in range(2):
                    take(0, b, True)
                with dve.Fori(1, NW // 2) as i:
                    for b in range(2):
                        stage_(i, b, False)
                    for b in range(2):
                        take(i, b, False)
            staged_and_taken(stage0, take0)
            norm(1)

            def add_attr(i, b):
                dve.wait_ge(s_rows[1][b], 16 * GT * (i + 1))
                dve.wait_ge(s_attr[b], 16 * (i + 1))
                V.tensor_tensor(rows[:, b, :, 0:D], rows[:, b, :, 0:D], attr[:, b, :, :], ALU.add).then_inc(s_add, 1)

            def turn_edges(i, b):
                g = RING * i + b
                dve.wait_ge(s_turned, g + 1)
                for j in range(GT):
                    lane, tile, low, high = (moves[:, k, bass.ds(g, 1), j] for k in range(4))
                    V.tensor_scalar(turn_t[:, j, 0:NG * GT], tile_iota, tile, None, ALU.is_equal)
                    V.tensor_scalar(turn_p[:, j, 0, :], lane_iota, lane, low, ALU.is_equal, ALU.mult)
                    last = V.tensor_scalar(turn_p[:, j, 1, :], lane_iota, lane, high, ALU.is_equal, ALU.mult)
                last.then_inc(s_turn, 1)
            sums(1, D, src_idx, add_attr, turn_edges)
            dve.wait_ge(s_turned, NG + 2)
            HALF = (NG * GT + 1) // 2
            flat = lambda t: t.rearrange("p g j -> p (g j)")
            for k in range(2):
                V.tensor_copy(flat(moves[:, k, :, :])[:, 0:HALF], bank[2 * k][:, 0:HALF])
                last = V.tensor_copy(flat(moves[:, k, :, :])[:, HALF:], bank[2 * k + 1][:, 0:NG * GT - HALF])
            last.then_inc(s_perm, 1)

            def stage1(i, b, first):
                if not first:
                    dve.wait_ge(s_nt[1], 2 * i + b - 1)
                w = 2 * i + b
                V.tensor_tensor(nodes_b[:, b, 0:D], acc[:, bass.ds(w, 1), 0:D].rearrange("p w d -> p (w d)"),
                                window(h, w), ALU.add).then_inc(s_nb[1], 1)
            pairs(dve, stage1)
            with dve.Fori(0, NC) as c:
                for m in range(KH):
                    dve.wait_ge(s_z1, KH * c + m + 1)
                    V.bn_stats(st1[:, m, bass.ds(c, 1), :].rearrange("p c s -> p (c s)"), z1T[:, m, bass.ds(CN * c, CN)])
            dve.drain()
            for m in range(KH):
                V.bn_aggr(mv1[:, m, :], st1[:, m, :, :].rearrange("p c s -> p (c s)"))
            dve.drain()
            V.tensor_scalar_add(sc1[:, 0, :], mv1[:, :, 1], EPS).then_inc(s_st1, 1)
            dve.wait_ge(s_sd1, 1)
            V.reciprocal(sc1[:, 0, :], sc1[:, 0, :])
            dve.drain()
            V.tensor_tensor(sc1[:, 0, :], sc1[:, 0, :], v1[:, 1, :], ALU.mult)
            dve.drain()
            V.tensor_tensor(sc1[:, 1, :], mv1[:, :, 0], sc1[:, 0, :], ALU.mult)
            dve.drain()
            V.tensor_tensor(sc1[:, 1, :], v1[:, 2, :], sc1[:, 1, :], ALU.subtract).then_inc(s_bn, 1)
            with dve.Fori(0, NC) as c:
                for m in range(KD):
                    dve.wait_ge(s_z2, KD * c + m + 1)
                    V.bn_stats(st2[:, m, bass.ds(c, 1), :].rearrange("p c s -> p (c s)"), hT[:, m, bass.ds(CN * c, CN)])
            dve.drain()
            for m in range(KD):
                V.bn_aggr(mv2[:, m, :], st2[:, m, :, :].rearrange("p c s -> p (c s)"))
            dve.drain()
            mean, var = mv2[:, :, 0], mv2[:, :, 1]
            ln_w, ln_b, gn_w, gn_b, gn_ms = (v2[:, i, :] for i in range(1, 6))
            V.tensor_reduce(g1[:, 0:1], mean, AX.X, ALU.add).then_inc(s_g, 1)
            dve.wait_ge(s_gp, 1)
            V.tensor_scalar(g1[:, 2:3], bank[4][:, 0:1], 1.0 / D, None, ALU.mult)
            dve.drain()
            V.tensor_scalar(t2[:, 0, :], mean, g1[:, 2:3], None, ALU.subtract)
            dve.drain()
            V.tensor_tensor(t2[:, 1, :], t2[:, 0, :], t2[:, 0, :], ALU.mult)
            dve.drain()
            V.tensor_tensor(t2[:, 1, :], t2[:, 1, :], var, ALU.add)
            dve.drain()
            V.tensor_reduce(g1[:, 1:2], t2[:, 1, :], AX.X, ALU.add).then_inc(s_g, 1)
            dve.wait_ge(s_gp, 2)
            V.tensor_scalar(g1[:, 3:4], bank[4][:, 0:1], 1.0 / D, EPS, ALU.mult, ALU.add).then_inc(s_sd, 1)
            dve.wait_ge(s_sdr, 1)
            V.reciprocal(g1[:, 3:4], g1[:, 3:4])
            dve.drain()
            V.tensor_scalar(t2[:, 2, :], ln_w, g1[:, 3:4], None, ALU.mult)
            dve.drain()
            V.tensor_tensor(t2[:, 3, :], t2[:, 0, :], t2[:, 2, :], ALU.mult)
            dve.drain()
            V.tensor_tensor(t2[:, 3, :], t2[:, 3, :], ln_b, ALU.add)
            dve.drain()
            V.tensor_tensor(t2[:, 4, :], t2[:, 3, :], gn_ms, ALU.mult)
            dve.drain()
            V.tensor_tensor(t2[:, 4, :], t2[:, 3, :], t2[:, 4, :], ALU.subtract)
            V.tensor_tensor(t2[:, 5, :], t2[:, 2, :], t2[:, 2, :], ALU.mult)
            dve.drain()
            V.tensor_tensor(t2[:, 5, :], t2[:, 5, :], var, ALU.mult)
            V.tensor_tensor(t2[:, 1, :], t2[:, 4, :], t2[:, 4, :], ALU.mult)
            dve.drain()
            V.scalar_tensor_tensor(t2[:, 5, :], t2[:, 5, :], EPS, t2[:, 1, :], ALU.add, ALU.add).then_inc(s_sd, 1)
            dve.wait_ge(s_sdr, 2)
            V.reciprocal(t2[:, 5, :], t2[:, 5, :])
            dve.drain()
            V.tensor_tensor(t2[:, 5, :], t2[:, 5, :], gn_w, ALU.mult)
            dve.drain()
            V.tensor_tensor(t2[:, 6, :], t2[:, 2, :], t2[:, 5, :], ALU.mult)
            V.tensor_tensor(t2[:, 7, :], t2[:, 4, :], t2[:, 5, :], ALU.mult)
            dve.drain()
            V.tensor_tensor(t2[:, 7, :], t2[:, 7, :], gn_b, ALU.add)
            V.tensor_tensor(t2[:, 1, :], t2[:, 6, :], mean, ALU.mult)
            dve.drain()
            V.tensor_tensor(t2[:, 7, :], t2[:, 7, :], t2[:, 1, :], ALU.subtract).then_inc(s_fin, 1)

            def take1(i, b, first):
                w = 2 * i + b
                dve.wait_ge(s_obt, w + 1)
                V.tensor_tensor(prod[:, b, :], bank[2 + b][0:WN, 0:D], window(h, w), ALU.add).then_inc(s_ev[1], 1)
                dve.drain()
                V.tensor_tensor(window(x, w), window(x, w), prod[:, b, :], ALU.add)
                dve.drain()
                statistics(w, window(x, w))
            pairs(dve, take1)
            norm(2)

            def stage_h(l):
                def step(i, b, first):
                    dve.wait_ge(s_h[l], 2 * i + b + 1)
                    if not first:
                        dve.wait_ge(s_nt[l], 2 * i + b - 1)
                    V.tensor_copy(nodes_b[:, b, 0:D], window(h, 2 * i + b)).then_inc(s_nb[l], 1)
                return step

            def take2(i, b, first):
                if not first:
                    dve.wait_ge(s_xt[b], 16 * i)
                for q in range(R // 2):
                    dve.wait_ge(s_mm[2], R // 2 * (2 * i + b) + q + 1)
                    V.tensor_copy(xt_out[:, b, 2 * D * q:2 * D * q + 2 * D], bank[2 + q][0:WN, :]).then_inc(s_ev[2], 1)
            low, high, place, spare2 = (flat(moves[:, k, :, :]) for k in range(4))
            V.tensor_copy(ints(spare2), high)
            dve.drain()
            V.tensor_single_scalar(ints(high), ints(spare2), 15, ALU.bitwise_and)
            V.tensor_single_scalar(ints(spare2), ints(spare2), 4, ALU.arith_shift_right)
            dve.drain()
            V.scalar_tensor_tensor(flat(rel_idx[:, 0:NG, :]), ints(high), 2048.0, low, ALU.mult, ALU.add)
            V.tensor_copy(flat(src_f[:]), ints(spare2))
            dve.wait_ge(s_posi, 1)
            dve.drain()
            for w in range(1, NW):
                V.tensor_scalar(low, place, offset[:, w:w + 1], float(WN), ALU.is_ge, ALU.mult)
                dve.drain()
                V.tensor_tensor(flat(src_f[:]), flat(src_f[:]), low, ALU.add)
                dve.drain()
            for q in range(2):
                V.tensor_copy(span_f[:, q:q + 1], place_of_group[:, q:q + 1])
            dve.drain()
            span(offset[0:NG, 1:NW])
            V.tensor_copy(span_f[:, 0:1], span_f[:, 0:1]).then_inc(s_flt, 1)
            staged_and_taken(stage_h(2), take2)
            dve.wait_ge(s_lists_t, 3)
            V.tensor_copy(spans[0:1, 1, :], bank[6][0:1, 0:NG]).then_inc(s_lists, 1)
            dve.wait_ge(s_lists, 2)
            sums(2, D, rel_idx, lambda i, b: None)
            dve.drain()
            V.tensor_tensor(acc[:, :, 0:D], acc[:, :, 0:D], bias_rel[:].rearrange("p (a d) -> p a d", a=1).broadcast_to([WN, NW, D]),
                            ALU.add)
            dve.drain()
            V.scalar_tensor_tensor(x[:], acc[:, :, 0:D], 0.0, x[:], ALU.max, ALU.add).then_inc(s_x_new[2], 1)
            dve.drain()
            with dve.Fori(0, NW) as w:
                statistics(w, window(x, w))
            norm(3)

            def take3(i, b, first):
                if not first:
                    dve.wait_ge(s_hh[b], 16 * i)
                w = 2 * i + b
                dve.wait_ge(s_mm[3], w + 1)
                hh = bank[2 + b][0:WN, 0:D]
                V.tensor_copy(hh_out[:, b, 0:D], hh)
                V.tensor_tensor(prod[:, 0, :], hh, a_src[:], ALU.mult)
                V.tensor_tensor(prod[:, 1, :], hh, a_dst[:], ALU.mult)
                dve.drain()
                V.tensor_reduce(window(s_dst, w), prod[:, 1, :].rearrange("p (h d) -> p h d", h=H), AX.X, ALU.add)
                V.tensor_reduce(hh_out[:, b, D:DH], prod[:, 0, :].rearrange("p (h d) -> p h d", h=H), AX.X, ALU.add
                                ).then_inc(s_ev[3], 1)
                dve.drain()
            staged_and_taken(stage_h(3), take3)
            V.memset(run_max[:], -BIG)
            for b in range(RING - 1):
                fill_slot(src_idx, b, b, 3)
            visits, tiles, fast, pending = Visits(dve), Visits(dve, GT), Visits(dve), window_register()
            dve.wait_ge(s_zero[3], 1)
            V.memset(weight[:], 0.0).then_inc(s_exp, 1)
            V.memset(decay[:], 1.0).then_inc(s_dexp, 1)
            heads = lambda t: t.rearrange("p (h d) -> p h d", h=H)
            dve.drain()

            def weigh(b, v):
                dve.wait_ge(s_exp, v)
                V.tensor_copy(msg[:, :, D:DH], weight[:])
                V.tensor_tensor(msg[:, :, 0:D].rearrange("p j (h d) -> p j h d", h=H),
                                rows[:, b, :, 0:D].rearrange("p j (h d) -> p j h d", h=H),
                                weight[:].rearrange("p j (h e) -> p j h e", e=1).broadcast_to([128, GT, H, HD]), ALU.mult
                                ).then_inc(s_msg, 1)

            def shrink(w, v):
                dve.wait_ge(s_dexp, v)
                mine = acc[:, bass.ds(w, 1), :].rearrange("p w d -> p (w d)")
                V.tensor_tensor(heads(mine[:, 0:D]), heads(mine[:, 0:D]),
                                decay[:].rearrange("p (h d) -> p h d", d=1).broadcast_to([WN, H, HD]), ALU.mult)
                V.tensor_tensor(mine[:, D:DH], mine[:, D:DH], decay[:], ALU.mult)
                dve.drain()

            def add(w, b, v):
                mine = acc[:, bass.ds(w, 1), :].rearrange("p w d -> p (w d)")
                dve.wait_ge(s_sum[3], v)
                V.tensor_tensor(mine, mine, bank[6 + b % 2][0:WN, 0:DH], ALU.add)
                dve.drain()

            def attention(i, b):
                g = RING * i + b
                last = ring_before(b)
                dve.wait_ge(s_starts[b], 16 * (i + 1))

                def scan(u):
                    dve.wait_ge(s_sT, u)
                    V.tensor_tensor_scan(run, starts[:, b, :], psum[0:H, 1024:1024 + GE], -BIG, ALU.add, ALU.max
                                         ).then_inc(s_run, 1)

                def highest_by_scan(v, w_before, weigh_before):
                    u = fast.next()
                    scan(v)
                    weigh_before()
                    dve.wait_ge(s_runT, u)
                    is_last = last_f[:, bass.ds(g, 1), :].rearrange("p g (j h) -> p (g j) h", h=1)
                    V.tensor_tensor(last_max[:, :, 0:H], bank[5][:, 0:GT * H].rearrange("p (j h) -> p j h", j=GT),
                                    is_last.broadcast_to([128, GT, H]), ALU.mult)
                    V.tensor_copy(last_max[:, :, H:H + 1], is_last).then_inc(s_lastv, 1)
                    shrink(w_before, v)
                    dve.wait_ge(s_nmax, u)
                    V.tensor_scalar(seen[:], bank[5][0:WN, 64 + H:64 + H + 1], BIG, -BIG, ALU.mult, ALU.add)
                    dve.drain()
                    V.tensor_scalar(node_ref[:, H:2 * H], bank[5][0:WN, 64:64 + H], seen[:], None, ALU.add)

                def highest_by_mask(v, w_before, weigh_before):
                    weigh_before()
                    shrink(w_before, v)
                    dve.wait_ge(s_sT, v)
                    dve.wait_ge(s_ohtc, v)
                    V.tensor_scalar(penalty[:], onehot_t[:], BIG, -BIG, ALU.mult, ALU.add)
                    for j in range(GT):
                        s_src = rows[:, b, j, D:DH].rearrange("p (h e) -> p h e", e=1).broadcast_to([128, H, TE])
                        V.tensor_tensor(diag, ident[:].rearrange("p (h e) -> p h e", h=1).broadcast_to([128, H, TE]), s_src,
                                        ALU.mult).then_inc(s_diag, 1)
                        dve.drain()
                        dve.wait_ge(s_spread, tiles.next())
                        pen = penalty[:, TE * j:TE * j + TE].rearrange("p (h e) -> p h e", h=1).broadcast_to([WN, 4, TE])
                        for q in range(2):
                            V.tensor_tensor(masked[:, 4 * q:4 * q + 4, :],
                                            bank[2 + q][0:WN, :].rearrange("p (h e) -> p h e", h=4), pen, ALU.add)
                        dve.drain()
                        V.tensor_reduce(tile_max[:, j, :], masked, AX.X, ALU.max)
                    dve.drain()
                    V.tensor_reduce(node_ref[:, H:2 * H], tile_max[:].rearrange("p j h -> p h j"), AX.X, ALU.max)

                def visit(before, apart):
                    def body(w, mixed):
                        v = visits.next()
                        w_before = held(pending)
                        if not apart:
                            weigh(before, v)
                            dve.wait_ge(s_sum[3], dve.snap(v + 1))
                        onehots(g, w, 3, b % 2)

                        def weigh_before():
                            if apart:
                                weigh(before, v)
                        with dve.If(mixed > 0):
                            highest_by_mask(v, w_before, weigh_before)
                        with dve.Else():
                            highest_by_scan(v, w_before, weigh_before)
                        dve.drain()
                        V.tensor_tensor(node_ref[:, H:2 * H], node_ref[:, H:2 * H], window(s_dst, w), ALU.add)
                        V.tensor_copy(node_ref[:, 0:H], window(s_dst, w))
                        dve.drain()
                        V.scalar_tensor_tensor(node_ref[:, H:2 * H], node_ref[:, H:2 * H], SLOPE, node_ref[:, H:2 * H],
                                               ALU.mult, ALU.max)
                        dve.drain()
                        V.tensor_tensor(node_ref[:, H:2 * H], window(run_max, w), node_ref[:, H:2 * H], ALU.max).then_inc(s_ref, 1)
                        dve.drain()
                        V.tensor_tensor(decay[:], window(run_max, w), node_ref[:, H:2 * H], ALU.subtract).then_inc(s_dec, 1)
                        dve.drain()
                        V.tensor_copy(window(run_max, w), node_ref[:, H:2 * H])
                        add(w_before, before, dve.snap(v + 1))
                        if before != b:
                            fill_slot(src_idx, g + RING - 1, last, 3)
                        dve.wait_ge(s_back, v)
                        back = bank[4][:, 0:GT * 2 * H].rearrange("p (j c) -> p j c", j=GT)
                        V.tensor_tensor(score[:], rows[:, b, :, D:DH], back[:, :, 0:H], ALU.add)
                        dve.drain()
                        V.scalar_tensor_tensor(score[:], score[:], SLOPE, score[:], ALU.mult, ALU.max)
                        dve.drain()
                        V.tensor_tensor(score[:], score[:], back[:, :, H:2 * H], ALU.subtract)
                        dve.drain()
                        V.tensor_scalar_min(score[:], score[:], 0.0).then_inc(s_arg, 1)
                        hold(pending, w)
                    return body
                each_window(dve, g, visit(last, last % 2 != b % 2), visit(b, False))
            rings(dve, attention)
            v = visits.next()
            w_before = held(pending)
            weigh(RING - 1, v)
            shrink(w_before, v)
            add(w_before, RING - 1, dve.snap(v + 1))
            V.tensor_scalar_max(s_dst[:], acc[:, :, D:DH], 1e-30)
            dve.drain()
            V.reciprocal(s_dst[:], s_dst[:])
            dve.drain()
            V.tensor_tensor(acc[:, :, 0:D].rearrange("p w (h d) -> p w h d", h=H),
                            acc[:, :, 0:D].rearrange("p w (h d) -> p w h d", h=H),
                            s_dst[:].rearrange("p w (h d) -> p w h d", d=1).broadcast_to([WN, NW, H, HD]), ALU.mult)
            dve.drain()
            V.tensor_tensor(h[:], acc[:, :, 0:D], h[:], ALU.add)
            dve.drain()
            with dve.Fori(0, NW) as w:
                statistics(w, window(h, w))
            norm(4)
            dve.drain()
            with dve.Fori(0, NW) as w:
                V.tensor_scalar(window(h, w), window(h, w), rstd[:, bass.ds(w, 1)], shift[:, bass.ds(w, 1)], ALU.mult, ALU.add)
            dve.drain()
            all_windows = lambda t: t[:].rearrange("p (a d) -> p a d", a=1).broadcast_to([WN, NW, D])
            V.tensor_tensor(h[:], h[:], all_windows(gamma), ALU.mult)
            dve.drain()
            V.tensor_tensor(h[:], h[:], all_windows(beta), ALU.add)
            dve.drain()
            V.tensor_scalar_min(acc[:, :, 0:D], h[:], 0.0).then_inc(s_elu, 1)
            V.scalar_tensor_tensor(x[:], h[:], 0.0, x[:], ALU.max, ALU.add)
            dve.wait_ge(s_elud, 1)
            dve.drain()
            V.scalar_tensor_tensor(x[:], acc[:, :, 0:D], -1.0, x[:], ALU.add, ALU.add).then_inc(s_x_new[3], 1)


_INPUTS = ["x", "src", "dst", "edge_attr_256", "edge_type_8", "L0_gnn_W_l", "L0_gnn_W_r", "L0_gnn_b_r", "L1_gnn_W1",
           "L1_gnn_b1", "L1_gnn_bn_gamma", "L1_gnn_bn_beta", "L1_gnn_W2", "L1_gnn_b2", "L1_gnn_ln_w", "L1_gnn_ln_b",
           "L1_gnn_gn_w", "L1_gnn_gn_b", "L1_gnn_gn_ms", "L2_gnn_weight", "L2_gnn_bias", "L3_gnn_W", "L3_gnn_a_src",
           "L3_gnn_a_dst", "L3_gnn_gamma", "L3_gnn_beta"]
_TRANSPOSED = ("L0_gnn_W_l", "L0_gnn_W_r")


def kernel(**inputs):
    import numpy as np
    import concourse.bacc as bacc
    from concourse import mybir as mb
    from concourse.bass_utils import run_bass_kernel_spmd as run

    nc = bacc.Bacc("TRN2", target_bir_lowering=False, num_devices=1)
    arrays, aps = {}, {}
    for name in _INPUTS:
        v = np.asarray(inputs[name])
        v = np.ascontiguousarray(v.T if name in _TRANSPOSED else v)
        arrays[f"in_{name}"] = v
        aps[name] = nc.dram_tensor(f"in_{name}", v.shape, mb.dt.from_np(v.dtype), kind="ExternalInput").ap()
    out = nc.dram_tensor("out_x", arrays["in_x"].shape, mb.dt.float32, kind="ExternalOutput").ap()
    gnn_kernel(nc, aps, out)
    r = run(nc, [arrays], core_ids=[0])
    return r.results[0]["out_x"]
```
